# Optimizing a Trainium2 kernel written in Bass

```python
import numpy as np
import jax
import jax.numpy as jnp

def _softmax(x, axis=-1):
    return jax.nn.softmax(x, axis=axis)

def _gelu(x):
    return jax.nn.gelu(x, approximate=True)

def _silu(x):
    return jax.nn.silu(x)

def _sigmoid(x):
    return jax.nn.sigmoid(x)

def _layernorm(x, axis=-1, eps=1e-05):
    m = jnp.mean(x, axis=axis, keepdims=True)
    v = jnp.var(x, axis=axis, keepdims=True)
    return (x - m) / jnp.sqrt(v + eps)

def _scatter_add(tgt, idx, src, axis=0):
    return tgt.at[idx].add(src)

def _segment_sum(src, seg, n):
    return jax.ops.segment_sum(src, seg, n)
kernel_name = 'mk_decoder_preln_d1_seqx_r8_758483'

def setup_inputs(seed: int=0):
    np.random.seed(seed)
    _w = jnp.asarray

    def _rec_inputs():
        import jax
        import jax.numpy as jnp
        _rk = jax.random.key(seed)
        x = -0.0002928 + 1 * jax.random.normal(jax.random.fold_in(_rk, 1), (16, 56, 128), jnp.float32)
        _lenS = 56 - jax.random.randint(jax.random.fold_in(_rk, 7), (16,), 0, max(1, 56 // 4) + 1, jnp.int32)
        _lenS2 = 1500 - jax.random.randint(jax.random.fold_in(_rk, 8), (16,), 0, max(1, 1500 // 4) + 1, jnp.int32)
        _ctx_768P = jax.random.normal(jax.random.fold_in(_rk, 11), (16, 16, 96), jnp.float32)
        _ctx_768c = jax.random.dirichlet(jax.random.fold_in(_rk, 511), 0.3 * jnp.ones((16,), jnp.float32), (16, 1500))
        _ctx_768t = jnp.einsum('bsk,bkd->bsd', _ctx_768c, _ctx_768P)
        _ctx_768t = _ctx_768t * jax.lax.rsqrt(jnp.mean(jnp.square(_ctx_768t)) + 1e-12) * 0.953939
        ctx_768 = 2.09791e-05 + 1.00001 * (_ctx_768t + 0.3 * jax.random.normal(jax.random.fold_in(_rk, 611), (16, 1500, 96), jnp.float32))
        return (x, ctx_768)
    x, ctx_768 = _rec_inputs()

    def _L0_attn_setup():
        import jax, jax.numpy as jnp
        import numpy as np
        from math import sqrt
        EMBED = 128
        HEADS = 16
        key = jax.random.key(seed)
        k1, k2, k3, k4, k5 = jax.random.split(key, 5)
        x = jax.random.normal(k1, (2, 256, EMBED), dtype=jnp.float32)
        s = 1.0 / sqrt(EMBED)
        W_qkv = jax.random.normal(k2, (EMBED, 3 * EMBED), dtype=jnp.float32) * s
        b_qkv = jax.random.normal(k3, (3 * EMBED,), dtype=jnp.float32) * 0.01
        W_out = jax.random.normal(k4, (EMBED, EMBED), dtype=jnp.float32) * s
        b_out = jax.random.normal(k5, (EMBED,), dtype=jnp.float32) * 0.01
        return {'x': x, 'W_qkv': W_qkv, 'b_qkv': b_qkv, 'W_out': W_out, 'b_out': b_out}
    _L0_attn_all = _L0_attn_setup()
    _L0_attn_in = {k: v for k, v in _L0_attn_all.items() if k in ('W_qkv', 'b_qkv', 'W_out', 'b_out')}
    del _L0_attn_all

    def _L0_xattn_setup():
        import jax, jax.numpy as jnp
        import numpy as np
        B, LQ, LKV = (2, 256, 256)
        C, CTX, H, DK = (128, 96, 16, 64)
        SCALE = DK ** (-0.5)
        key = jax.random.key(seed)
        kx, ky, kq, kkv, kp, kb = jax.random.split(key, 6)
        return {'x': jax.random.normal(kx, (B, LQ, C), dtype=jnp.float32), 'y': jax.random.normal(ky, (B, LKV, CTX), dtype=jnp.float32), 'Wq': jax.random.normal(kq, (C, H * DK), dtype=jnp.float32) * C ** (-0.5), 'Wkv': jax.random.normal(kkv, (CTX, 2 * H * DK), dtype=jnp.float32) * CTX ** (-0.5), 'Wproj': jax.random.normal(kp, (H * DK, C), dtype=jnp.float32) * (H * DK) ** (-0.5), 'bproj': jax.random.normal(kb, (C,), dtype=jnp.float32) * 0.01}
    _L0_xattn_all = _L0_xattn_setup()
    _L0_xattn_in = {k: v for k, v in _L0_xattn_all.items() if k in ('Wq', 'Wkv', 'Wproj', 'bproj')}
    del _L0_xattn_all

    def _L0_ffn_setup():
        import jax, jax.numpy as jnp
        import numpy as np
        EMBED_DIM = 128
        MLP_RATIO = 4
        NUM_EXPERTS = 8
        CAPACITY = 1.0
        LN_EPS = 1e-05

        def _layernorm(y, gamma, beta):
            mu = jnp.mean(y, axis=-1, keepdims=True)
            var = jnp.mean(jnp.square(y - mu), axis=-1, keepdims=True)
            return (y - mu) * jax.lax.rsqrt(var + LN_EPS) * gamma + beta
        key = jax.random.key(seed)
        k0, k1, k2, k3, k4, k5 = jax.random.split(key, 6)
        d = EMBED_DIM
        dd = EMBED_DIM * MLP_RATIO
        n = NUM_EXPERTS
        x = jax.random.normal(k0, (4, 256, d), dtype=jnp.float32)
        gate_w = jax.random.normal(k1, (n, d), dtype=jnp.float32) * 0.02
        ln_gamma = jnp.ones((d,), dtype=jnp.float32)
        ln_beta = jnp.zeros((d,), dtype=jnp.float32)
        fc1s = jax.random.normal(k2, (n, dd, d), dtype=jnp.float32) * (1.0 / np.sqrt(d))
        b1s = jax.random.normal(k3, (n, dd), dtype=jnp.float32) * 0.02
        fc2s = jax.random.normal(k4, (n, d, dd), dtype=jnp.float32) * (1.0 / np.sqrt(dd))
        b2s = jax.random.normal(k5, (n, d), dtype=jnp.float32) * 0.02
        return {'x': x, 'gate_w': gate_w, 'ln_gamma': ln_gamma, 'ln_beta': ln_beta, 'fc1s': fc1s, 'b1s': b1s, 'fc2s': fc2s, 'b2s': b2s}
    _L0_ffn_all = _L0_ffn_setup()
    _L0_ffn_in = {k: v for k, v in _L0_ffn_all.items() if k in ('gate_w', 'ln_gamma', 'ln_beta', 'fc1s', 'b1s', 'fc2s', 'b2s')}
    del _L0_ffn_all
    return {'x': x, 'ctx_768': ctx_768, 'L0_attn_W_qkv': _L0_attn_in['W_qkv'], 'L0_attn_b_qkv': _L0_attn_in['b_qkv'], 'L0_attn_W_out': _L0_attn_in['W_out'], 'L0_attn_b_out': _L0_attn_in['b_out'], 'L0_xattn_Wq': _L0_xattn_in['Wq'], 'L0_xattn_Wkv': _L0_xattn_in['Wkv'], 'L0_xattn_Wproj': _L0_xattn_in['Wproj'], 'L0_xattn_bproj': _L0_xattn_in['bproj'], 'L0_ffn_gate_w': _L0_ffn_in['gate_w'], 'L0_ffn_ln_gamma': _L0_ffn_in['ln_gamma'], 'L0_ffn_ln_beta': _L0_ffn_in['ln_beta'], 'L0_ffn_fc1s': _L0_ffn_in['fc1s'], 'L0_ffn_b1s': _L0_ffn_in['b1s'], 'L0_ffn_fc2s': _L0_ffn_in['fc2s'], 'L0_ffn_b2s': _L0_ffn_in['b2s']}

def reference(x, ctx_768, L0_attn_W_qkv, L0_attn_b_qkv, L0_attn_W_out, L0_attn_b_out, L0_xattn_Wq, L0_xattn_Wkv, L0_xattn_Wproj, L0_xattn_bproj, L0_ffn_gate_w, L0_ffn_ln_gamma, L0_ffn_ln_beta, L0_ffn_fc1s, L0_ffn_b1s, L0_ffn_fc2s, L0_ffn_b2s):
    import jax
    import jax.numpy as jnp

    def _L0_attn_ref(x, W_qkv, b_qkv, W_out, b_out):
        import jax, jax.numpy as jnp
        import numpy as np
        from math import sqrt
        EMBED = 128
        HEADS = 16
        B, N, E = x.shape
        H = HEADS
        d = E // H
        qkv = x @ W_qkv + b_qkv
        q, k, v = jnp.split(qkv, 3, axis=2)
        q = q.reshape(B, N, H, d)
        k = k.reshape(B, N, H, d)
        v = v.reshape(B, N, H, d)
        energy = jnp.einsum('bqhe,bkhe->bqhk', q, k)
        attn = jax.nn.softmax(energy, axis=-1) / sqrt(E)
        out = jnp.einsum('bihv,bvhd->bihd', attn, v)
        out = out.reshape(B, N, E)
        return out @ W_out + b_out

    def _L0_xattn_ref(x, y, Wq, Wkv, Wproj, bproj):
        import jax, jax.numpy as jnp
        import numpy as np
        B, LQ, LKV = (2, 256, 256)
        C, CTX, H, DK = (128, 96, 16, 64)
        SCALE = DK ** (-0.5)
        b, lq, _ = x.shape
        lkv = y.shape[1]
        q = (x @ Wq).reshape(b, lq, H, DK).transpose(0, 2, 1, 3)
        kv = (y @ Wkv).reshape(b, lkv, 2, H, DK).transpose(2, 0, 3, 1, 4)
        k, v = (kv[0], kv[1])
        atten = jax.nn.softmax(jnp.einsum('bhid,bhjd->bhij', q, k) * SCALE, axis=-1)
        res = jnp.einsum('bhij,bhjd->bhid', atten, v)
        res = res.transpose(0, 2, 1, 3).reshape(b, lq, H * DK)
        out = res @ Wproj + bproj
        return out

    def _L0_ffn_ref(x, gate_w, ln_gamma, ln_beta, fc1s, b1s, fc2s, b2s):
        import jax, jax.numpy as jnp
        import numpy as np
        EMBED_DIM = 128
        MLP_RATIO = 4
        NUM_EXPERTS = 8
        CAPACITY = 1.0
        LN_EPS = 1e-05

        def _layernorm(y, gamma, beta):
            mu = jnp.mean(y, axis=-1, keepdims=True)
            var = jnp.mean(jnp.square(y - mu), axis=-1, keepdims=True)
            return (y - mu) * jax.lax.rsqrt(var + LN_EPS) * gamma + beta
        og_shape = x.shape
        d = og_shape[-1]
        xf = x.reshape(-1, d)
        bs = xf.shape[0]
        n = gate_w.shape[0]
        k = int(bs * CAPACITY) // n
        scores = xf @ gate_w.T
        scores = (jnp.tanh(scores) + 1.0) * 0.5
        vals, idx = jax.lax.top_k(scores.T, k)
        kept_w = vals.T
        flat_idx = idx.T.reshape(-1)
        y = xf[flat_idx].reshape(k, n, d)
        y = _layernorm(y, ln_gamma, ln_beta)
        h = jnp.einsum('knd,nfd->knf', y, fc1s) + b1s
        h = jax.nn.gelu(h, approximate=True)
        o = jnp.einsum('knf,ndf->knd', h, fc2s) + b2s
        o = o * kept_w[:, :, None]
        out = xf.at[flat_idx].add(o.reshape(k * n, d))
        return out.reshape(og_shape)
    x = x + _L0_attn_ref(_layernorm(x, axis=-1), L0_attn_W_qkv, L0_attn_b_qkv, L0_attn_W_out, L0_attn_b_out)
    x = x + _L0_xattn_ref(_layernorm(x, axis=-1), ctx_768, L0_xattn_Wq, L0_xattn_Wkv, L0_xattn_Wproj, L0_xattn_bproj)
    x = x + _L0_ffn_ref(_layernorm(x, axis=-1), L0_ffn_gate_w, L0_ffn_ln_gamma, L0_ffn_ln_beta, L0_ffn_fc1s, L0_ffn_b1s, L0_ffn_fc2s, L0_ffn_b2s)
    return x

_drawn_inputs = setup_inputs


def setup_inputs(seed=0):
    import zlib

    import numpy as np

    out = dict(_drawn_inputs(seed))
    spreads = {'L0_ffn_ln_gamma': (1.0, 0.2), 'L0_ffn_ln_beta': (0.0, 0.37)}
    factors = {'L0_attn_b_qkv': 22.507,
     'L0_attn_b_out': 3.647,
     'L0_xattn_bproj': 4.71,
     'L0_ffn_b1s': 8.0,
     'L0_ffn_b2s': 8.0}
    for name, (base, spread) in spreads.items():
        noise = np.random.default_rng([zlib.crc32(name.encode()), seed]).standard_normal(out[name].shape)
        drawn = base * np.exp(spread * noise) if base else spread * noise
        out[name] = jnp.asarray(drawn.astype(out[name].dtype))
    for name, factor in factors.items():
        out[name] = (out[name] * factor).astype(out[name].dtype)
    return out
```

```python
from contextlib import ExitStack

import concourse.bass as bass
from concourse import mybir

F32 = mybir.dt.float32
F16 = mybir.dt.float16
I32 = mybir.dt.int32
ALU = mybir.AluOpType
ACT = mybir.ActivationFunctionType
X = mybir.AxisListType.X

P = 128
EPS = 1e-5


def decoder_layer(nc, x, ctx_768, W_qkv, b_qkv, W_out, b_out, Wq, Wkv, Wproj, bproj,
                  gate_w, ln_gamma, ln_beta, fc1s, b1s, fc2s, b2s, out):
    B, N, C = x.shape
    L, E = ctx_768.shape[1:]
    H = 16
    DH = C // H
    DK = Wq.shape[1] // H
    T = B * N
    ROWS = H * N
    TILES = ROWS // P
    KP = 125
    KC = L // KP
    GROUPS = 3
    GB = KC // GROUPS
    GW = GB * KP
    NE, F = fc1s.shape[:2]
    FC = F // P
    CAP = T // NE
    TT = T // CAP
    REP = P // NE
    ROUNDS = 7
    SCALE = float(DK) ** -0.5
    ATT = float(C) ** -0.5
    HALF = T // 2

    ctx = ExitStack()
    with ctx:
        def sb(name, shape, dt=F32):
            return ctx.enter_context(nc.sbuf_tensor(name, shape, dt))

        def sem(name):
            return ctx.enter_context(nc.semaphore(name))

        bank = [ctx.enter_context(nc.psum_tensor(f"bank{i}", [P, 512], F32)) for i in range(8)]
        SC = bank[0:3]
        TP = [bank[3], bank[4], bank[3]]
        ACC = bank[5]
        MISC = bank[6:8]

        ident = sb("ident", [P, P])
        ident16 = sb("ident16", [P, P], F16)
        headmask = sb("headmask", [P, H])
        tri = sb("tri", [CAP, CAP], F16)
        ones16 = sb("ones16", [CAP, CAP], F16)
        onesrow = sb("onesrow", [1, CAP])
        block = sb("block", [P, P], F16)
        jcol_i = sb("jcol_i", [P, NE], I32)
        jcol8 = sb("jcol8", [P, NE])
        jcol = sb("jcol", [P, 1])
        iota_i = sb("iota_i", [CAP, CAP], I32)
        iota1 = sb("iota1", [CAP, CAP])
        neghalf = sb("neghalf", [P, TT])

        wqkv = sb("wqkv", [C, 3 * C])
        wout = sb("wout", [C, C])
        bq = sb("bq", [C, 1])
        bk = sb("bk", [C, 1])
        bv = sb("bv", [N, C])
        bout = sb("bout", [N, C])
        bpr = sb("bpr", [C, 1])
        M = sb("M", [C, H, E])
        U = sb("U", [E, H, C])

        first_space = ExitStack()

        def at_first(name, shape, dt=F32):
            return first_space.enter_context(nc.sbuf_tensor(name, shape, dt))

        wq = at_first("wq", [C, H * DK])
        wkv = at_first("wkv", [E, 2 * H * DK])
        wproj = at_first("wproj", [P, H // 2, C])
        wqT = at_first("wqT", [P, H // 2, C])
        wkT = at_first("wkT", [P, H // 2, E])
        wvT = at_first("wvT", [P, H // 2, E])
        first_space.close()
        fc1 = sb("fc1", [P, NE * FC, C])
        fc2 = sb("fc2", [C, NE, F])

        x1 = sb("x1", [N, B, C])
        x1p = sb("x1p", [CAP, TT, C])
        gam = sb("gam", [CAP, C])
        bet = sb("bet", [CAP, C])
        gate = sb("gate", [NE, C])
        b1r = sb("b1r", [NE * FC, P])
        b2r = sb("b2r", [1, NE, C])

        oT_space = ExitStack()
        oT = oT_space.enter_context(nc.sbuf_tensor("oT", [E, B, ROWS], F32))

        early_space = ExitStack()

        def early(name, shape, dt=F32):
            return early_space.enter_context(nc.sbuf_tensor(name, shape, dt))

        xin = early("xin", [N, B, C])
        xb = early("xb", [N, B, C])
        st = early("st", [N, 6])
        mv = early("mv", [N, 2])
        ve = early("ve", [N, 1])
        rs = early("rs", [N, 1])
        xn = early("xn", [N, C])
        xT = early("xT", [C, N])
        kT = early("kT", [C, N])
        v = early("v", [N, C])
        qblk = early("qblk", [C, H, N])
        es = early("es", [P, TILES, N])
        ep = early("ep", [P, TILES, N])
        en = early("en", [P, TILES, N])
        amax = early("amax", [P, TILES])
        asum = early("asum", [P, TILES])
        arec = early("arec", [P, TILES])
        aT = early("aT", [N, ROWS])
        ao = early("ao", [N, C])
        aoT = early("aoT", [C, N])
        x1T = early("x1T", [C, N])

        cf = [early(f"cf{i}", [KP, KC, E]) for i in range(2)]
        chi = early("chi", [KP, KC, E], F16)
        clo = early("clo", [KP, KC, E], F16)
        cT = [early(f"cT{i}", [E, 2, KC, KP], F16) for i in range(2)]
        qhi = [early(f"qhi{i}", [E, ROWS], F16) for i in range(2)]
        qlo = [early(f"qlo{i}", [E, ROWS], F16) for i in range(2)]
        prob = [early(f"prob{i}", [P, L]) for i in range(2)]
        pT = [early(f"pT{k}", [KP, GB, P]) for k in range(GROUPS)]
        mx3 = early("mx3", [P, GROUPS])
        nmax = early("nmax", [P, 1])
        sum3 = [early(f"sum3_{i}", [P, GROUPS]) for i in range(2)]
        den = early("den", [P, 1])
        rden = early("rden", [P, 1])
        on = early("on", [P, E])

        early_space.close()
        oT_space.close()

        fc1T = sb("fc1T", [C, NE * FC, P])
        fc2T = sb("fc2T", [P, NE * FC, C])
        G = sb("G", [CAP, TT, NE, CAP], F16)
        th = sb("th", [P, T])
        vals = sb("vals", [P, T])
        mge = sb("mge", [P, T], F16)
        mgt = sb("mgt", [P, T], F16)

        yT = sb("yT", [C, T])
        x2 = sb("x2", [CAP, TT, C])
        xf = sb("xf", [CAP, TT, C])
        base = sb("base", [CAP, TT, C])
        y1 = sb("y1", [CAP, TT, C])
        yhi = sb("yhi", [CAP, TT, C], F16)
        ylo = sb("ylo", [CAP, TT, C], F16)
        fst = sb("fst", [CAP, TT, 6])
        fmv = sb("fmv", [CAP, TT, 2])
        fve = sb("fve", [CAP, TT])
        frs = sb("frs", [CAP, TT])
        gateT = sb("gateT", [C, NE, REP])
        xfT = sb("xfT", [C, T])
        junk = sb("junk", [P, T], F16)
        thr = sb("thr", [P, 1])
        low = sb("low", [P, 1])
        cnt = sb("cnt", [P, 1])
        flag = sb("flag", [P, 1], F16)
        ge = sb("ge", [CAP, TT, NE])
        sel = sb("sel", [CAP, 2, TT, NE], F16)
        vn = sb("vn", [CAP, TT, NE])
        v2 = sb("v2", [CAP, TT, NE, 2], F16)
        cg = sb("cg", [CAP, NE])
        pa = sb("pa", [CAP, TT, NE])
        pb = sb("pb", [CAP, TT, NE])
        slot = sb("slot", [CAP, TT, NE])
        GT = sb("GT", [CAP, NE, TT, CAP], F16)
        wslot = sb("wslot", [CAP, NE])
        w2s = sb("w2s", [CAP, NE, 2])
        ygT = sb("ygT", [C, NE, CAP])
        b1T = sb("b1T", [P, NE, FC])
        hb = [sb(f"hb{i}", [P, FC, CAP]) for i in range(2)]
        hg = [sb(f"hg{i}", [P, FC, CAP]) for i in range(2)]
        ohi = [sb(f"ohi{i}", [CAP, C], F16) for i in range(2)]
        olo = [sb(f"olo{i}", [CAP, C], F16) for i in range(2)]
        res = sb("res", [CAP, TT, C])

        ld_x, ld_wq, ld_wkv, ld_qkv, ld_small, ld_ffn, ld_x1 = (sem("ld_" + n) for n in (
            "x", "wq", "wkv", "qkv", "small", "ffn", "x1"))
        ld_ctx = [sem("ld_ctx0"), sem("ld_ctx1")]
        stored = sem("stored")
        passed = sem("passed")
        const_ready = sem("const_ready")
        wT_full = sem("wT_full")
        wT_ready = sem("wT_ready")
        mu_full = sem("mu_full")
        mu_ready = sem("mu_ready")
        misc_full = sem("misc_full")
        stats_done, aggr_done, eps_done, rstd_done, norm_done = (sem(n) for n in (
            "stats_done", "aggr_done", "eps_done", "rstd_done", "norm_done"))
        xT_ready, qkv_ready, amax_ready, es_ready, ep_ready, asum_ready, arec_ready, en_ready = (sem(n) for n in (
            "xT_ready", "qkv_ready", "amax_ready", "es_ready", "ep_ready", "asum_ready", "arec_ready", "en_ready"))
        aT_ready, ao_ready, aoT_ready, x1_ready = (sem(n) for n in ("aT_ready", "ao_ready", "aoT_ready", "x1_ready"))
        qhi_ready, qlo_ready, cs_ready, ctA_ready, ctB_ready = (sem(n) for n in (
            "qhi_ready", "qlo_ready", "cs_ready", "ctA_ready", "ctB_ready"))
        xb_ready = sem("xb_ready")
        sc_full, mx_done, nmax_ready, exp_done = (sem(n) for n in ("sc_full", "mx_done", "nmax_ready", "exp_done"))
        tp_full, pTA_ready, pTB_ready, pv_done = (sem(n) for n in ("tp_full", "pTA_ready", "pTB_ready", "pv_done"))
        den_ready, rden_ready, on_ready, oT_full, oT_ready = (sem(n) for n in (
            "den_ready", "rden_ready", "on_ready", "oT_full", "oT_ready"))
        f_pe, f_dve, f_act, f_pool = (sem(n) for n in ("f_pe", "f_dve", "f_act", "f_pool"))

        def count(p, h, per, off):
            return p * (2 * per) + (h * per + off)

        def wait(eng, s, val):
            if isinstance(val, int) and val <= 0:
                return
            eng.wait_ge(s, val)

        USES = ["xT", "qkv", "S", "PT0", "PT1", "PV", "aoT", "y", "cA", "cB", "x1T", "q0", "q1", "cC"]
        NU = len(USES)
        READ = {"xT": (xT_ready, 2, 1), "qkv": (qkv_ready, 1, 1), "S": (es_ready, 1, 1),
                "PT0": (aT_ready, 2, 1), "PT1": (aT_ready, 2, 2), "PV": (ao_ready, 1, 1),
                "aoT": (aoT_ready, 1, 1), "y": (x1_ready, 1, 1), "cA": (ctA_ready, 2, 1),
                "cB": (ctB_ready, 1, 1), "x1T": (xT_ready, 2, 2), "q0": (qlo_ready, 2, 1),
                "q1": (qlo_ready, 2, 2), "cC": (ctA_ready, 2, 2)}

        def use_bank(name):
            return MISC[USES.index(name) % 2]

        def wait_full(eng, p, h, name):
            eng.wait_ge(misc_full, count(p, h, NU, USES.index(name) + 1))

        def wait_bank_read(eng, p, h, name):
            n = USES.index(name)
            s, per, off = READ[USES[n - 2]]
            wait(eng, s, count(p, h, per, off if n >= 2 else off - per))

        def batch(p, h):
            return p * 2 + h

        CONSTS = 20
        LD_SMALL = 11 * 16
        LD_FFN = 2 * 16

        AGGR3 = 4 + 2 * TT
        NORM3 = AGGR3 + TT
        GATE_T = NORM3 + 2
        AGGR4 = GATE_T + 2 * TT
        NORM4 = AGGR4 + TT
        VALS = NORM4 + 5
        FLAG = [VALS + 4 * r + 3 for r in range(ROUNDS)]
        MGE = VALS + 4 * ROUNDS + 1
        MGT = MGE + 1
        V2 = MGT + 4
        SEL = V2 + 3
        G0 = SEL + 8
        YG = G0 + TT + 1
        HB = [YG + 3] + [YG + 4 + 3 * e for e in range(NE - 1)]
        OLO = [YG + 6 + 3 * e for e in range(NE - 1)] + [YG + 5 + 3 * (NE - 1)]
        OUT_READY = [OLO[-1] + 1, OLO[-1] + 2]
        PE_BEFORE_SEARCH = 9
        SEARCH_GROUPS = [3, 3, 2, 2, 2, 2, 2]
        SEARCH = [PE_BEFORE_SEARCH + r + 1 + sum(SEARCH_GROUPS[:r]) for r in range(ROUNDS)]
        VN_FULL = PE_BEFORE_SEARCH + ROUNDS + 2 * NE + 1
        MASK_FULL = VN_FULL + 2
        TOT_FULL = MASK_FULL + 3
        G_FULL = TOT_FULL + 1
        f = G_FULL + TT
        HID = [f] + [f + 1 if e == 1 else f + 3 * (e - 1) for e in range(1, NE)]
        DOWN = [f + 2] + [f + 1 + 3 * e for e in range(1, NE - 1)] + [f + 3 * (NE - 1)]
        SCAT = [f + 5 + 3 * e for e in range(NE - 2)] + [f + 3 * (NE - 1) + 1, f + 3 * (NE - 1) + 2]
        WT0 = 4
        GT0 = WT0 + 2 * NE
        GELU0 = GT0 + TT + 1

        def pass_wait(eng):
            eng.sem_inc(passed, 1)

        blk = ctx.enter_context(nc.Block())

        @blk.sync
        def _(sp):
            sp.dma_start(wq[:, :], Wq).then_inc(ld_wq, 16)
            sp.dma_start(wkv[:, :], Wkv).then_inc(ld_wkv, 16)
            sp.dma_start(xin[:, :, :], x.rearrange("b n c -> n b c")).then_inc(ld_x, 16)
            sp.dma_start(wqkv[:, :], W_qkv).then_inc(ld_qkv, 16)
            sp.dma_start(cf[0][:, :, :], ctx_768[0].rearrange("(p c) e -> p c e", p=KP)).then_inc(ld_ctx[0], 16)
            sp.dma_start(cf[1][:, :, :], ctx_768[1].rearrange("(p c) e -> p c e", p=KP)).then_inc(ld_ctx[1], 16)
            sp.dma_start(wproj[:, :, :], Wproj.rearrange("(a p) c -> p a c", p=P)).then_inc(ld_small, 16)
            sp.wait_ge(mu_ready, 8)
            sp.dma_start(fc1[:, :, :], fc1s.rearrange("e (f p) c -> p (e f) c", p=P)).then_inc(ld_ffn, 16)
            sp.dma_start(fc2[:, :, :], fc2s.rearrange("e c f -> c e f")).then_inc(ld_ffn, 16)

            def load_context(s, b, tiles):
                sp.wait_ge(pv_done, tiles)
                sp.dma_start(cf[s][:, :, :], ctx_768[b].rearrange("(p c) e -> p c e", p=KP)).then_inc(ld_ctx[s], 16)

            with sp.Fori(1, B // 2) as p:
                for h in range(2):
                    load_context(h, p * 2 + h, p * (2 * TILES) + (h * TILES - TILES))
            sp.wait_ge(x1_ready, B)
            for h in range(2):
                sp.dma_start(x1p[h * N:(h + 1) * N, :, :], x1[:, h::2, :]).then_inc(ld_x1, 16)
            o = out.rearrange("b n c -> (b n) c").rearrange("(j t) c -> t j c", t=CAP)
            for g in range(2):
                sp.wait_ge(f_dve, OUT_READY[g])
                sp.dma_start(o[:, 4 * g:4 * g + 4, :], res[:, 4 * g:4 * g + 4, :]).then_inc(stored, 16)
            sp.wait_ge(stored, 32)

        @blk.gpsimd
        def _(pool):
            steps = [0]

            def made(ins):
                steps[0] += 1
                ins.then_inc(const_ready, 1)

            def follows():
                pool.wait_ge(const_ready, steps[0])

            made(pool.memset(ident[:, :], 0.0))
            made(pool.memset(headmask[:, :], 1.0))
            made(pool.memset(neghalf[:, :], -0.5))
            made(pool.memset(tri[:, :], 1.0))
            made(pool.memset(block[:, :], 1.0))
            made(pool.memset(ones16[:, :], 1.0))
            made(pool.memset(onesrow[:, :], 1.0))
            made(pool.iota(iota_i[:, :], pattern=[[1, CAP]], base=1, channel_multiplier=0))
            made(pool.iota(jcol_i[:, :], pattern=[[-REP, NE]], base=0, channel_multiplier=1))
            follows()
            made(pool.affine_select(out=ident[:, :], in_=ident[:, :], compare_op=ALU.not_equal, fill=1.0, base=0,
                                    pattern=[[-1, P]], channel_multiplier=1))
            made(pool.affine_select(out=headmask[:, :], in_=headmask[:, :], compare_op=ALU.is_ge, fill=0.0, base=0,
                                    pattern=[[-DH, H]], channel_multiplier=1))
            made(pool.affine_select(out=tri[:, :], in_=tri[:, :], compare_op=ALU.is_ge, fill=0.0, base=0,
                                    pattern=[[1, CAP]], channel_multiplier=-1))
            made(pool.affine_select(out=block[:, :], in_=block[:, :], compare_op=ALU.is_ge, fill=0.0, base=-1,
                                    pattern=[[-REP, NE], [0, REP]], channel_multiplier=1))
            made(pool.tensor_copy(iota1[:, :], iota_i[:, :]))
            made(pool.tensor_copy(jcol8[:, :], jcol_i[:, :]))
            follows()
            made(pool.affine_select(out=jcol8[:, :], in_=jcol8[:, :], compare_op=ALU.is_ge, fill=0.0, base=0,
                                    pattern=[[-REP, NE]], channel_multiplier=1))
            made(pool.tensor_copy(ident16[:, :], ident[:, :]))
            made(pool.affine_select(out=headmask[:, :], in_=headmask[:, :], compare_op=ALU.is_ge, fill=0.0, base=DH - 1,
                                    pattern=[[DH, H]], channel_multiplier=-1))
            made(pool.affine_select(out=block[:, :], in_=block[:, :], compare_op=ALU.is_ge, fill=0.0, base=REP - 1,
                                    pattern=[[REP, NE], [0, REP]], channel_multiplier=-1))
            follows()
            made(pool.affine_select(out=jcol8[:, :], in_=jcol8[:, :], compare_op=ALU.is_ge, fill=0.0, base=REP - 1,
                                    pattern=[[REP, NE]], channel_multiplier=-1))
            assert steps[0] == CONSTS, steps[0]

            def rstd(p, h, k):
                pool.wait_ge(aggr_done, count(p, h, 2, k + 1))
                pass_wait(pool)
                pool.tensor_scalar(ve[:, :], mv[:, 1:2], EPS, None, ALU.add).then_inc(eps_done, 1)
                pool.wait_ge(eps_done, count(p, h, 2, k + 1))
                pool.tensor_tensor(rs[:, :], ve[:, :], neghalf[0:N, 0:1], ALU.pow).then_inc(rstd_done, 1)

            def split_context(p, h, s):
                pool.wait_ge(ld_ctx[s], (p + 1) * 16)
                wait(pool, ctA_ready, count(p, h, 2, 0))
                wait(pool, ctB_ready, count(p, h, 1, 0))
                pass_wait(pool)
                pool.tensor_copy(chi[:, :, :], cf[s][:, :, :]).then_inc(cs_ready, 1)
                pool.wait_ge(cs_ready, count(p, h, 2, 1))
                pool.tensor_tensor(clo[:, :, :], cf[s][:, :, :], chi[:, :, :], ALU.subtract).then_inc(cs_ready, 1)

            def prepare(p, h):
                rstd(p, h, 0)
                split_context(p, h, h)
                rstd(p, h, 1)

            pool.wait_ge(const_ready, CONSTS)
            prepare(0, 0)
            prepare(0, 1)
            with pool.Fori(1, B // 2) as p:
                prepare(p, 0)
                prepare(p, 1)

            def f_rstd(n, after):
                pool.wait_ge(f_dve, after)
                pool.tensor_scalar(fve[:, :], fmv[:, :, 1], EPS, None, ALU.add).then_inc(f_pool, 1)
                pool.wait_ge(f_pool, n)
                pool.tensor_tensor(frs[:, :], fve[:, :], neghalf[0:CAP, :], ALU.pow).then_inc(f_pool, 1)

            f_rstd(1, AGGR3)
            f_rstd(3, AGGR4)
            pool.wait_ge(f_dve, NORM4)
            pool.tensor_tensor(y1[:, :, :], y1[:, :, :], gam[:, :].unsqueeze(1).to_broadcast([CAP, TT, C]),
                               ALU.mult).then_inc(f_pool, 1)
            pool.wait_ge(f_pool, 5)
            pool.tensor_tensor(y1[:, :, :], y1[:, :, :], bet[:, :].unsqueeze(1).to_broadcast([CAP, TT, C]),
                               ALU.add).then_inc(f_pool, 1)
            pool.wait_ge(f_pool, 6)
            pool.tensor_copy(yhi[:, :, :], y1[:, :, :]).then_inc(f_pool, 1)
            pool.wait_ge(f_pool, 7)
            pool.tensor_tensor(ylo[:, :, :], y1[:, :, :], yhi[:, :, :], ALU.subtract).then_inc(f_pool, 1)

        @blk.tensor
        def _(pe):
            def prep(name, p, h):
                m = use_bank(name)
                s = h
                wait_bank_read(pe, p, h, name)
                if name == "xT":
                    pe.wait_ge(norm_done, count(p, h, 2, 1))
                    pass_wait(pe)
                    ins = pe.transpose(m[:, 0:N], xn[:, :], ident[0:N, 0:N])
                elif name == "qkv":
                    pe.wait_ge(xT_ready, count(p, h, 2, 1))
                    pe.matmul(m[:, 0:N], wqkv[:, 0:C], xT[:, :], start=True, stop=True)
                    pe.matmul(m[:, N:2 * N], wqkv[:, C:2 * C], xT[:, :], start=True, stop=True)
                    ins = pe.matmul(m[0:N, P:2 * P], xT[:, :], wqkv[:, 2 * C:3 * C], start=True, stop=True)
                elif name == "S":
                    pe.wait_ge(qkv_ready, count(p, h, 1, 1))
                    q = qblk[:, :, :].rearrange("c h n -> c (h n)")
                    for t in range(TILES):
                        ins = pe.matmul(m[:, t * N:(t + 1) * N], q[:, t * P:(t + 1) * P], kT[:, :],
                                        start=True, stop=True)
                elif name in ("PT0", "PT1"):
                    pe.wait_ge(en_ready, count(p, h, 1, 1))
                    pass_wait(pe)
                    first = 0 if name == "PT0" else 4
                    for t in range(first, min(first + 4, TILES)):
                        ins = pe.transpose(m[0:N, (t - first) * P:(t - first + 1) * P], en[:, t, :], ident[:, :])
                elif name == "PV":
                    pe.wait_ge(aT_ready, count(p, h, 2, 2))
                    pass_wait(pe)
                    for k in range(H):
                        ins = pe.matmul(m[0:N, k * DH:(k + 1) * DH], aT[:, k * N:(k + 1) * N],
                                        v[:, k * DH:(k + 1) * DH], start=True, stop=True)
                elif name == "aoT":
                    pe.wait_ge(ao_ready, count(p, h, 1, 1))
                    pass_wait(pe)
                    ins = pe.transpose(m[:, 0:N], ao[:, :], ident[0:N, 0:N])
                elif name == "y":
                    pe.wait_ge(aoT_ready, count(p, h, 1, 1))
                    ins = pe.matmul(m[0:N, 0:C], aoT[:, :], wout[:, :], start=True, stop=True)
                elif name == "x1T":
                    pe.wait_ge(norm_done, count(p, h, 2, 2))
                    pass_wait(pe)
                    ins = pe.transpose(m[:, 0:N], xn[:, :], ident[0:N, 0:N])
                elif name in ("q0", "q1"):
                    pe.wait_ge(xT_ready, count(p, h, 2, 2))
                    first = 0 if name == "q0" else H // 2
                    for k in range(H // 2):
                        ins = pe.matmul(m[0:E, k * N:(k + 1) * N], M[:, first + k, :], x1T[:, :],
                                        start=True, stop=True)
                else:
                    pe.wait_ge(cs_ready, count(p, h, 2, 2))
                    m16 = m[:, :].bitcast(F16).rearrange("p (j k) -> p j k", k=P)
                    first = 8 * "ABC".index(name[1])
                    for j in range(first, first + 8):
                        src = chi if j < KC else clo
                        ins = pe.transpose(m16[0:E, j - first, 0:KP], src[:, j % KC, :], ident16[0:KP, 0:KP])
                ins.then_inc(misc_full, 1)

            def scores(p, h, t, k):
                if t == 0 and k == 0:
                    pe.wait_ge(qlo_ready, count(p, h, 2, 2))
                    pe.wait_ge(ctA_ready, count(p, h, 2, 1))
                    pe.wait_ge(ctB_ready, count(p, h, 1, 1))
                if t == 0 and k == 1:
                    pe.wait_ge(ctA_ready, count(p, h, 2, 2))
                wait(pe, exp_done, count(p, h, 3 * TILES, 3 * t + k - 2))
                rows = slice(t * P, (t + 1) * P)
                hi = cT[h][:, 0, GB * k:GB * k + GB, :].rearrange("e b k -> e (b k)")
                lo = cT[h][:, 1, GB * k:GB * k + GB, :].rearrange("e b k -> e (b k)")
                o = SC[k][:, 0:GW]
                pe.matmul(o, qhi[h][:, rows], hi, start=True, stop=False)
                pe.matmul(o, qhi[h][:, rows], lo, start=False, stop=False)
                pe.matmul(o, qlo[h][:, rows], hi, start=False, stop=True).then_inc(sc_full, 1)

            def turn(p, h, t, k):
                pe.wait_ge(exp_done, count(p, h, 3 * TILES, 3 * t + k + 1))
                if k == 0:
                    wait(pe, pTA_ready, count(p, h, 2 * TILES, 2 * t))
                elif k == 1:
                    wait(pe, pTB_ready, count(p, h, TILES, t))
                else:
                    pe.wait_ge(pTA_ready, count(p, h, 2 * TILES, 2 * t + 1))
                src = prob[(h * TILES + t) % 2]
                for j in range(GB):
                    c = (GB * k + j) * KP
                    ins = pe.transpose(TP[k][0:KP, j * P:(j + 1) * P], src[:, c:c + KP], ident[:, :])
                ins.then_inc(tp_full, 1)

            def weigh(p, h, t, k):
                if k == 0:
                    wait(pe, oT_ready, count(p, h, TILES, t))
                    pe.wait_ge(pTA_ready, count(p, h, 2 * TILES, 2 * t + 1))
                elif k == 1:
                    pe.wait_ge(pTB_ready, count(p, h, TILES, t + 1))
                else:
                    pe.wait_ge(pTA_ready, count(p, h, 2 * TILES, 2 * t + 2))
                for j in range(GB):
                    ins = pe.matmul(ACC[:, 0:E], pT[k][:, j, :], cf[h][:, GB * k + j, :],
                                    start=(k == 0 and j == 0), stop=(k == GROUPS - 1 and j == GB - 1))
                if k == GROUPS - 1:
                    ins.then_inc(pv_done, 1)

            def turn_out(p, h, t):
                pe.wait_ge(on_ready, count(p, h, TILES, t))
                pe.transpose(ACC[0:E, P:2 * P], on[:, :], ident[:, :]).then_inc(oT_full, 1)

            AT = {(0, "c"): ["xT"], (1, "a"): ["qkv"], (2, "a"): ["S"], (3, "b"): ["PT0", "PT1"],
                  (3, "d"): ["PV"], (4, "a"): ["aoT"], (4, "b"): ["y"], (4, "c"): ["cA"], (4, "d"): ["cB"],
                  (5, "a"): ["x1T"], (5, "b"): ["q0", "q1"], (5, "c"): ["cC"]}

            def half(p, h, first=False, last=False):
                np_, nh = (p, 1) if h == 0 else (p + 1, 0)

                def prepare(t, place):
                    if not last:
                        for name in AT.get((t, place), []):
                            prep(name, np_, nh)

                for t in range(TILES):
                    nxt = (p, h, t + 1) if t < TILES - 1 else (np_, nh, 0)
                    more = not (last and t == TILES - 1)
                    turn(p, h, t, 0)
                    if more:
                        scores(*nxt, 0)
                    if not (first and t == 0):
                        turn_out(p, h, t)
                    prepare(t, "a")
                    turn(p, h, t, 1)
                    if more:
                        scores(*nxt, 1)
                        scores(*nxt, 2)
                    prepare(t, "b")
                    weigh(p, h, t, 0)
                    turn(p, h, t, 2)
                    prepare(t, "c")
                    weigh(p, h, t, 1)
                    weigh(p, h, t, 2)
                    prepare(t, "d")

            pe.wait_ge(const_ready, CONSTS)
            pe.wait_ge(ld_wq, 16)
            for g in range(2):
                for a in range(4):
                    ins = pe.transpose(bank[g][:, a * P:(a + 1) * P], wq[:, (4 * g + a) * P:(4 * g + a + 1) * P],
                                       ident[:, :])
                ins.then_inc(wT_full, 1)
            pe.wait_ge(ld_wkv, 16)
            for g in range(2, 6):
                if g >= 4:
                    pe.wait_ge(wT_ready, g - 3)
                for a in range(4):
                    c = (4 * (g - 2) + a) * P
                    ins = pe.transpose(bank[g % 4][:, a * P:a * P + E], wkv[:, c:c + P], ident[0:E, 0:E])
                ins.then_inc(wT_full, 1)
            pe.wait_ge(wT_ready, 4)
            for g in range(4):
                for k in range(4):
                    a, q = 4 * (g // 2) + k, g % 2
                    ins = pe.matmul(bank[4 + g][:, k * P:k * P + E], wqT[q * DK:(q + 1) * DK, a, :],
                                    wkT[q * DK:(q + 1) * DK, a, :], start=True, stop=True)
                ins.then_inc(mu_full, 1)
            pe.wait_ge(wT_ready, 6)
            pe.wait_ge(ld_small, LD_SMALL)
            for g in range(4):
                for k in range(4):
                    a, q = 4 * (g // 2) + k, g % 2
                    ins = pe.matmul(bank[g][0:E, k * P:(k + 1) * P], wvT[q * DK:(q + 1) * DK, a, :],
                                    wproj[q * DK:(q + 1) * DK, a, :], start=True, stop=True)
                ins.then_inc(mu_full, 1)
            pe.wait_ge(mu_ready, 8)
            pe.wait_ge(ld_qkv, 32)
            for name in USES:
                prep(name, 0, 0)
            for k in range(GROUPS):
                scores(0, 0, 0, k)
            half(0, 0, first=True)
            half(0, 1)
            with pe.Fori(1, B // 2 - 1) as p:
                half(p, 0)
                half(p, 1)
            half(B // 2 - 1, 0)
            half(B // 2 - 1, 1, last=True)
            turn_out(B // 2, 0, 0)

            def done(ins):
                ins.then_inc(f_pe, 1)

            pe.wait_ge(oT_ready, B * TILES)
            for g in range(2):
                for k in range(H):
                    ins = pe.matmul(bank[g][:, 0:HALF], U[:, k, :],
                                    oT[:, g * B // 2:(g + 1) * B // 2, k * N:(k + 1) * N],
                                    start=(k == 0), stop=(k == H - 1))
                done(ins)
            for g in range(2):
                pe.wait_ge(f_dve, 1 + g)
                for a in range(4):
                    j = 4 * g + a
                    ins = pe.transpose(bank[2 + g][0:CAP, a * P:(a + 1) * P], yT[:, j * CAP:(j + 1) * CAP],
                                       ident[:, :])
                done(ins)
            pe.wait_ge(ld_small, LD_SMALL)
            pe.transpose(bank[6][:, 0:NE], gate[:, :], ident[0:NE, 0:NE])
            ins = pe.transpose(bank[6][:, P:P + NE * FC], b1r[:, :], ident[0:NE * FC, 0:NE * FC])
            done(ins)
            pe.wait_ge(f_dve, NORM3)
            for g in range(2):
                for a in range(4):
                    j = 4 * g + a
                    ins = pe.transpose(bank[4 + g][:, a * CAP:(a + 1) * CAP], xf[:, j, :], ident[0:CAP, 0:CAP])
                done(ins)
            pe.wait_ge(f_dve, GATE_T)
            for g in range(2):
                pe.wait_ge(f_act, 1 + g)
                ins = pe.matmul(bank[6 + g][:, 0:HALF], gateT[:, :, :].rearrange("c e r -> c (e r)"),
                                xfT[:, g * HALF:(g + 1) * HALF], start=True, stop=True)
                done(ins)
            pe.wait_ge(ld_ffn, LD_FFN)
            def turn_weights(g):
                if g >= 2:
                    pe.wait_ge(f_act, WT0 + g - 1)
                for a in range(4):
                    if g < NE:
                        src = fc1[:, 4 * g + a, :]
                    else:
                        src = fc2[:, g - NE, a * P:(a + 1) * P]
                    ins = pe.transpose(bank[1 + g % 2][:, a * P:(a + 1) * P], src, ident[:, :])
                done(ins)

            assert 9 == PE_BEFORE_SEARCH
            g = 0
            for r in range(ROUNDS):
                pe.wait_ge(f_dve, FLAG[r])
                done(pe.matmul(bank[0][:, 0:1], block[:, :], flag[:, :], start=True, stop=True))
                for _ in range(SEARCH_GROUPS[r]):
                    turn_weights(g)
                    g += 1
            assert g == 2 * NE
            pe.wait_ge(f_dve, VALS)
            for g in range(2):
                for a in range(4):
                    j = 4 * g + a
                    ins = pe.transpose(bank[3 + g][0:CAP, a * P:(a + 1) * P], vals[:, j * CAP:(j + 1) * CAP],
                                       ident[:, :])
                done(ins)
            for g, (m, after) in enumerate(((mge, MGE), (mgt, MGT))):
                pe.wait_ge(f_dve, after)
                m16 = bank[5 + g][:, :].bitcast(F16).rearrange("p (j k) -> p j k", k=P)
                for j in range(TT):
                    ins = pe.transpose(m16[0:CAP, j, :], m[:, j * CAP:(j + 1) * CAP], ident16[:, :])
                done(ins)
            pe.wait_ge(f_dve, SEL)
            cum = bank[7][0:CAP, 0:2 * TT * NE].rearrange("p (k j e) -> p k j e", k=2, e=NE)
            pe.matmul(cum, tri[:, :], sel[:, :, :, :], start=True, stop=False, skip_group_check=True)
            for s in range(1, TT):
                ins = pe.matmul(cum[:, :, s:TT, :], ones16[:, :], sel[:, :, 0:TT - s, :], start=False,
                                stop=(s == TT - 1), skip_group_check=True)
            done(ins)
            for j in range(TT):
                ins = pe.matmul(bank[0][0:CAP, 0:NE], ones16[:, :], sel[:, 0, j, :], start=(j == 0),
                                stop=(j == TT - 1))
            done(ins)
            pe.wait_ge(f_pool, 8)
            pe.wait_ge(f_dve, V2)
            pe.wait_ge(f_act, GT0)
            for j in range(TT):
                pe.wait_ge(f_dve, G0 + j)
                gj = G[:, j, :, :].rearrange("p e s -> p (e s)")
                for g in range(2):
                    for part, w in enumerate((yhi, ylo)):
                        pe.matmul(bank[3 + g][:, 0:HALF], w[:, j, :], gj[:, g * HALF:(g + 1) * HALF],
                                  start=(j == 0 and part == 0), stop=(j == TT - 1 and part == 1))
                for e in range(NE):
                    ins = pe.matmul(bank[0][0:CAP, P + 2 * e:P + 2 * e + 2], G[:, j, e, :], v2[:, j, e, :],
                                    start=(j == 0 and e == 0), stop=(j == TT - 1), skip_group_check=True)
                if j >= 2:
                    pe.wait_ge(f_act, GT0 + j - 1)
                m16 = bank[1 + j % 2][:, :].bitcast(F16).rearrange("p (e k) -> p e k", k=P)
                for e in range(NE):
                    ins = pe.transpose(m16[0:CAP, e, 0:CAP], G[:, j, e, :], ident16[0:CAP, 0:CAP])
                done(ins)
            def hidden(e):
                if e == 0:
                    pe.wait_ge(f_dve, YG)
                if e >= 2:
                    pe.wait_ge(f_dve, HB[e - 2])
                for a in range(FC):
                    ins = pe.matmul(bank[5 + e % 2][:, a * CAP:(a + 1) * CAP], fc1T[:, FC * e + a, :],
                                    ygT[:, e, :], start=True, stop=True)
                done(ins)

            def down(e):
                pe.wait_ge(f_act, GELU0 + e)
                if e >= 1:
                    pe.wait_ge(f_dve, OLO[e - 1])
                o = bank[7][0:CAP, 0:C]
                for a in range(FC):
                    pe.matmul(o, hg[e % 2][:, a, :], fc2T[:, FC * e + a, :], start=(a == 0), stop=False)
                done(pe.matmul(o, onesrow[:, :], b2r[:, e, :], start=False, stop=True))

            def scatter(e):
                pe.wait_ge(f_dve, OLO[e])
                if e == 0:
                    pe.wait_ge(f_act, GT0 + TT)
                for j in range(TT):
                    for part, w in enumerate((ohi, olo)):
                        ins = pe.matmul(bank[1 + j // 4][0:CAP, (j % 4) * C:(j % 4 + 1) * C], GT[:, e, j, :],
                                        w[e % 2][:, :], start=(e == 0 and j % 4 == 0 and part == 0),
                                        stop=(e == NE - 1 and part == 1), skip_group_check=True)
                done(ins)

            hidden(0)
            for e in range(NE):
                if e + 1 < NE:
                    hidden(e + 1)
                down(e)
                if e >= 1:
                    scatter(e - 1)
            scatter(NE - 1)

        @blk.scalar
        def _(act):
            for a, b, s in ((wout[:, :], W_out, ld_qkv),
                            (bq[:, :], b_qkv[0:C].rearrange("(c a) -> c a", a=1), ld_small),
                            (bk[:, :], b_qkv[C:2 * C].rearrange("(c a) -> c a", a=1), ld_small),
                            (bv[:, :], b_qkv[2 * C:3 * C].partition_broadcast(N), ld_small),
                            (bout[:, :], b_out.partition_broadcast(N), ld_small),
                            (bpr[:, :], bproj.rearrange("(c a) -> c a", a=1), ld_small),
                            (gate[:, :], gate_w, ld_small),
                            (gam[:, :], ln_gamma.partition_broadcast(CAP), ld_small),
                            (bet[:, :], ln_beta.partition_broadcast(CAP), ld_small),
                            (b1r[:, :], b1s.rearrange("e (f p) -> (e f) p", p=P), ld_small),
                            (b2r[:, :, :], b2s.unsqueeze(0), ld_small)):
                act.dma_start(a, b).then_inc(s, 16)
            act.preload_act_table(ACT.Exp)

            def copy(o, i):
                return act.activation(o, i, ACT.Copy)

            for g in range(6):
                act.wait_ge(wT_full, g + 1)
                b = bank[g % 4][:, :].rearrange("p (a k) -> p a k", k=P)
                if g < 2:
                    copy(wqT[:, 4 * g:4 * g + 4, :], b).then_inc(wT_ready, 1)
                else:
                    w = wkT if g < 4 else wvT
                    copy(w[:, 4 * (g % 2):4 * (g % 2) + 4, :], b[:, :, 0:E]).then_inc(wT_ready, 1)
            for g in range(4):
                act.wait_ge(mu_full, g + 1)
                act.activation(M[:, 8 * (g // 2) + g % 2:8 * (g // 2) + 8:2, :],
                               bank[4 + g][:, :].rearrange("p (a k) -> p a k", k=P)[:, :, 0:E],
                               ACT.Copy, scale=SCALE).then_inc(mu_ready, 1)
            for g in range(4):
                act.wait_ge(mu_full, g + 5)
                copy(U[:, 8 * (g // 2) + g % 2:8 * (g // 2) + 8:2, :],
                     bank[g][0:E, :].rearrange("p (a k) -> p a k", k=P)).then_inc(mu_ready, 1)

            def prep(name, p, h):
                if name == "exp":
                    act.wait_ge(es_ready, count(p, h, 1, 1))
                    act.activation(ep[:, :, :], es[:, :, :], ACT.Exp).then_inc(ep_ready, 1)
                    return
                m = use_bank(name)
                wait_full(act, p, h, name)
                if name == "xT":
                    copy(xT[:, :], m[:, 0:N]).then_inc(xT_ready, 1)
                elif name == "x1T":
                    copy(x1T[:, :], m[:, 0:N]).then_inc(xT_ready, 1)
                elif name == "PT0":
                    copy(aT[:, 0:4 * P], m[0:N, :]).then_inc(aT_ready, 1)
                elif name == "PT1":
                    copy(aT[:, 4 * P:ROWS], m[0:N, 0:ROWS - 4 * P]).then_inc(aT_ready, 1)
                elif name == "PV":
                    copy(ao[:, :], m[0:N, 0:C]).then_inc(ao_ready, 1)
                elif name == "aoT":
                    copy(aoT[:, :], m[:, 0:N]).then_inc(aoT_ready, 1)
                elif name in ("q0", "q1"):
                    c = HALF * (name == "q1")
                    copy(qhi[h][:, c:c + HALF], m[0:E, 0:HALF]).then_inc(qhi_ready, 1)
                else:
                    m16 = m[:, :].bitcast(F16).rearrange("p (j k) -> p j k", k=P)
                    first = 8 * "ABC".index(name[1])
                    copy(cT[h][:, :, :, :].rearrange("e a b k -> e (a b) k")[:, first:first + 8, :],
                         m16[0:E, :, 0:KP]).then_inc(ctA_ready, 1)

            def expo(p, h, t):
                act.wait_ge(nmax_ready, count(p, h, TILES, t + 1))
                i = (h * TILES + t) % 2
                for k in range(GROUPS):
                    act.activation(prob[i][:, k * GW:(k + 1) * GW], SC[k][:, 0:GW], ACT.Exp, bias=nmax[:, 0:1],
                                   accum_out=sum3[i][:, k:k + 1]).then_inc(exp_done, 1)

            def take(p, h, t, k):
                act.wait_ge(tp_full, count(p, h, 3 * TILES, 3 * t + k + 1))
                copy(pT[k][:, :, :].rearrange("p j k -> p (j k)"), TP[k][0:KP, :]).then_inc(pTA_ready, 1)

            def take_out(p, h, t, b):
                act.wait_ge(oT_full, count(p, h, TILES, t))
                copy(oT[:, b, ((t - 1) % TILES) * P:((t - 1) % TILES + 1) * P], ACC[0:E, P:2 * P]).then_inc(oT_ready, 1)

            AT = {(0, "c"): ["xT"], (2, "c"): ["exp"], (3, "b"): ["PT0", "PT1"], (3, "d"): ["PV"],
                  (4, "a"): ["aoT"], (4, "c"): ["cA"], (5, "a"): ["x1T"], (5, "b"): ["q0", "q1"], (5, "c"): ["cC"]}

            def half(p, h, first=False, last=False):
                np_, nh = (p, 1) if h == 0 else (p + 1, 0)

                def prepare(t, place):
                    if not last:
                        for name in AT.get((t, place), []):
                            prep(name, np_, nh)

                for t in range(TILES):
                    nxt = (p, h, t + 1) if t < TILES - 1 else (np_, nh, 0)
                    take(p, h, t, 0)
                    if not (first and t == 0):
                        take_out(p, h, t, batch(p, h) - (t == 0))
                    prepare(t, "a")
                    prepare(t, "b")
                    take(p, h, t, 2)
                    if not (last and t == TILES - 1):
                        expo(*nxt)
                    prepare(t, "c")
                    prepare(t, "d")

            for name in ("xT", "exp", "PT0", "PT1", "PV", "aoT", "cA", "x1T", "q0", "q1", "cC"):
                prep(name, 0, 0)
            expo(0, 0, 0)
            half(0, 0, first=True)
            half(0, 1)
            with act.Fori(1, B // 2 - 1) as p:
                half(p, 0)
                half(p, 1)
            half(B // 2 - 1, 0)
            half(B // 2 - 1, 1, last=True)
            take_out(B // 2, 0, 0, B - 1)

            def done(ins):
                ins.then_inc(f_act, 1)

            for g in range(2):
                act.wait_ge(f_pe, 6 + g)
                done(copy(xfT[:, g * HALF:(g + 1) * HALF], bank[4 + g][:, 0:HALF]))
            for g in range(2):
                act.wait_ge(f_pe, 8 + g)
                done(act.activation(th[:, g * HALF:(g + 1) * HALF], bank[6 + g][:, 0:HALF], ACT.Tanh))
            g = 0
            for r in range(ROUNDS):
                for _ in range(SEARCH_GROUPS[r]):
                    act.wait_ge(f_pe, PE_BEFORE_SEARCH + (r + 1) + g + 1)
                    w = fc1T if g < NE else fc2T
                    a = 4 * (g % NE)
                    done(copy(w[:, a:a + 4, :].rearrange("p a k -> p (a k)"), bank[1 + g % 2][:, :]))
                    g += 1
            for j in range(TT):
                act.wait_ge(f_pe, G_FULL + j)
                m16 = bank[1 + j % 2][:, :].bitcast(F16).rearrange("p (e k) -> p e k", k=P)
                done(copy(GT[:, :, j, :], m16[0:CAP, :, 0:CAP]))
            for e in range(NE):
                act.wait_ge(f_dve, HB[e])
                if e >= 2:
                    act.wait_ge(f_pe, DOWN[e - 2])
                done(act.activation(hg[e % 2][:, :, :], hb[e % 2][:, :, :], ACT.Gelu_apprx_tanh))

        @blk.vector
        def _(dve):
            def bc(ap, shape, axis):
                return ap.unsqueeze(axis).to_broadcast(shape)

            def stats(src, p, h, k):
                wait(dve, norm_done, count(p, h, 2, k))
                pass_wait(dve)
                dve.bn_stats(st[:, :], src).then_inc(stats_done, 1)
                dve.wait_ge(stats_done, count(p, h, 2, k + 1))
                wait(dve, rstd_done, count(p, h, 2, k))
                pass_wait(dve)
                dve.bn_aggr(mv[:, :], st[:, :]).then_inc(aggr_done, 1)

            def norm(src, p, h, k):
                dve.wait_ge(rstd_done, count(p, h, 2, k + 1))
                dve.tensor_scalar(xn[:, :], src, mv[:, 0:1], rs[:, 0:1], ALU.subtract, ALU.mult).then_inc(norm_done, 1)

            def prep(name, p, h):
                b = batch(p, h)
                m = use_bank(name) if name in USES else None
                if name in USES:
                    wait_full(dve, p, h, name)
                if name == "stats1":
                    stats(xin[:, b, :], p, h, 0)
                elif name == "norm1":
                    norm(xin[:, b, :], p, h, 0)
                elif name == "qkv":
                    dve.scalar_tensor_tensor(qblk[:, :, :], bc(m[:, 0:N], [C, H, N], 1), bq[:, 0:1],
                                             bc(headmask[:, :], [C, H, N], 2), ALU.add, ALU.mult)
                    dve.tensor_scalar(kT[:, :], m[:, N:2 * N], bk[:, 0:1], None, ALU.add)
                    dve.tensor_tensor(v[:, :], m[0:N, P:2 * P], bv[:, :], ALU.add).then_inc(qkv_ready, 1)
                elif name == "S":
                    s = m[:, 0:TILES * N].rearrange("p (t n) -> p t n", n=N)
                    dve.tensor_reduce(amax[:, :], s, X, ALU.max, negate=True).then_inc(amax_ready, 1)
                    dve.wait_ge(amax_ready, count(p, h, 1, 1))
                    dve.tensor_tensor(es[:, :, :], s, bc(amax[:, :], [P, TILES, N], 2), ALU.add).then_inc(es_ready, 1)
                elif name == "soft":
                    dve.wait_ge(ep_ready, count(p, h, 1, 1))
                    dve.tensor_reduce(asum[:, :], ep[:, :, :], X, ALU.add).then_inc(asum_ready, 1)
                    dve.wait_ge(asum_ready, count(p, h, 1, 1))
                    dve.reciprocal(arec[:, :], asum[:, :]).then_inc(arec_ready, 1)
                    dve.wait_ge(arec_ready, count(p, h, 1, 1))
                    dve.scalar_tensor_tensor(en[:, :, :], ep[:, :, :], ATT, bc(arec[:, :], [P, TILES, N], 2),
                                             ALU.mult, ALU.mult).then_inc(en_ready, 1)
                elif name == "y":
                    dve.tensor_tensor(x1[:, b, :], m[0:N, 0:C], xb[:, b, :], ALU.add).then_inc(x1_ready, 1)
                    dve.wait_ge(x1_ready, count(p, h, 1, 1))
                    stats(x1[:, b, :], p, h, 1)
                elif name == "norm2":
                    norm(x1[:, b, :], p, h, 1)
                elif name in ("q0", "q1"):
                    k = int(name == "q1")
                    dve.wait_ge(qhi_ready, count(p, h, 2, k + 1))
                    cols = slice(k * HALF, (k + 1) * HALF)
                    dve.tensor_tensor(qlo[h][:, cols], m[0:E, 0:HALF], qhi[h][:, cols],
                                      ALU.subtract).then_inc(qlo_ready, 1)
                elif name == "cB":
                    m16 = m[:, :].bitcast(F16).rearrange("p (j k) -> p j k", k=P)
                    dve.tensor_copy(cT[h][:, :, :, :].rearrange("e a b k -> e (a b) k")[:, 8:16, :],
                                    m16[0:E, :, 0:KP]).then_inc(ctB_ready, 1)

            def maxima(p, h, t):
                for k in range(GROUPS):
                    dve.wait_ge(sc_full, count(p, h, 3 * TILES, 3 * t + k + 1))
                    if k == 0:
                        wait(dve, nmax_ready, count(p, h, TILES, t))
                    dve.tensor_reduce(mx3[:, k:k + 1], SC[k][:, 0:GW], X, ALU.max).then_inc(mx_done, 1)
                dve.wait_ge(mx_done, count(p, h, 3 * TILES, 3 * t + 3))
                wait(dve, exp_done, count(p, h, 3 * TILES, 3 * t))
                dve.tensor_reduce(nmax[:, :], mx3[:, :], X, ALU.max, negate=True).then_inc(nmax_ready, 1)

            def take(p, h, t):
                dve.wait_ge(tp_full, count(p, h, 3 * TILES, 3 * t + 2))
                dve.tensor_copy(pT[1][:, :, :].rearrange("p j k -> p (j k)"), TP[1][0:KP, :]).then_inc(pTB_ready, 1)

            def normalise(p, h, t):
                i = (h * TILES + t + 1) % 2
                dve.wait_ge(exp_done, count(p, h, 3 * TILES, 3 * t))
                wait(dve, on_ready, count(p, h, TILES, t - 1))
                dve.tensor_reduce(den[:, :], sum3[i][:, :], X, ALU.add).then_inc(den_ready, 1)
                dve.wait_ge(den_ready, count(p, h, TILES, t))
                dve.reciprocal(rden[:, :], den[:, :]).then_inc(rden_ready, 1)
                dve.wait_ge(rden_ready, count(p, h, TILES, t))
                dve.wait_ge(pv_done, count(p, h, TILES, t))
                wait(dve, oT_full, count(p, h, TILES, t - 1))
                dve.tensor_scalar(on[:, :], ACC[:, 0:E], rden[:, 0:1], None, ALU.mult).then_inc(on_ready, 1)

            AT = {(0, "a"): ["stats1"], (0, "b"): ["norm1"], (1, "b"): ["qkv"], (2, "b"): ["S"], (3, "a"): ["soft"],
                  (4, "c"): ["y"], (4, "d"): ["cB"], (5, "a"): ["norm2"], (5, "b"): ["q0", "q1"]}

            def half(p, h, first=False, last=False):
                np_, nh = (p, 1) if h == 0 else (p + 1, 0)

                def prepare(t, place):
                    if not last:
                        for name in AT.get((t, place), []):
                            prep(name, np_, nh)

                for t in range(TILES):
                    nxt = (p, h, t + 1) if t < TILES - 1 else (np_, nh, 0)
                    if not (first and t == 0):
                        normalise(p, h, t)
                    prepare(t, "a")
                    take(p, h, t)
                    if not (last and t == TILES - 1):
                        maxima(*nxt)
                    prepare(t, "b")
                    prepare(t, "c")
                    prepare(t, "d")

            dve.wait_ge(const_ready, CONSTS)
            dve.wait_ge(ld_x, 16)
            prep("stats1", 0, 0)
            prep("norm1", 0, 0)
            dve.wait_ge(ld_small, LD_SMALL)
            dve.tensor_tensor(xb[:, :, :], xin[:, :, :], bc(bout[:, :], [N, B, C], 1), ALU.add).then_inc(xb_ready, 1)
            dve.wait_ge(xb_ready, 1)
            for name in ("qkv", "S", "soft", "y", "cB", "norm2", "q0", "q1"):
                prep(name, 0, 0)
            maxima(0, 0, 0)
            half(0, 0, first=True)
            half(0, 1)
            with dve.Fori(1, B // 2 - 1) as p:
                half(p, 0)
                half(p, 1)
            half(B // 2 - 1, 0)
            half(B // 2 - 1, 1, last=True)
            normalise(B // 2, 0, 0)

            n = [0]

            def done(ins, at=None):
                n[0] += 1
                ins.then_inc(f_dve, 1)
                assert at is None or at == n[0], (at, n[0])

            def settle():
                dve.wait_ge(f_dve, n[0])

            for g in range(2):
                dve.wait_ge(f_pe, 1 + g)
                done(dve.tensor_scalar(yT[:, g * HALF:(g + 1) * HALF], bank[g][:, 0:HALF], bpr[:, 0:1], None, ALU.add))
            dve.wait_ge(ld_x1, 32)
            for g in range(2):
                dve.wait_ge(f_pe, 3 + g)
                done(dve.tensor_tensor(x2[:, 4 * g:4 * g + 4, :],
                                       bank[2 + g][0:CAP, :].rearrange("p (a k) -> p a k", k=P),
                                       x1p[:, 4 * g:4 * g + 4, :], ALU.add))

            def f_stats(src, at):
                settle()
                for j in range(TT):
                    done(dve.bn_stats(fst[:, j, :], src[:, j, :]))
                settle()
                for j in range(TT):
                    done(dve.bn_aggr(fmv[:, j, :], fst[:, j, :]), at if j == TT - 1 else None)

            def f_norm(dst, src, pool_steps, at):
                dve.wait_ge(f_pool, pool_steps)
                settle()
                for j in range(TT):
                    done(dve.tensor_scalar(dst[:, j, :], src[:, j, :], fmv[:, j, 0:1], frs[:, j:j + 1],
                                           ALU.subtract, ALU.mult), at if j == TT - 1 else None)

            f_stats(x2, AGGR3)
            f_norm(xf, x2, 2, NORM3)
            dve.wait_ge(f_pe, 5)
            done(dve.tensor_copy(gateT[:, :, :], bc(bank[6][:, 0:NE], [C, NE, REP], 2)))
            done(dve.tensor_copy(b1T[:, :, :], bank[6][:, P:P + NE * FC].rearrange("p (e f) -> p e f", f=FC)), GATE_T)
            f_stats(xf, AGGR4)
            f_norm(y1, xf, 4, NORM4)
            done(dve.tensor_tensor(base[:, :, :], x2[:, :, :], xf[:, :, :], ALU.add))
            done(dve.tensor_reduce(jcol[:, :], jcol8[:, :], X, ALU.add))
            done(dve.memset(low[:, :], 0.0))
            for g in range(2):
                dve.wait_ge(f_act, 3 + g)
                done(dve.tensor_scalar(vals[:, g * HALF:(g + 1) * HALF], th[:, g * HALF:(g + 1) * HALF], 1.0, 0.5,
                                       ALU.add, ALU.mult), VALS if g else None)
            for r in range(ROUNDS):
                step = 2.0 ** -(3 + 4 * r)
                settle()
                done(dve.tensor_scalar(thr[:, :], jcol[:, :], step, low[:, 0:1], ALU.mult, ALU.add))
                settle()
                done(dve.tensor_scalar(junk[:, :], vals[:, :], thr[:, 0:1], None, ALU.is_ge, ALU.add,
                                       accum_out=cnt[:, :]))
                settle()
                done(dve.tensor_scalar(flag[:, :], cnt[:, :], float(CAP), None, ALU.is_ge), FLAG[r])
                dve.wait_ge(f_pe, SEARCH[r])
                done(dve.tensor_scalar(low[:, :], bank[0][:, 0:1], step, low[:, 0:1], ALU.mult, ALU.add))
            settle()
            done(dve.tensor_scalar(mge[:, :], vals[:, :], low[:, 0:1], None, ALU.is_ge), MGE)
            done(dve.tensor_scalar(mgt[:, :], vals[:, :], low[:, 0:1], None, ALU.is_gt), MGT)
            for g in range(2):
                dve.wait_ge(f_pe, VN_FULL + g)
                done(dve.tensor_copy(vn[:, 4 * g:4 * g + 4, :],
                                     bank[3 + g][0:CAP, :].rearrange("p (a e r) -> p a e r", a=4, r=REP)[:, :, :, 0]))
            settle()
            done(dve.tensor_copy(v2[:, :, :, 0], vn[:, :, :]))
            settle()
            done(dve.tensor_tensor(v2[:, :, :, 1], vn[:, :, :], v2[:, :, :, 0], ALU.subtract), V2)
            mask = [bank[5 + g][0:CAP, :].bitcast(F16).rearrange("p (j e r) -> p j e r", e=NE, r=REP)[:, :, :, 0]
                    for g in range(2)]
            dve.wait_ge(f_pe, MASK_FULL)
            done(dve.tensor_copy(ge[:, :, :], mask[0]))
            dve.wait_ge(f_pe, MASK_FULL + 1)
            done(dve.tensor_copy(sel[:, 0, :, :], mask[1]))
            settle()
            done(dve.tensor_tensor(sel[:, 1, :, :], ge[:, :, :], sel[:, 0, :, :], ALU.subtract), SEL)
            cum = bank[7][0:CAP, 0:2 * TT * NE].rearrange("p (k j e) -> p k j e", k=2, e=NE)
            dve.wait_ge(f_pe, TOT_FULL)
            done(dve.tensor_copy(cg[:, :], bank[0][0:CAP, 0:NE]))
            settle()
            done(dve.tensor_tensor(pa[:, :, :], cum[:, 1, :, :], bc(cg[:, :], [CAP, TT, NE], 1), ALU.add))
            done(dve.tensor_tensor(pb[:, :, :], cum[:, 0, :, :], sel[:, 0, :, :], ALU.mult))
            settle()
            done(dve.tensor_tensor(pa[:, :, :], pa[:, :, :], sel[:, 1, :, :], ALU.mult))
            settle()
            done(dve.tensor_tensor(pa[:, :, :], pa[:, :, :], pb[:, :, :], ALU.add))
            settle()
            done(dve.tensor_scalar(pb[:, :, :], ge[:, :, :], -2.0 * T, 2.0 * T, ALU.mult, ALU.add))
            settle()
            done(dve.tensor_tensor(slot[:, :, :], pa[:, :, :], pb[:, :, :], ALU.add))
            settle()
            for j in range(TT):
                done(dve.tensor_tensor(G[:, j, :, :], bc(iota1[:, :], [CAP, NE, CAP], 1),
                                       bc(slot[:, j, :], [CAP, NE, CAP], 2), ALU.is_equal), G0 + j)
            dve.wait_ge(f_pe, G_FULL + TT - 1)
            for g in range(2):
                done(dve.tensor_copy(ygT[:, 4 * g:4 * g + 4, :],
                                     bank[3 + g][:, 0:HALF].rearrange("p (e s) -> p e s", s=CAP)), YG if g else None)
            done(dve.tensor_copy(w2s[:, :, :], bank[0][0:CAP, P:P + 2 * NE].rearrange("p (e k) -> p e k", k=2)))
            settle()
            done(dve.tensor_tensor(wslot[:, :], w2s[:, :, 0], w2s[:, :, 1], ALU.add))

            def add_b1(e):
                dve.wait_ge(f_pe, HID[e])
                if e >= 2:
                    dve.wait_ge(f_act, GELU0 + e - 2)
                done(dve.tensor_tensor(hb[e % 2][:, :, :], bank[5 + e % 2][:, 0:HALF].rearrange("p (f s) -> p f s", s=CAP),
                                       bc(b1T[:, e, :], [P, FC, CAP], 2), ALU.add), HB[e])

            settle()
            add_b1(0)
            for e in range(NE):
                if e + 1 < NE:
                    add_b1(e + 1)
                dve.wait_ge(f_pe, DOWN[e])
                if e >= 2:
                    dve.wait_ge(f_pe, SCAT[e - 2])
                o = bank[7][0:CAP, 0:C]
                done(dve.tensor_scalar(ohi[e % 2][:, :], o, wslot[:, e:e + 1], None, ALU.mult))
                settle()
                done(dve.scalar_tensor_tensor(olo[e % 2][:, :], o, wslot[:, e:e + 1], ohi[e % 2][:, :],
                                              ALU.mult, ALU.subtract), OLO[e])
            dve.wait_ge(f_pe, SCAT[NE - 1])
            for g in range(2):
                done(dve.tensor_tensor(res[:, 4 * g:4 * g + 4, :],
                                       bank[1 + g][0:CAP, :].rearrange("p (a k) -> p a k", k=P),
                                       base[:, 4 * g:4 * g + 4, :], ALU.add), OUT_READY[g])


_INS = ['x', 'ctx_768', 'L0_attn_W_qkv', 'L0_attn_b_qkv', 'L0_attn_W_out', 'L0_attn_b_out', 'L0_xattn_Wq',
        'L0_xattn_Wkv', 'L0_xattn_Wproj', 'L0_xattn_bproj', 'L0_ffn_gate_w', 'L0_ffn_ln_gamma', 'L0_ffn_ln_beta',
        'L0_ffn_fc1s', 'L0_ffn_b1s', 'L0_ffn_fc2s', 'L0_ffn_b2s']


def kernel(**inputs):
    import numpy as _np
    import concourse.bacc as _bacc
    from concourse import mybir as _mybir
    from concourse.bass_utils import run_bass_kernel_spmd as _run

    nc = _bacc.Bacc("TRN2", target_bir_lowering=False, num_devices=1)
    arrays, args = {}, []
    for name in _INS:
        a = _np.ascontiguousarray(inputs[name])
        arrays[f"in_{name}"] = a
        args.append(nc.dram_tensor(f"in_{name}", a.shape, _mybir.dt.from_np(a.dtype), kind="ExternalInput").ap())
    shape = arrays["in_x"].shape
    args.append(nc.dram_tensor("out_0", shape, _mybir.dt.float32, kind="ExternalOutput").ap())
    decoder_layer(nc, *args)
    r = _run(nc, [arrays], core_ids=[0])
    return r.results[0]["out_0"]
```

```python
from contextlib import ExitStack

import concourse.bass as bass
from concourse import mybir

F32 = mybir.dt.float32
F16 = mybir.dt.float16
I32 = mybir.dt.int32
ALU = mybir.AluOpType
ACT = mybir.ActivationFunctionType
X = mybir.AxisListType.X

P = 128
EPS = 1e-5


def decoder_layer(nc, x, ctx_768, W_qkv, b_qkv, W_out, b_out, Wq, Wkv, Wproj, bproj,
                  gate_w, ln_gamma, ln_beta, fc1s, b1s, fc2s, b2s, out):
    B, N, C = x.shape
    L, E = ctx_768.shape[1:]
    H = 16
    DH = C // H
    DK = Wq.shape[1] // H
    T = B * N
    ROWS = H * N
    TILES = ROWS // P
    KP = 125
    KC = L // KP
    GROUPS = 3
    GB = KC // GROUPS
    GW = GB * KP
    NE, F = fc1s.shape[:2]
    FC = F // P
    CAP = T // NE
    TT = T // CAP
    REP = P // NE
    ROUNDS = 7
    SCALE = float(DK) ** -0.5
    ATT = float(C) ** -0.5
    HALF = T // 2

    ctx = ExitStack()
    with ctx:
        def sb(name, shape, dt=F32):
            return ctx.enter_context(nc.sbuf_tensor(name, shape, dt))

        def sem(name):
            return ctx.enter_context(nc.semaphore(name))

        bank = [ctx.enter_context(nc.psum_tensor(f"bank{i}", [P, 512], F32)) for i in range(8)]
        SC = bank[0:3]
        TP = bank[3:5]
        ACC = bank[5]
        MISC = bank[6:8]

        ident = sb("ident", [P, P])
        ident16 = sb("ident16", [P, P], F16)
        headmask = sb("headmask", [P, H])
        tri = sb("tri", [CAP, CAP], F16)
        ones16 = sb("ones16", [CAP, CAP], F16)
        onesrow = sb("onesrow", [1, CAP])
        block = sb("block", [P, P], F16)
        jcol_i = sb("jcol_i", [P, NE], I32)
        jcol8 = sb("jcol8", [P, NE])
        jcol = sb("jcol", [P, 1])
        iota_i = sb("iota_i", [CAP, CAP], I32)
        iota1 = sb("iota1", [CAP, CAP])
        neghalf = sb("neghalf", [P, TT])

        wqkv = sb("wqkv", [C, 3 * C])
        wout = sb("wout", [C, C])
        bq = sb("bq", [C, 1])
        bk = sb("bk", [C, 1])
        bv = sb("bv", [N, C])
        bout = sb("bout", [1, C])
        bpr = sb("bpr", [C, 1])
        Mhi = sb("Mhi", [C, H, E], F16)
        Mlo = sb("Mlo", [C, H, E], F16)
        U = sb("U", [E, H, C])

        first_space = ExitStack()

        def at_first(name, shape, dt=F32):
            return first_space.enter_context(nc.sbuf_tensor(name, shape, dt))

        wq = at_first("wq", [C, H * DK])
        wkv = at_first("wkv", [E, 2 * H * DK])
        wproj = at_first("wproj", [P, H // 2, C])
        wqT = at_first("wqT", [P, H // 2, C])
        wkT = at_first("wkT", [P, H // 2, E])
        wvT = at_first("wvT", [P, H // 2, E])
        first_space.close()
        fc1 = sb("fc1", [P, NE * FC, C])
        fc2 = sb("fc2", [C, NE, F])

        x1 = sb("x1", [N, B, C])
        gate = sb("gate", [NE, C])
        b1r = sb("b1r", [NE * FC, P])

        oT_space = ExitStack()
        oT = oT_space.enter_context(nc.sbuf_tensor("oT", [E, B, ROWS], F32))

        early_space = ExitStack()

        def early(name, shape, dt=F32):
            return early_space.enter_context(nc.sbuf_tensor(name, shape, dt))

        xin = early("xin", [N, B, C])
        st = [early(f"st{k}", [N, 6]) for k in range(2)]
        mv = [early(f"mv{k}", [N, 2]) for k in range(2)]
        ve = [early(f"ve{k}", [N, 1]) for k in range(2)]
        rs = [early(f"rs{k}", [N, 1]) for k in range(2)]
        xn = [early(f"xn{k}", [N, C]) for k in range(2)]
        xT = early("xT", [C, N])
        kT = early("kT", [C, N])
        v = early("v", [N, C])
        qblk = early("qblk", [C, H, N])
        es = early("es", [P, TILES, N])
        ep = early("ep", [P, TILES, N])
        en = early("en", [P, TILES, N])
        amax = early("amax", [P, TILES])
        asum = early("asum", [P, TILES])
        arec = early("arec", [P, TILES])
        aT = early("aT", [N, ROWS])
        ao = early("ao", [N, C])
        aoT = early("aoT", [C, N])
        x1Thi = early("x1Thi", [C, N], F16)
        x1Tlo = early("x1Tlo", [C, N], F16)
        qT = early("qT", [C, N])

        cf = [early(f"cf{i}", [KP, KC, E]) for i in range(2)]
        cs = [early(f"cs{i}", [KP, 2, KC, E], F16) for i in range(2)]
        cT = [early(f"cT{i}", [E, 2, L], F16) for i in range(2)]
        qhi = [early(f"qhi{i}", [E, ROWS], F16) for i in range(2)]
        qlo = [early(f"qlo{i}", [E, ROWS], F16) for i in range(2)]
        prob = [early(f"prob{i}", [P, L]) for i in range(2)]
        pThi = [[early(f"pThi{k}_{i}", [KP, GB, P], F16) for i in range(2 if k < GROUPS - 1 else 1)]
                for k in range(GROUPS)]
        pTlo = [[early(f"pTlo{k}_{i}", [KP, GB, P], F16) for i in range(2 if k < GROUPS - 1 else 1)]
                for k in range(GROUPS)]
        mx3 = early("mx3", [P, GROUPS])
        nmax = early("nmax", [P, 1])
        sum3 = [early(f"sum3_{i}", [P, GROUPS]) for i in range(2)]
        den = early("den", [P, 1])
        rden = early("rden", [P, 1])
        on = early("on", [P, E])

        early_space.close()
        oT_space.close()

        fc1T = sb("fc1T", [C, NE * FC, P])
        fc2T = sb("fc2T", [P, NE * FC, C])
        G = sb("G", [CAP, TT, NE, CAP], F16)
        th = sb("th", [P, T])
        vals = sb("vals", [P, T])
        mge = sb("mge", [P, T], F16)
        mgt = sb("mgt", [P, T], F16)

        yT = sb("yT", [C, T])
        x2 = sb("x2", [CAP, TT, C])
        xf = sb("xf", [CAP, TT, C])
        base = sb("base", [CAP, TT, C])
        y1 = sb("y1", [CAP, TT, C])
        yhi = sb("yhi", [CAP, TT, C], F16)
        ylo = sb("ylo", [CAP, TT, C], F16)
        fst = sb("fst", [CAP, TT, 6])
        fmv = sb("fmv", [CAP, TT, 2])
        fve = sb("fve", [CAP, TT])
        frs = sb("frs", [CAP, TT])
        gateT = sb("gateT", [C, NE, REP])
        xfT = sb("xfT", [C, T])
        junk = sb("junk", [P, T], F16)
        thr = sb("thr", [P, 1])
        low = sb("low", [P, 1])
        cnt = sb("cnt", [P, 1])
        flag = sb("flag", [P, 1], F16)
        ge = sb("ge", [CAP, TT, NE])
        sel = sb("sel", [CAP, 2, TT, NE], F16)
        vn = sb("vn", [CAP, TT, NE])
        v2 = sb("v2", [CAP, TT, NE, 2], F16)
        cg = sb("cg", [CAP, NE])
        pa = sb("pa", [CAP, TT, NE])
        pb = sb("pb", [CAP, TT, NE])
        slot = sb("slot", [CAP, TT, NE])
        GT = sb("GT", [CAP, NE, TT, CAP], F16)
        wslot = sb("wslot", [CAP, NE])
        w2s = sb("w2s", [CAP, NE, 2])
        ygT = sb("ygT", [C, NE, CAP])
        b1T = sb("b1T", [P, NE, FC])
        hb = [sb(f"hb{i}", [P, FC, CAP]) for i in range(2)]
        hg = [sb(f"hg{i}", [P, FC, CAP]) for i in range(2)]
        ohi = [sb(f"ohi{i}", [CAP, C], F16) for i in range(2)]
        olo = [sb(f"olo{i}", [CAP, C], F16) for i in range(2)]
        res = sb("res", [CAP, TT, C])
        x1p = sb("x1p", [CAP, TT, C])
        gam = sb("gam", [CAP, C])
        bet = sb("bet", [CAP, C])
        b2r = sb("b2r", [1, NE, C])

        ld_x, ld_wq, ld_wkv, ld_qkv, ld_bias, ld_wproj, ld_small, ld_ffn, ld_late = (sem("ld_" + n) for n in (
            "x", "wq", "wkv", "qkv", "bias", "wproj", "small", "ffn", "late"))
        ld_ctx = [sem("ld_ctx0"), sem("ld_ctx1")]
        stored = sem("stored")
        passed = sem("passed")
        const_ready = sem("const_ready")
        wT_full = sem("wT_full")
        wT_ready = sem("wT_ready")
        mu_full = sem("mu_full")
        mu_ready = sem("mu_ready")
        mlo_ready = sem("mlo_ready")
        misc_full = [sem("misc_full0"), sem("misc_full1")]
        stats_done, aggr_done, eps_done, rstd_done, norm_done = ([sem(n + str(k)) for k in range(2)] for n in (
            "stats_done", "aggr_done", "eps_done", "rstd_done", "norm_done"))
        xT_ready, qkv_ready, amax_ready, es_ready, ep_ready, asum_ready, arec_ready, en_ready = (sem(n) for n in (
            "xT_ready", "qkv_ready", "amax_ready", "es_ready", "ep_ready", "asum_ready", "arec_ready", "en_ready"))
        aT_ready, ao_ready, aoT_ready, x1_ready = (sem(n) for n in ("aT_ready", "ao_ready", "aoT_ready", "x1_ready"))
        qT_ready, qblk_ready, arec_scaled, x1Thi_ready, x1Tlo_ready = (sem(n) for n in (
            "qT_ready", "qblk_ready", "arec_scaled", "x1Thi_ready", "x1Tlo_ready"))
        qhi_ready, qlo_ready, cs_ready = (sem(n) for n in ("qhi_ready", "qlo_ready", "cs_ready"))
        cThi_ready, cTlo_ready = sem("cThi_ready"), sem("cTlo_ready")
        sc_full, mx_done, nmax_ready, exp_done = (sem(n) for n in ("sc_full", "mx_done", "nmax_ready", "exp_done"))
        tp_full, pThi_ready, pTlo_ready, pv_done = (sem(n) for n in ("tp_full", "pThi_ready", "pTlo_ready", "pv_done"))
        den_ready, rden_ready, on_ready, oT_full, oT_ready = (sem(n) for n in (
            "den_ready", "rden_ready", "on_ready", "oT_full", "oT_ready"))
        f_pe, f_dve, f_act, f_pool = (sem(n) for n in ("f_pe", "f_dve", "f_act", "f_pool"))

        def count(p, h, per, off):
            return p * (2 * per) + (h * per + off)

        def wait(eng, s, val):
            if isinstance(val, int) and val <= 0:
                return
            eng.wait_ge(s, val)

        USES = [["xT", "qkv", "S", "PT0", "PT1", "c0", "c1"], ["PV", "aoT", "y", "x1T", "c2", "q0", "q1"]]
        READ = {"xT": (xT_ready, 1, 1), "qkv": (qkv_ready, 1, 1), "S": (es_ready, 1, 1),
                "PT0": (aT_ready, 2, 1), "PT1": (aT_ready, 2, 2), "PV": (ao_ready, 1, 1),
                "aoT": (aoT_ready, 1, 1), "y": (x1_ready, 1, 1), "x1T": (x1Tlo_ready, 1, 1),
                "c0": (cTlo_ready, 3, 1), "c1": (cTlo_ready, 3, 2), "c2": (cTlo_ready, 3, 3),
                "q0": (qlo_ready, 2, 1), "q1": (qlo_ready, 2, 2)}

        def stage(name):
            k = int(name in USES[1])
            return (k, USES[k].index(name)) if name in USES[k] else (None, None)

        def wait_full(eng, p, h, name):
            k, n = stage(name)
            eng.wait_ge(misc_full[k], count(p, h, len(USES[k]), n + 1))

        def wait_bank_read(eng, p, h, name):
            k, n = stage(name)
            s, per, off = READ[USES[k][n - 1]]
            wait(eng, s, count(p, h, per, off if n >= 1 else off - per))

        def batch(p, h):
            return p * 2 + h

        def tp_bank(h, t, k):
            return TP[(3 * (h * TILES + t) + k) % 2]

        def parts(h, t, k):
            i = (h * TILES + t) % len(pThi[k])
            return pThi[k][i], pTlo[k][i]

        M_BANK, U_BANK = [0, 1, 2, 3], [4, 5, 0, 1]

        CONSTS = 20
        LD_SMALL = 5 * 16
        LD_LATE = 5 * 16
        LD_FFN = 2 * 16

        AGGR3 = 4 + 2 * TT
        NORM3 = AGGR3 + TT
        GATE_T = NORM3 + 2
        AGGR4 = GATE_T + 2 * TT
        NORM4 = AGGR4 + TT
        VALS = NORM4 + 5
        FLAG = [VALS + 4 * r + 3 for r in range(ROUNDS)]
        MGE = VALS + 4 * ROUNDS + 1
        MGT = MGE + 1
        V2 = MGT + 4
        SEL = V2 + 3
        G0 = SEL + 8
        YG = G0 + TT + 1
        HB = [YG + 3] + [YG + 4 + 3 * e for e in range(NE - 1)]
        OLO = [YG + 6 + 3 * e for e in range(NE - 1)] + [YG + 5 + 3 * (NE - 1)]
        OUT_READY = [OLO[-1] + 1, OLO[-1] + 2]
        PE_BEFORE_SEARCH = 9
        SEARCH_GROUPS = [3, 3, 2, 2, 2, 2, 2]
        SEARCH = [PE_BEFORE_SEARCH + r + 1 + sum(SEARCH_GROUPS[:r]) for r in range(ROUNDS)]
        VN_FULL = PE_BEFORE_SEARCH + ROUNDS + 2 * NE + 1
        MASK_FULL = VN_FULL + 2
        TOT_FULL = MASK_FULL + 3
        G_FULL = TOT_FULL + 1
        f = G_FULL + TT
        HID = [f] + [f + 1 if e == 1 else f + 3 * (e - 1) for e in range(1, NE)]
        DOWN = [f + 2] + [f + 1 + 3 * e for e in range(1, NE - 1)] + [f + 3 * (NE - 1)]
        SCAT = [f + 5 + 3 * e for e in range(NE - 2)] + [f + 3 * (NE - 1) + 1, f + 3 * (NE - 1) + 2]
        WT0 = 4
        GT0 = WT0 + 2 * NE
        GELU0 = GT0 + TT + 1

        def pass_wait(eng):
            eng.sem_inc(passed, 1)

        blk = ctx.enter_context(nc.Block())

        @blk.sync
        def _(sp):
            sp.dma_start(xin[:, :, :], x.rearrange("b n c -> n b c")).then_inc(ld_x, 16)
            sp.dma_start(wq[:, :], Wq).then_inc(ld_wq, 16)
            sp.dma_start(wkv[:, :], Wkv).then_inc(ld_wkv, 16)
            sp.dma_start(wqkv[:, :], W_qkv).then_inc(ld_qkv, 16)
            sp.dma_start(cf[0][:, :, :], ctx_768[0].rearrange("(p c) e -> p c e", p=KP)).then_inc(ld_ctx[0], 16)
            sp.dma_start(cf[1][:, :, :], ctx_768[1].rearrange("(p c) e -> p c e", p=KP)).then_inc(ld_ctx[1], 16)
            sp.dma_start(wproj[:, :, :], Wproj.rearrange("(a p) c -> p a c", p=P)).then_inc(ld_wproj, 16)
            sp.wait_ge(mu_ready, 8)
            sp.dma_start(fc1[:, :, :], fc1s.rearrange("e (f p) c -> p (e f) c", p=P)).then_inc(ld_ffn, 16)
            sp.dma_start(fc2[:, :, :], fc2s.rearrange("e c f -> c e f")).then_inc(ld_ffn, 16)

            def load_context(s, b):
                sp.dma_start(cf[s][:, :, :], ctx_768[b].rearrange("(p c) e -> p c e", p=KP)).then_inc(ld_ctx[s], 16)

            with sp.Fori(1, B // 2) as p:
                for h in range(2):
                    sp.wait_ge(cs_ready, count(p, h, 2, -2))
                    sp.wait_ge(cTlo_ready, count(p, h, GROUPS, -GROUPS))
                    load_context(h, p * 2 + h)
            sp.wait_ge(oT_ready, B * TILES)
            for h in range(2):
                sp.dma_start(x1p[h * N:(h + 1) * N, :, :], x1[:, h::2, :]).then_inc(ld_late, 16)
            sp.dma_start(gam[:, :], ln_gamma.partition_broadcast(CAP)).then_inc(ld_late, 16)
            sp.dma_start(bet[:, :], ln_beta.partition_broadcast(CAP)).then_inc(ld_late, 16)
            sp.dma_start(b2r[:, :, :], b2s.unsqueeze(0)).then_inc(ld_late, 16)
            o = out.rearrange("b n c -> (b n) c").rearrange("(j t) c -> t j c", t=CAP)
            for g in range(2):
                sp.wait_ge(f_dve, OUT_READY[g])
                sp.dma_start(o[:, 4 * g:4 * g + 4, :], res[:, 4 * g:4 * g + 4, :]).then_inc(stored, 16)
            sp.wait_ge(stored, 32)

        @blk.gpsimd
        def _(pool):
            steps = [0]

            def made(ins):
                steps[0] += 1
                ins.then_inc(const_ready, 1)

            def follows():
                pool.wait_ge(const_ready, steps[0])

            made(pool.memset(ident[:, :], 0.0))
            made(pool.memset(headmask[:, :], 1.0))
            made(pool.memset(neghalf[:, :], -0.5))
            made(pool.memset(tri[:, :], 1.0))
            made(pool.memset(block[:, :], 1.0))
            made(pool.memset(ones16[:, :], 1.0))
            made(pool.memset(onesrow[:, :], 1.0))
            made(pool.iota(iota_i[:, :], pattern=[[1, CAP]], base=1, channel_multiplier=0))
            made(pool.iota(jcol_i[:, :], pattern=[[-REP, NE]], base=0, channel_multiplier=1))
            follows()
            made(pool.affine_select(out=ident[:, :], in_=ident[:, :], compare_op=ALU.not_equal, fill=1.0, base=0,
                                    pattern=[[-1, P]], channel_multiplier=1))
            made(pool.affine_select(out=headmask[:, :], in_=headmask[:, :], compare_op=ALU.is_ge, fill=0.0, base=0,
                                    pattern=[[-DH, H]], channel_multiplier=1))
            made(pool.affine_select(out=tri[:, :], in_=tri[:, :], compare_op=ALU.is_ge, fill=0.0, base=0,
                                    pattern=[[1, CAP]], channel_multiplier=-1))
            made(pool.affine_select(out=block[:, :], in_=block[:, :], compare_op=ALU.is_ge, fill=0.0, base=-1,
                                    pattern=[[-REP, NE], [0, REP]], channel_multiplier=1))
            made(pool.tensor_copy(iota1[:, :], iota_i[:, :]))
            made(pool.tensor_copy(jcol8[:, :], jcol_i[:, :]))
            follows()
            made(pool.affine_select(out=jcol8[:, :], in_=jcol8[:, :], compare_op=ALU.is_ge, fill=0.0, base=0,
                                    pattern=[[-REP, NE]], channel_multiplier=1))
            made(pool.tensor_copy(ident16[:, :], ident[:, :]))
            made(pool.affine_select(out=headmask[:, :], in_=headmask[:, :], compare_op=ALU.is_ge, fill=0.0, base=DH - 1,
                                    pattern=[[DH, H]], channel_multiplier=-1))
            made(pool.affine_select(out=block[:, :], in_=block[:, :], compare_op=ALU.is_ge, fill=0.0, base=REP - 1,
                                    pattern=[[REP, NE], [0, REP]], channel_multiplier=-1))
            follows()
            made(pool.affine_select(out=jcol8[:, :], in_=jcol8[:, :], compare_op=ALU.is_ge, fill=0.0, base=REP - 1,
                                    pattern=[[REP, NE]], channel_multiplier=-1))
            assert steps[0] == CONSTS, steps[0]

            def rstd(p, h, k):
                pool.wait_ge(aggr_done[k], count(p, h, 1, 1))
                pass_wait(pool)
                pool.tensor_scalar(ve[k][:, :], mv[k][:, 1:2], EPS, None, ALU.add).then_inc(eps_done[k], 1)
                pool.wait_ge(eps_done[k], count(p, h, 1, 1))
                pool.tensor_tensor(rs[k][:, :], ve[k][:, :], neghalf[0:N, 0:1], ALU.pow).then_inc(rstd_done[k], 1)

            def bc(ap, shape, axis):
                return ap.unsqueeze(axis).to_broadcast(shape)

            def mask_q(p, h):
                pool.wait_ge(qT_ready, count(p, h, 1, 1))
                pool.tensor_tensor(qblk[:, :, :], bc(qT[:, :], [C, H, N], 1), bc(headmask[:, :], [C, H, N], 2),
                                   ALU.mult).then_inc(qblk_ready, 1)

            def soften(p, h):
                pool.wait_ge(arec_scaled, count(p, h, 1, 1))
                pool.tensor_tensor(en[:, :, :], ep[:, :, :], bc(arec[:, :], [P, TILES, N], 2),
                                   ALU.mult).then_inc(en_ready, 1)

            def split_high(p, h):
                pool.wait_ge(ld_ctx[h], (p + 1) * 16)
                wait(pool, pv_done, count(p, h, TILES, -TILES))
                pass_wait(pool)
                pool.tensor_copy(cs[h][:, 0, :, :], cf[h][:, :, :]).then_inc(cs_ready, 1)

            def split_low(p, h):
                pool.wait_ge(cs_ready, count(p, h, 2, 1))
                pool.tensor_tensor(cs[h][:, 1, :, :], cf[h][:, :, :], cs[h][:, 0, :, :],
                                   ALU.subtract).then_inc(cs_ready, 1)

            def half(p, h, last=False):
                np_, nh = (p, 1) if h == 0 else (p + 1, 0)
                if not last:
                    rstd(p + 1, h, 0)
                split_high(np_, nh)
                rstd(np_, nh, 1)
                if not last:
                    mask_q(p + 1, h)
                split_low(np_, nh)
                if not last:
                    soften(p + 1, h)

            pool.wait_ge(const_ready, CONSTS)
            rstd(0, 0, 0)
            mask_q(0, 0)
            rstd(0, 1, 0)
            split_high(0, 0)
            soften(0, 0)
            split_low(0, 0)
            rstd(0, 0, 1)
            mask_q(0, 1)
            soften(0, 1)
            half(0, 0)
            half(0, 1)
            with pool.Fori(1, B // 2 - 1) as p:
                half(p, 0)
                half(p, 1)
            half(B // 2 - 1, 0, last=True)

            def f_rstd(n, after):
                pool.wait_ge(f_dve, after)
                pool.tensor_scalar(fve[:, :], fmv[:, :, 1], EPS, None, ALU.add).then_inc(f_pool, 1)
                pool.wait_ge(f_pool, n)
                pool.tensor_tensor(frs[:, :], fve[:, :], neghalf[0:CAP, :], ALU.pow).then_inc(f_pool, 1)

            f_rstd(1, AGGR3)
            f_rstd(3, AGGR4)
            pool.wait_ge(f_dve, NORM4)
            pool.wait_ge(ld_late, LD_LATE)
            pool.tensor_tensor(y1[:, :, :], y1[:, :, :], gam[:, :].unsqueeze(1).to_broadcast([CAP, TT, C]),
                               ALU.mult).then_inc(f_pool, 1)
            pool.wait_ge(f_pool, 5)
            pool.tensor_tensor(y1[:, :, :], y1[:, :, :], bet[:, :].unsqueeze(1).to_broadcast([CAP, TT, C]),
                               ALU.add).then_inc(f_pool, 1)
            pool.wait_ge(f_pool, 6)
            pool.tensor_copy(yhi[:, :, :], y1[:, :, :]).then_inc(f_pool, 1)
            pool.wait_ge(f_pool, 7)
            pool.tensor_tensor(ylo[:, :, :], y1[:, :, :], yhi[:, :, :], ALU.subtract).then_inc(f_pool, 1)

        @blk.tensor
        def _(pe):
            def prep(name, p, h):
                m = MISC[stage(name)[0]]
                wait_bank_read(pe, p, h, name)
                if name == "xT":
                    pe.wait_ge(norm_done[0], count(p, h, 1, 1))
                    pass_wait(pe)
                    ins = pe.transpose(m[:, 0:N], xn[0][:, :], ident[0:N, 0:N])
                elif name == "qkv":
                    pe.wait_ge(xT_ready, count(p, h, 1, 1))
                    pe.matmul(m[:, 0:N], wqkv[:, 0:C], xT[:, :], start=True, stop=True)
                    pe.matmul(m[:, N:2 * N], wqkv[:, C:2 * C], xT[:, :], start=True, stop=True)
                    ins = pe.matmul(m[0:N, P:2 * P], xT[:, :], wqkv[:, 2 * C:3 * C], start=True, stop=True)
                elif name == "S":
                    pe.wait_ge(qkv_ready, count(p, h, 1, 1))
                    pe.wait_ge(qblk_ready, count(p, h, 1, 1))
                    q = qblk[:, :, :].rearrange("c h n -> c (h n)")
                    for t in range(TILES):
                        ins = pe.matmul(m[:, t * N:(t + 1) * N], q[:, t * P:(t + 1) * P], kT[:, :],
                                        start=True, stop=True)
                elif name in ("PT0", "PT1"):
                    pe.wait_ge(en_ready, count(p, h, 1, 1))
                    pass_wait(pe)
                    first = 0 if name == "PT0" else 4
                    for t in range(first, min(first + 4, TILES)):
                        ins = pe.transpose(m[0:N, (t - first) * P:(t - first + 1) * P], en[:, t, :], ident[:, :])
                elif name == "PV":
                    pe.wait_ge(aT_ready, count(p, h, 2, 2))
                    pass_wait(pe)
                    for k in range(H):
                        ins = pe.matmul(m[0:N, k * DH:(k + 1) * DH], aT[:, k * N:(k + 1) * N],
                                        v[:, k * DH:(k + 1) * DH], start=True, stop=True)
                elif name == "aoT":
                    pe.wait_ge(ao_ready, count(p, h, 1, 1))
                    pass_wait(pe)
                    ins = pe.transpose(m[:, 0:N], ao[:, :], ident[0:N, 0:N])
                elif name == "y":
                    pe.wait_ge(aoT_ready, count(p, h, 1, 1))
                    pe.matmul(m[0:N, 0:C], aoT[:, :], wout[:, :], start=True, stop=False)
                    ins = pe.matmul(m[0:N, 0:C], onesrow[:, 0:N], bout[:, :], start=False, stop=True)
                elif name == "x1T":
                    pe.wait_ge(norm_done[1], count(p, h, 1, 1))
                    pass_wait(pe)
                    ins = pe.transpose(m[:, 0:N], xn[1][:, :], ident[0:N, 0:N])
                elif name in ("c0", "c1", "c2"):
                    k = int(name[1])
                    if k == 0:
                        pe.wait_ge(ld_ctx[h], (p + 1) * 16)
                    for j in range(GB):
                        ins = pe.transpose(m[0:E, j * KP:(j + 1) * KP], cf[h][:, GB * k + j, :], ident[0:KP, 0:KP])
                else:
                    pe.wait_ge(x1Tlo_ready, count(p, h, 1, 1))
                    first = 0 if name == "q0" else H // 2
                    for k in range(H // 2):
                        o = m[0:E, k * N:(k + 1) * N]
                        pe.matmul(o, Mhi[:, first + k, :], x1Thi[:, :], start=True, stop=False)
                        pe.matmul(o, Mhi[:, first + k, :], x1Tlo[:, :], start=False, stop=False)
                        ins = pe.matmul(o, Mlo[:, first + k, :], x1Thi[:, :], start=False, stop=True)
                ins.then_inc(misc_full[stage(name)[0]], 1)

            def scores(p, h, t, k):
                if t == 0 and k == 0:
                    pe.wait_ge(qlo_ready, count(p, h, 2, 2))
                if t == 0:
                    pe.wait_ge(cTlo_ready, count(p, h, GROUPS, k + 1))
                wait(pe, exp_done, count(p, h, 3 * TILES, 3 * t + k - 2))
                rows = slice(t * P, (t + 1) * P)
                hi, lo = cT[h][:, 0, k * GW:(k + 1) * GW], cT[h][:, 1, k * GW:(k + 1) * GW]
                o = SC[k][:, 0:GW]
                pe.matmul(o, qhi[h][:, rows], hi, start=True, stop=False)
                pe.matmul(o, qhi[h][:, rows], lo, start=False, stop=False)
                pe.matmul(o, qlo[h][:, rows], hi, start=False, stop=True).then_inc(sc_full, 1)

            def turn(p, h, t, k):
                pe.wait_ge(exp_done, count(p, h, 3 * TILES, 3 * t + k + 1))
                wait(pe, pTlo_ready, count(p, h, 3 * TILES, 3 * t + k - 1))
                src = prob[(h * TILES + t) % 2]
                for j in range(GB):
                    c = (GB * k + j) * KP
                    ins = pe.transpose(tp_bank(h, t, k)[0:KP, j * P:(j + 1) * P], src[:, c:c + KP], ident[:, :])
                ins.then_inc(tp_full, 1)

            def weigh(p, h, t, k):
                s = h if t >= 0 else 1 - h
                if t == 0 and k == 0:
                    pe.wait_ge(cs_ready, count(p, h, 2, 2))
                if k == 0:
                    wait(pe, oT_ready, count(p, h, TILES, t))
                pe.wait_ge(pTlo_ready, count(p, h, 3 * TILES, 3 * t + k + 1))
                o = ACC[:, 0:E]
                pt = parts(h, t, k)
                for j in range(GB):
                    hi, lo = cs[s][:, 0, GB * k + j, :], cs[s][:, 1, GB * k + j, :]
                    pe.matmul(o, pt[0][:, j, :], hi, start=(k == 0 and j == 0), stop=False)
                    pe.matmul(o, pt[0][:, j, :], lo, start=False, stop=False)
                    ins = pe.matmul(o, pt[1][:, j, :], hi, start=False, stop=(k == GROUPS - 1 and j == GB - 1))
                if k == GROUPS - 1:
                    ins.then_inc(pv_done, 1)

            def turn_out(p, h, t):
                pe.wait_ge(on_ready, count(p, h, TILES, t))
                pe.transpose(ACC[0:E, P:2 * P], on[:, :], ident[:, :]).then_inc(oT_full, 1)

            FIRST_STAGE = {(1, "c"): ["xT"], (2, "b"): ["qkv"], (3, "b"): ["S"], (5, "a"): ["PT0"], (5, "c"): ["PT1"],
                           (6, "b"): ["PV", "c0"]}
            SECOND_STAGE = {(0, "a"): ["aoT"], (0, "c"): ["c1", "y"], (2, "a"): ["x1T"], (2, "c"): ["c2"],
                            (3, "c"): ["q0"], (4, "c"): ["q1"]}

            def half(p, h, first=False, last=False, more_first=True):
                np_, nh = (p, 1) if h == 0 else (p + 1, 0)

                def prepare(t, place):
                    for name in FIRST_STAGE.get((t, place), []) if more_first else []:
                        prep(name, p + 1, h)
                    for name in SECOND_STAGE.get((t, place), []) if not last else []:
                        prep(name, np_, nh)

                for t in range(TILES):
                    nxt = (p, h, t + 1) if t < TILES - 1 else (np_, nh, 0)
                    before = not (first and t == 0)
                    more = not (last and t == TILES - 1)
                    if more:
                        scores(*nxt, 0)
                    if before:
                        turn(p, h, t - 1, 2)
                    if more:
                        scores(*nxt, 1)
                    turn(p, h, t, 0)
                    if not (first and t < 2):
                        turn_out(p, h, t - 1)
                    prepare(t, "a")
                    if more:
                        scores(*nxt, 2)
                    turn(p, h, t, 1)
                    if before:
                        weigh(p, h, t - 1, 0)
                    prepare(t, "b")
                    if before:
                        weigh(p, h, t - 1, 1)
                        weigh(p, h, t - 1, 2)
                    prepare(t, "c")

            def turn_weight(g):
                for a in range(4):
                    if g < 2:
                        c = (4 * g + a) * P
                        ins = pe.transpose(bank[g][:, a * P:(a + 1) * P], wq[:, c:c + P], ident[:, :])
                    else:
                        c = (4 * (g - 2) + a) * P
                        ins = pe.transpose(bank[g][:, a * P:a * P + E], wkv[:, c:c + P], ident[0:E, 0:E])
                ins.then_inc(wT_full, 1)

            def make_m(g):
                if g == 0:
                    pe.wait_ge(wT_ready, 4)
                for k in range(4):
                    a, q = 4 * (g // 2) + k, g % 2
                    ins = pe.matmul(bank[M_BANK[g]][:, k * P:k * P + E], wqT[q * DK:(q + 1) * DK, a, :],
                                    wkT[q * DK:(q + 1) * DK, a, :], start=True, stop=True)
                ins.then_inc(mu_full, 1)

            def make_u(g):
                if g == 0:
                    pe.wait_ge(wT_ready, 6)
                    pe.wait_ge(ld_wproj, 16)
                if g >= 2:
                    pe.wait_ge(mu_ready, g - 1)
                    pe.wait_ge(mlo_ready, g - 1)
                for k in range(4):
                    a, q = 4 * (g // 2) + k, g % 2
                    ins = pe.matmul(bank[U_BANK[g]][0:E, k * P:(k + 1) * P], wvT[q * DK:(q + 1) * DK, a, :],
                                    wproj[q * DK:(q + 1) * DK, a, :], start=True, stop=True)
                ins.then_inc(mu_full, 1)

            pe.wait_ge(const_ready, CONSTS)
            pe.wait_ge(ld_wq, 16)
            turn_weight(0)
            turn_weight(1)
            prep("xT", 0, 0)
            pe.wait_ge(ld_wkv, 16)
            turn_weight(2)
            turn_weight(3)
            pe.wait_ge(ld_qkv, 16)
            prep("qkv", 0, 0)
            turn_weight(4)
            turn_weight(5)
            make_m(0)
            prep("S", 0, 0)
            make_m(1)
            make_m(2)
            prep("PT0", 0, 0)
            make_m(3)
            prep("PT1", 0, 0)
            make_u(0)
            prep("PV", 0, 0)
            prep("c0", 0, 0)
            make_u(1)
            prep("aoT", 0, 0)
            prep("c1", 0, 0)
            pe.wait_ge(ld_small, LD_SMALL)
            prep("y", 0, 0)
            prep("xT", 0, 1)
            make_u(2)
            prep("x1T", 0, 0)
            prep("qkv", 0, 1)
            prep("c2", 0, 0)
            make_u(3)
            prep("S", 0, 1)
            pe.wait_ge(mlo_ready, 4)
            prep("q0", 0, 0)
            prep("PT0", 0, 1)
            prep("q1", 0, 0)
            prep("PT1", 0, 1)
            prep("PV", 0, 1)
            prep("c0", 0, 1)
            pe.wait_ge(mu_ready, 8)
            for k in range(GROUPS):
                scores(0, 0, 0, k)
            half(0, 0, first=True)
            half(0, 1)
            with pe.Fori(1, B // 2 - 1) as p:
                half(p, 0)
                half(p, 1)
            half(B // 2 - 1, 0, more_first=False)
            half(B // 2 - 1, 1, last=True, more_first=False)
            turn(B // 2, 0, -1, 2)
            turn_out(B // 2, 0, -1)
            for k in range(GROUPS):
                weigh(B // 2, 0, -1, k)
            turn_out(B // 2, 0, 0)

            def done(ins):
                ins.then_inc(f_pe, 1)

            pe.wait_ge(oT_ready, B * TILES)
            for g in range(2):
                for k in range(H):
                    ins = pe.matmul(bank[g][:, 0:HALF], U[:, k, :],
                                    oT[:, g * B // 2:(g + 1) * B // 2, k * N:(k + 1) * N],
                                    start=(k == 0), stop=(k == H - 1))
                done(ins)
            for g in range(2):
                pe.wait_ge(f_dve, 1 + g)
                for a in range(4):
                    j = 4 * g + a
                    ins = pe.transpose(bank[2 + g][0:CAP, a * P:(a + 1) * P], yT[:, j * CAP:(j + 1) * CAP],
                                       ident[:, :])
                done(ins)
            pe.wait_ge(ld_small, LD_SMALL)
            pe.transpose(bank[6][:, 0:NE], gate[:, :], ident[0:NE, 0:NE])
            ins = pe.transpose(bank[6][:, P:P + NE * FC], b1r[:, :], ident[0:NE * FC, 0:NE * FC])
            done(ins)
            pe.wait_ge(f_dve, NORM3)
            for g in range(2):
                for a in range(4):
                    j = 4 * g + a
                    ins = pe.transpose(bank[4 + g][:, a * CAP:(a + 1) * CAP], xf[:, j, :], ident[0:CAP, 0:CAP])
                done(ins)
            pe.wait_ge(f_dve, GATE_T)
            for g in range(2):
                pe.wait_ge(f_act, 1 + g)
                ins = pe.matmul(bank[6 + g][:, 0:HALF], gateT[:, :, :].rearrange("c e r -> c (e r)"),
                                xfT[:, g * HALF:(g + 1) * HALF], start=True, stop=True)
                done(ins)
            pe.wait_ge(ld_ffn, LD_FFN)
            def turn_weights(g):
                if g >= 2:
                    pe.wait_ge(f_act, WT0 + g - 1)
                for a in range(4):
                    if g < NE:
                        src = fc1[:, 4 * g + a, :]
                    else:
                        src = fc2[:, g - NE, a * P:(a + 1) * P]
                    ins = pe.transpose(bank[1 + g % 2][:, a * P:(a + 1) * P], src, ident[:, :])
                done(ins)

            assert 9 == PE_BEFORE_SEARCH
            g = 0
            for r in range(ROUNDS):
                pe.wait_ge(f_dve, FLAG[r])
                done(pe.matmul(bank[0][:, 0:1], block[:, :], flag[:, :], start=True, stop=True))
                for _ in range(SEARCH_GROUPS[r]):
                    turn_weights(g)
                    g += 1
            assert g == 2 * NE
            pe.wait_ge(f_dve, VALS)
            for g in range(2):
                for a in range(4):
                    j = 4 * g + a
                    ins = pe.transpose(bank[3 + g][0:CAP, a * P:(a + 1) * P], vals[:, j * CAP:(j + 1) * CAP],
                                       ident[:, :])
                done(ins)
            for g, (m, after) in enumerate(((mge, MGE), (mgt, MGT))):
                pe.wait_ge(f_dve, after)
                m16 = bank[5 + g][:, :].bitcast(F16).rearrange("p (j k) -> p j k", k=P)
                for j in range(TT):
                    ins = pe.transpose(m16[0:CAP, j, :], m[:, j * CAP:(j + 1) * CAP], ident16[:, :])
                done(ins)
            pe.wait_ge(f_dve, SEL)
            cum = bank[7][0:CAP, 0:2 * TT * NE].rearrange("p (k j e) -> p k j e", k=2, e=NE)
            pe.matmul(cum, tri[:, :], sel[:, :, :, :], start=True, stop=False, skip_group_check=True)
            for s in range(1, TT):
                ins = pe.matmul(cum[:, :, s:TT, :], ones16[:, :], sel[:, :, 0:TT - s, :], start=False,
                                stop=(s == TT - 1), skip_group_check=True)
            done(ins)
            for j in range(TT):
                ins = pe.matmul(bank[0][0:CAP, 0:NE], ones16[:, :], sel[:, 0, j, :], start=(j == 0),
                                stop=(j == TT - 1))
            done(ins)
            pe.wait_ge(f_pool, 8)
            pe.wait_ge(f_dve, V2)
            pe.wait_ge(f_act, GT0)
            for j in range(TT):
                pe.wait_ge(f_dve, G0 + j)
                gj = G[:, j, :, :].rearrange("p e s -> p (e s)")
                for g in range(2):
                    for part, w in enumerate((yhi, ylo)):
                        pe.matmul(bank[3 + g][:, 0:HALF], w[:, j, :], gj[:, g * HALF:(g + 1) * HALF],
                                  start=(j == 0 and part == 0), stop=(j == TT - 1 and part == 1))
                for e in range(NE):
                    ins = pe.matmul(bank[0][0:CAP, P + 2 * e:P + 2 * e + 2], G[:, j, e, :], v2[:, j, e, :],
                                    start=(j == 0 and e == 0), stop=(j == TT - 1), skip_group_check=True)
                if j >= 2:
                    pe.wait_ge(f_act, GT0 + j - 1)
                m16 = bank[1 + j % 2][:, :].bitcast(F16).rearrange("p (e k) -> p e k", k=P)
                for e in range(NE):
                    ins = pe.transpose(m16[0:CAP, e, 0:CAP], G[:, j, e, :], ident16[0:CAP, 0:CAP])
                done(ins)
            def hidden(e):
                if e == 0:
                    pe.wait_ge(f_dve, YG)
                if e >= 2:
                    pe.wait_ge(f_dve, HB[e - 2])
                for a in range(FC):
                    ins = pe.matmul(bank[5 + e % 2][:, a * CAP:(a + 1) * CAP], fc1T[:, FC * e + a, :],
                                    ygT[:, e, :], start=True, stop=True)
                done(ins)

            def down(e):
                pe.wait_ge(f_act, GELU0 + e)
                if e >= 1:
                    pe.wait_ge(f_dve, OLO[e - 1])
                o = bank[7][0:CAP, 0:C]
                for a in range(FC):
                    pe.matmul(o, hg[e % 2][:, a, :], fc2T[:, FC * e + a, :], start=(a == 0), stop=False)
                done(pe.matmul(o, onesrow[:, :], b2r[:, e, :], start=False, stop=True))

            def scatter(e):
                pe.wait_ge(f_dve, OLO[e])
                if e == 0:
                    pe.wait_ge(f_act, GT0 + TT)
                for j in range(TT):
                    for part, w in enumerate((ohi, olo)):
                        ins = pe.matmul(bank[1 + j // 4][0:CAP, (j % 4) * C:(j % 4 + 1) * C], GT[:, e, j, :],
                                        w[e % 2][:, :], start=(e == 0 and j % 4 == 0 and part == 0),
                                        stop=(e == NE - 1 and part == 1), skip_group_check=True)
                done(ins)

            pe.wait_ge(ld_late, LD_LATE)
            hidden(0)
            for e in range(NE):
                if e + 1 < NE:
                    hidden(e + 1)
                down(e)
                if e >= 1:
                    scatter(e - 1)
            scatter(NE - 1)

        @blk.scalar
        def _(act):
            for a, b, s in ((bq[:, :], b_qkv[0:C].rearrange("(c a) -> c a", a=1), ld_bias),
                            (bk[:, :], b_qkv[C:2 * C].rearrange("(c a) -> c a", a=1), ld_bias),
                            (bv[:, :], b_qkv[2 * C:3 * C].partition_broadcast(N), ld_bias),
                            (wout[:, :], W_out, ld_small),
                            (bout[:, :], b_out.unsqueeze(0), ld_small),
                            (bpr[:, :], bproj.rearrange("(c a) -> c a", a=1), ld_small),
                            (gate[:, :], gate_w, ld_small),
                            (b1r[:, :], b1s.rearrange("e (f p) -> (e f) p", p=P), ld_small)):
                act.dma_start(a, b).then_inc(s, 16)
            act.preload_act_table(ACT.Exp)

            def copy(o, i):
                return act.activation(o, i, ACT.Copy)

            def turn_weight(g):
                act.wait_ge(wT_full, g + 1)
                b = bank[g][:, :].rearrange("p (a k) -> p a k", k=P)
                if g < 2:
                    copy(wqT[:, 4 * g:4 * g + 4, :], b).then_inc(wT_ready, 1)
                else:
                    w = wkT if g < 4 else wvT
                    copy(w[:, 4 * (g % 2):4 * (g % 2) + 4, :], b[:, :, 0:E]).then_inc(wT_ready, 1)

            def heads(g):
                return slice(8 * (g // 2) + g % 2, 8 * (g // 2) + 8, 2)

            def make_m(g):
                act.wait_ge(mu_full, g + 1)
                act.activation(Mhi[:, heads(g), :], bank[M_BANK[g]][:, :].rearrange("p (a k) -> p a k", k=P)[:, :, 0:E],
                               ACT.Copy, scale=SCALE).then_inc(mu_ready, 1)

            def make_u(g):
                act.wait_ge(mu_full, g + 5)
                copy(U[:, heads(g), :], bank[U_BANK[g]][0:E, :].rearrange("p (a k) -> p a k", k=P)).then_inc(mu_ready, 1)

            def prep(name, p, h):
                if name == "exp":
                    act.wait_ge(es_ready, count(p, h, 1, 1))
                    act.activation(ep[:, :, :], es[:, :, :], ACT.Exp).then_inc(ep_ready, 1)
                    return
                m = MISC[stage(name)[0]]
                wait_full(act, p, h, name)
                if name == "xT":
                    copy(xT[:, :], m[:, 0:N]).then_inc(xT_ready, 1)
                elif name == "x1T":
                    copy(x1Thi[:, :], m[:, 0:N]).then_inc(x1Thi_ready, 1)
                elif name in ("c0", "c1", "c2"):
                    k = int(name[1])
                    copy(cT[h][:, 0, k * GW:(k + 1) * GW], m[0:E, 0:GW]).then_inc(cThi_ready, 1)
                elif name == "PT0":
                    copy(aT[:, 0:4 * P], m[0:N, :]).then_inc(aT_ready, 1)
                elif name == "PT1":
                    copy(aT[:, 4 * P:ROWS], m[0:N, 0:ROWS - 4 * P]).then_inc(aT_ready, 1)
                elif name == "PV":
                    copy(ao[:, :], m[0:N, 0:C]).then_inc(ao_ready, 1)
                elif name == "aoT":
                    copy(aoT[:, :], m[:, 0:N]).then_inc(aoT_ready, 1)
                else:
                    c = HALF * (name == "q1")
                    copy(qhi[h][:, c:c + HALF], m[0:E, 0:HALF]).then_inc(qhi_ready, 1)

            def expo(p, h, t):
                act.wait_ge(nmax_ready, count(p, h, TILES, t + 1))
                i = (h * TILES + t) % 2
                for k in range(GROUPS):
                    act.activation(prob[i][:, k * GW:(k + 1) * GW], SC[k][:, 0:GW], ACT.Exp, bias=nmax[:, 0:1],
                                   accum_out=sum3[i][:, k:k + 1]).then_inc(exp_done, 1)

            def take(p, h, t, k):
                act.wait_ge(tp_full, count(p, h, 3 * TILES, 3 * t + k + 1))
                copy(parts(h, t, k)[0][:, :, :].rearrange("p j k -> p (j k)"), tp_bank(h, t, k)[0:KP, :]).then_inc(pThi_ready, 1)

            def take_out(p, h, t, b):
                act.wait_ge(oT_full, count(p, h, TILES, t))
                copy(oT[:, b, ((t - 1) % TILES) * P:((t - 1) % TILES + 1) * P], ACC[0:E, P:2 * P]).then_inc(oT_ready, 1)

            FIRST_STAGE = {(2, "a"): ["xT"], (3, "c"): ["exp"], (5, "b"): ["PT0"], (6, "a"): ["PT1"],
                           (6, "c"): ["PV", "c0"]}
            SECOND_STAGE = {(0, "b"): ["aoT"], (1, "a"): ["c1"], (2, "b"): ["x1T"], (3, "a"): ["c2"], (4, "a"): ["q0"],
                            (5, "a"): ["q1"]}

            def half(p, h, first=False, last=False, more_first=True):
                np_, nh = (p, 1) if h == 0 else (p + 1, 0)

                def prepare(t, place):
                    for name in FIRST_STAGE.get((t, place), []) if more_first else []:
                        prep(name, p + 1, h)
                    for name in SECOND_STAGE.get((t, place), []) if not last else []:
                        prep(name, np_, nh)

                for t in range(TILES):
                    nxt = (p, h, t + 1) if t < TILES - 1 else (np_, nh, 0)
                    if not (first and t == 0):
                        take(p, h, t - 1, 2)
                    take(p, h, t, 0)
                    if not (first and t < 2):
                        take_out(p, h, t - 1, batch(p, h) - (t < 2))
                    prepare(t, "a")
                    take(p, h, t, 1)
                    prepare(t, "b")
                    if not (last and t == TILES - 1):
                        expo(*nxt)
                    prepare(t, "c")

            turn_weight(0)
            turn_weight(1)
            prep("xT", 0, 0)
            for g in range(2, 6):
                turn_weight(g)
            make_m(0)
            prep("exp", 0, 0)
            make_m(1)
            make_m(2)
            prep("PT0", 0, 0)
            make_m(3)
            prep("PT1", 0, 0)
            make_u(0)
            prep("PV", 0, 0)
            prep("c0", 0, 0)
            make_u(1)
            prep("aoT", 0, 0)
            prep("c1", 0, 0)
            prep("xT", 0, 1)
            make_u(2)
            prep("x1T", 0, 0)
            prep("c2", 0, 0)
            make_u(3)
            prep("exp", 0, 1)
            prep("q0", 0, 0)
            prep("PT0", 0, 1)
            prep("q1", 0, 0)
            prep("PT1", 0, 1)
            prep("PV", 0, 1)
            prep("c0", 0, 1)
            expo(0, 0, 0)
            half(0, 0, first=True)
            half(0, 1)
            with act.Fori(1, B // 2 - 1) as p:
                half(p, 0)
                half(p, 1)
            half(B // 2 - 1, 0, more_first=False)
            half(B // 2 - 1, 1, last=True, more_first=False)
            take(B // 2, 0, -1, 2)
            take_out(B // 2, 0, -1, B - 1)
            take_out(B // 2, 0, 0, B - 1)

            def done(ins):
                ins.then_inc(f_act, 1)

            for g in range(2):
                act.wait_ge(f_pe, 6 + g)
                done(copy(xfT[:, g * HALF:(g + 1) * HALF], bank[4 + g][:, 0:HALF]))
            for g in range(2):
                act.wait_ge(f_pe, 8 + g)
                done(act.activation(th[:, g * HALF:(g + 1) * HALF], bank[6 + g][:, 0:HALF], ACT.Tanh))
            g = 0
            for r in range(ROUNDS):
                for _ in range(SEARCH_GROUPS[r]):
                    act.wait_ge(f_pe, PE_BEFORE_SEARCH + (r + 1) + g + 1)
                    w = fc1T if g < NE else fc2T
                    a = 4 * (g % NE)
                    done(copy(w[:, a:a + 4, :].rearrange("p a k -> p (a k)"), bank[1 + g % 2][:, :]))
                    g += 1
            for j in range(TT):
                act.wait_ge(f_pe, G_FULL + j)
                m16 = bank[1 + j % 2][:, :].bitcast(F16).rearrange("p (e k) -> p e k", k=P)
                done(copy(GT[:, :, j, :], m16[0:CAP, :, 0:CAP]))
            for e in range(NE):
                act.wait_ge(f_dve, HB[e])
                if e >= 2:
                    act.wait_ge(f_pe, DOWN[e - 2])
                done(act.activation(hg[e % 2][:, :, :], hb[e % 2][:, :, :], ACT.Gelu_apprx_tanh))

        @blk.vector
        def _(dve):
            def bc(ap, shape, axis):
                return ap.unsqueeze(axis).to_broadcast(shape)

            def stats(src, p, h, k):
                wait(dve, norm_done[k], count(p, h, 1, 0))
                pass_wait(dve)
                dve.bn_stats(st[k][:, :], src).then_inc(stats_done[k], 1)
                dve.wait_ge(stats_done[k], count(p, h, 1, 1))
                wait(dve, rstd_done[k], count(p, h, 1, 0))
                pass_wait(dve)
                dve.bn_aggr(mv[k][:, :], st[k][:, :]).then_inc(aggr_done[k], 1)

            def norm(src, p, h, k):
                dve.wait_ge(rstd_done[k], count(p, h, 1, 1))
                dve.tensor_scalar(xn[k][:, :], src, mv[k][:, 0:1], rs[k][:, 0:1], ALU.subtract,
                                  ALU.mult).then_inc(norm_done[k], 1)

            def prep(name, p, h):
                b = batch(p, h)
                k, _ = stage(name)
                if k is not None:
                    m = MISC[k]
                    wait_full(dve, p, h, name)
                if name == "stats1":
                    stats(xin[:, b, :], p, h, 0)
                elif name == "norm1":
                    norm(xin[:, b, :], p, h, 0)
                elif name == "qkv":
                    dve.tensor_scalar(qT[:, :], m[:, 0:N], bq[:, 0:1], None, ALU.add).then_inc(qT_ready, 1)
                    dve.tensor_scalar(kT[:, :], m[:, N:2 * N], bk[:, 0:1], None, ALU.add)
                    dve.tensor_tensor(v[:, :], m[0:N, P:2 * P], bv[:, :], ALU.add).then_inc(qkv_ready, 1)
                elif name == "S":
                    s = m[:, 0:TILES * N].rearrange("p (t n) -> p t n", n=N)
                    dve.tensor_reduce(amax[:, :], s, X, ALU.max, negate=True).then_inc(amax_ready, 1)
                    dve.wait_ge(amax_ready, count(p, h, 1, 1))
                    dve.tensor_tensor(es[:, :, :], s, bc(amax[:, :], [P, TILES, N], 2), ALU.add).then_inc(es_ready, 1)
                elif name == "soft":
                    dve.wait_ge(ep_ready, count(p, h, 1, 1))
                    dve.tensor_reduce(asum[:, :], ep[:, :, :], X, ALU.add).then_inc(asum_ready, 1)
                    dve.wait_ge(asum_ready, count(p, h, 1, 1))
                    dve.reciprocal(arec[:, :], asum[:, :]).then_inc(arec_ready, 1)
                    dve.wait_ge(arec_ready, count(p, h, 1, 1))
                    dve.tensor_scalar(arec[:, :], arec[:, :], ATT, None, ALU.mult).then_inc(arec_scaled, 1)
                elif name == "y":
                    dve.tensor_tensor(x1[:, b, :], m[0:N, 0:C], xin[:, b, :], ALU.add).then_inc(x1_ready, 1)
                    dve.wait_ge(x1_ready, count(p, h, 1, 1))
                    stats(x1[:, b, :], p, h, 1)
                elif name == "norm2":
                    norm(x1[:, b, :], p, h, 1)
                elif name in ("q0", "q1"):
                    k = int(name == "q1")
                    dve.wait_ge(qhi_ready, count(p, h, 2, k + 1))
                    cols = slice(k * HALF, (k + 1) * HALF)
                    dve.tensor_tensor(qlo[h][:, cols], m[0:E, 0:HALF], qhi[h][:, cols],
                                      ALU.subtract).then_inc(qlo_ready, 1)
                elif name in ("c0", "c1", "c2"):
                    k = int(name[1])
                    dve.wait_ge(cThi_ready, count(p, h, GROUPS, k + 1))
                    dve.tensor_tensor(cT[h][:, 1, k * GW:(k + 1) * GW], m[0:E, 0:GW],
                                      cT[h][:, 0, k * GW:(k + 1) * GW], ALU.subtract).then_inc(cTlo_ready, 1)
                elif name == "x1T":
                    dve.wait_ge(x1Thi_ready, count(p, h, 1, 1))
                    dve.tensor_tensor(x1Tlo[:, :], m[:, 0:N], x1Thi[:, :], ALU.subtract).then_inc(x1Tlo_ready, 1)

            def maximum(p, h, t, k):
                dve.wait_ge(sc_full, count(p, h, 3 * TILES, 3 * t + k + 1))
                if k == 0:
                    wait(dve, nmax_ready, count(p, h, TILES, t))
                dve.tensor_reduce(mx3[:, k:k + 1], SC[k][:, 0:GW], X, ALU.max).then_inc(mx_done, 1)

            def maxima(p, h, t):
                dve.wait_ge(mx_done, count(p, h, 3 * TILES, 3 * t + 3))
                wait(dve, exp_done, count(p, h, 3 * TILES, 3 * t))
                dve.tensor_reduce(nmax[:, :], mx3[:, :], X, ALU.max, negate=True).then_inc(nmax_ready, 1)

            def take(p, h, t, k):
                dve.wait_ge(pThi_ready, count(p, h, 3 * TILES, 3 * t + k + 1))
                hi, lo = parts(h, t, k)
                dve.tensor_tensor(lo[:, :, :].rearrange("p j k -> p (j k)"), tp_bank(h, t, k)[0:KP, :],
                                  hi[:, :, :].rearrange("p j k -> p (j k)"),
                                  ALU.subtract).then_inc(pTlo_ready, 1)

            def denominators(p, h, t):
                dve.wait_ge(exp_done, count(p, h, 3 * TILES, 3 * t))
                wait(dve, rden_ready, count(p, h, TILES, t - 1))
                dve.tensor_reduce(den[:, :], sum3[(h * TILES + t - 1) % 2][:, :], X, ALU.add).then_inc(den_ready, 1)

            def invert(p, h, t):
                dve.wait_ge(den_ready, count(p, h, TILES, t))
                wait(dve, on_ready, count(p, h, TILES, t - 1))
                dve.reciprocal(rden[:, :], den[:, :]).then_inc(rden_ready, 1)

            def normalise(p, h, t):
                dve.wait_ge(rden_ready, count(p, h, TILES, t))
                dve.wait_ge(pv_done, count(p, h, TILES, t))
                wait(dve, oT_full, count(p, h, TILES, t - 1))
                dve.tensor_scalar(on[:, :], ACC[:, 0:E], rden[:, 0:1], None,
                                  ALU.mult).then_inc(on_ready, 1)

            FIRST_STAGE = {(0, "a"): ["stats1"], (0, "c"): ["norm1"], (2, "b"): ["qkv"], (3, "c"): ["S"], (4, "a"): ["soft"]}
            SECOND_STAGE = {(0, "a"): ["c0"], (1, "a"): ["y", "c1"], (1, "c"): ["norm2"], (2, "b"): ["x1T"],
                            (3, "a"): ["c2"], (4, "a"): ["q0"], (5, "a"): ["q1"]}

            def half(p, h, first=False, last=False, more_first=True):
                np_, nh = (p, 1) if h == 0 else (p + 1, 0)

                def prepare(t, place):
                    for name in FIRST_STAGE.get((t, place), []) if more_first else []:
                        prep(name, p + 1, h)
                    for name in SECOND_STAGE.get((t, place), []) if not last else []:
                        prep(name, np_, nh)

                for t in range(TILES):
                    nxt = (p, h, t + 1) if t < TILES - 1 else (np_, nh, 0)
                    before = not (first and t == 0)
                    more = not (last and t == TILES - 1)
                    if more:
                        maximum(*nxt, 0)
                    if not (first and t < 2):
                        normalise(p, h, t - 1)
                    if before:
                        denominators(p, h, t)
                    if before:
                        take(p, h, t - 1, 2)
                    if more:
                        maximum(*nxt, 1)
                    if before:
                        invert(p, h, t)
                    if more:
                        maximum(*nxt, 2)
                        maxima(*nxt)
                    prepare(t, "a")
                    take(p, h, t, 0)
                    prepare(t, "b")
                    take(p, h, t, 1)
                    prepare(t, "c")

            dve.wait_ge(const_ready, CONSTS)
            dve.wait_ge(ld_x, 16)
            prep("stats1", 0, 0)
            prep("norm1", 0, 0)
            dve.wait_ge(ld_bias, 48)

            def make_m(g):
                dve.wait_ge(mu_ready, g + 1)
                heads = slice(8 * (g // 2) + g % 2, 8 * (g // 2) + 8, 2)
                dve.scalar_tensor_tensor(Mlo[:, heads, :],
                                         bank[M_BANK[g]][:, :].rearrange("p (a k) -> p a k", k=P)[:, :, 0:E],
                                         SCALE, Mhi[:, heads, :], ALU.mult, ALU.subtract).then_inc(mlo_ready, 1)

            prep("qkv", 0, 0)
            prep("stats1", 0, 1)
            prep("norm1", 0, 1)
            make_m(0)
            prep("S", 0, 0)
            make_m(1)
            make_m(2)
            prep("soft", 0, 0)
            make_m(3)
            prep("c0", 0, 0)
            prep("c1", 0, 0)
            prep("y", 0, 0)
            prep("norm2", 0, 0)
            prep("qkv", 0, 1)
            prep("x1T", 0, 0)
            prep("c2", 0, 0)
            prep("S", 0, 1)
            prep("soft", 0, 1)
            prep("q0", 0, 0)
            prep("q1", 0, 0)
            for k in range(GROUPS):
                maximum(0, 0, 0, k)
            maxima(0, 0, 0)
            half(0, 0, first=True)
            half(0, 1)
            with dve.Fori(1, B // 2 - 1) as p:
                half(p, 0)
                half(p, 1)
            half(B // 2 - 1, 0, more_first=False)
            half(B // 2 - 1, 1, last=True, more_first=False)
            normalise(B // 2, 0, -1)
            take(B // 2, 0, -1, 2)
            denominators(B // 2, 0, 0)
            invert(B // 2, 0, 0)
            normalise(B // 2, 0, 0)

            n = [0]

            def done(ins, at=None):
                n[0] += 1
                ins.then_inc(f_dve, 1)
                assert at is None or at == n[0], (at, n[0])

            def settle():
                dve.wait_ge(f_dve, n[0])

            for g in range(2):
                dve.wait_ge(f_pe, 1 + g)
                done(dve.tensor_scalar(yT[:, g * HALF:(g + 1) * HALF], bank[g][:, 0:HALF], bpr[:, 0:1], None, ALU.add))
            dve.wait_ge(ld_late, LD_LATE)
            for g in range(2):
                dve.wait_ge(f_pe, 3 + g)
                done(dve.tensor_tensor(x2[:, 4 * g:4 * g + 4, :],
                                       bank[2 + g][0:CAP, :].rearrange("p (a k) -> p a k", k=P),
                                       x1p[:, 4 * g:4 * g + 4, :], ALU.add))

            def f_stats(src, at):
                settle()
                for j in range(TT):
                    done(dve.bn_stats(fst[:, j, :], src[:, j, :]))
                settle()
                for j in range(TT):
                    done(dve.bn_aggr(fmv[:, j, :], fst[:, j, :]), at if j == TT - 1 else None)

            def f_norm(dst, src, pool_steps, at):
                dve.wait_ge(f_pool, pool_steps)
                settle()
                for j in range(TT):
                    done(dve.tensor_scalar(dst[:, j, :], src[:, j, :], fmv[:, j, 0:1], frs[:, j:j + 1],
                                           ALU.subtract, ALU.mult), at if j == TT - 1 else None)

            f_stats(x2, AGGR3)
            f_norm(xf, x2, 2, NORM3)
            dve.wait_ge(f_pe, 5)
            done(dve.tensor_copy(gateT[:, :, :], bc(bank[6][:, 0:NE], [C, NE, REP], 2)))
            done(dve.tensor_copy(b1T[:, :, :], bank[6][:, P:P + NE * FC].rearrange("p (e f) -> p e f", f=FC)), GATE_T)
            f_stats(xf, AGGR4)
            f_norm(y1, xf, 4, NORM4)
            done(dve.tensor_tensor(base[:, :, :], x2[:, :, :], xf[:, :, :], ALU.add))
            done(dve.tensor_reduce(jcol[:, :], jcol8[:, :], X, ALU.add))
            done(dve.memset(low[:, :], 0.0))
            for g in range(2):
                dve.wait_ge(f_act, 3 + g)
                done(dve.tensor_scalar(vals[:, g * HALF:(g + 1) * HALF], th[:, g * HALF:(g + 1) * HALF], 1.0, 0.5,
                                       ALU.add, ALU.mult), VALS if g else None)
            for r in range(ROUNDS):
                step = 2.0 ** -(3 + 4 * r)
                settle()
                done(dve.tensor_scalar(thr[:, :], jcol[:, :], step, low[:, 0:1], ALU.mult, ALU.add))
                settle()
                done(dve.tensor_scalar(junk[:, :], vals[:, :], thr[:, 0:1], None, ALU.is_ge, ALU.add,
                                       accum_out=cnt[:, :]))
                settle()
                done(dve.tensor_scalar(flag[:, :], cnt[:, :], float(CAP), None, ALU.is_ge), FLAG[r])
                dve.wait_ge(f_pe, SEARCH[r])
                done(dve.tensor_scalar(low[:, :], bank[0][:, 0:1], step, low[:, 0:1], ALU.mult, ALU.add))
            settle()
            done(dve.tensor_scalar(mge[:, :], vals[:, :], low[:, 0:1], None, ALU.is_ge), MGE)
            done(dve.tensor_scalar(mgt[:, :], vals[:, :], low[:, 0:1], None, ALU.is_gt), MGT)
            for g in range(2):
                dve.wait_ge(f_pe, VN_FULL + g)
                done(dve.tensor_copy(vn[:, 4 * g:4 * g + 4, :],
                                     bank[3 + g][0:CAP, :].rearrange("p (a e r) -> p a e r", a=4, r=REP)[:, :, :, 0]))
            settle()
            done(dve.tensor_copy(v2[:, :, :, 0], vn[:, :, :]))
            settle()
            done(dve.tensor_tensor(v2[:, :, :, 1], vn[:, :, :], v2[:, :, :, 0], ALU.subtract), V2)
            mask = [bank[5 + g][0:CAP, :].bitcast(F16).rearrange("p (j e r) -> p j e r", e=NE, r=REP)[:, :, :, 0]
                    for g in range(2)]
            dve.wait_ge(f_pe, MASK_FULL)
            done(dve.tensor_copy(ge[:, :, :], mask[0]))
            dve.wait_ge(f_pe, MASK_FULL + 1)
            done(dve.tensor_copy(sel[:, 0, :, :], mask[1]))
            settle()
            done(dve.tensor_tensor(sel[:, 1, :, :], ge[:, :, :], sel[:, 0, :, :], ALU.subtract), SEL)
            cum = bank[7][0:CAP, 0:2 * TT * NE].rearrange("p (k j e) -> p k j e", k=2, e=NE)
            dve.wait_ge(f_pe, TOT_FULL)
            done(dve.tensor_copy(cg[:, :], bank[0][0:CAP, 0:NE]))
            settle()
            done(dve.tensor_tensor(pa[:, :, :], cum[:, 1, :, :], bc(cg[:, :], [CAP, TT, NE], 1), ALU.add))
            done(dve.tensor_tensor(pb[:, :, :], cum[:, 0, :, :], sel[:, 0, :, :], ALU.mult))
            settle()
            done(dve.tensor_tensor(pa[:, :, :], pa[:, :, :], sel[:, 1, :, :], ALU.mult))
            settle()
            done(dve.tensor_tensor(pa[:, :, :], pa[:, :, :], pb[:, :, :], ALU.add))
            settle()
            done(dve.tensor_scalar(pb[:, :, :], ge[:, :, :], -2.0 * T, 2.0 * T, ALU.mult, ALU.add))
            settle()
            done(dve.tensor_tensor(slot[:, :, :], pa[:, :, :], pb[:, :, :], ALU.add))
            settle()
            for j in range(TT):
                done(dve.tensor_tensor(G[:, j, :, :], bc(iota1[:, :], [CAP, NE, CAP], 1),
                                       bc(slot[:, j, :], [CAP, NE, CAP], 2), ALU.is_equal), G0 + j)
            dve.wait_ge(f_pe, G_FULL + TT - 1)
            for g in range(2):
                done(dve.tensor_copy(ygT[:, 4 * g:4 * g + 4, :],
                                     bank[3 + g][:, 0:HALF].rearrange("p (e s) -> p e s", s=CAP)), YG if g else None)
            done(dve.tensor_copy(w2s[:, :, :], bank[0][0:CAP, P:P + 2 * NE].rearrange("p (e k) -> p e k", k=2)))
            settle()
            done(dve.tensor_tensor(wslot[:, :], w2s[:, :, 0], w2s[:, :, 1], ALU.add))

            def add_b1(e):
                dve.wait_ge(f_pe, HID[e])
                if e >= 2:
                    dve.wait_ge(f_act, GELU0 + e - 2)
                done(dve.tensor_tensor(hb[e % 2][:, :, :], bank[5 + e % 2][:, 0:HALF].rearrange("p (f s) -> p f s", s=CAP),
                                       bc(b1T[:, e, :], [P, FC, CAP], 2), ALU.add), HB[e])

            settle()
            add_b1(0)
            for e in range(NE):
                if e + 1 < NE:
                    add_b1(e + 1)
                dve.wait_ge(f_pe, DOWN[e])
                if e >= 2:
                    dve.wait_ge(f_pe, SCAT[e - 2])
                o = bank[7][0:CAP, 0:C]
                done(dve.tensor_scalar(ohi[e % 2][:, :], o, wslot[:, e:e + 1], None, ALU.mult))
                settle()
                done(dve.scalar_tensor_tensor(olo[e % 2][:, :], o, wslot[:, e:e + 1], ohi[e % 2][:, :],
                                              ALU.mult, ALU.subtract), OLO[e])
            dve.wait_ge(f_pe, SCAT[NE - 1])
            for g in range(2):
                done(dve.tensor_tensor(res[:, 4 * g:4 * g + 4, :],
                                       bank[1 + g][0:CAP, :].rearrange("p (a k) -> p a k", k=P),
                                       base[:, 4 * g:4 * g + 4, :], ALU.add), OUT_READY[g])


_INS = ['x', 'ctx_768', 'L0_attn_W_qkv', 'L0_attn_b_qkv', 'L0_attn_W_out', 'L0_attn_b_out', 'L0_xattn_Wq',
        'L0_xattn_Wkv', 'L0_xattn_Wproj', 'L0_xattn_bproj', 'L0_ffn_gate_w', 'L0_ffn_ln_gamma', 'L0_ffn_ln_beta',
        'L0_ffn_fc1s', 'L0_ffn_b1s', 'L0_ffn_fc2s', 'L0_ffn_b2s']


def kernel(**inputs):
    import numpy as _np
    import concourse.bacc as _bacc
    from concourse import mybir as _mybir
    from concourse.bass_utils import run_bass_kernel_spmd as _run

    nc = _bacc.Bacc("TRN2", target_bir_lowering=False, num_devices=1)
    arrays, args = {}, []
    for name in _INS:
        a = _np.ascontiguousarray(inputs[name])
        arrays[f"in_{name}"] = a
        args.append(nc.dram_tensor(f"in_{name}", a.shape, _mybir.dt.from_np(a.dtype), kind="ExternalInput").ap())
    shape = arrays["in_x"].shape
    args.append(nc.dram_tensor("out_0", shape, _mybir.dt.float32, kind="ExternalOutput").ap())
    decoder_layer(nc, *args)
    r = _run(nc, [arrays], core_ids=[0])
    return r.results[0]["out_0"]
```

```python
from contextlib import ExitStack

import concourse.bass as bass
from concourse import mybir

F32 = mybir.dt.float32
F16 = mybir.dt.float16
I32 = mybir.dt.int32
ALU = mybir.AluOpType
ACT = mybir.ActivationFunctionType
X = mybir.AxisListType.X

P = 128
EPS = 1e-5


def decoder_layer(nc, x, ctx_768, W_qkv, b_qkv, W_out, b_out, Wq, Wkv, Wproj, bproj,
                  gate_w, ln_gamma, ln_beta, fc1s, b1s, fc2s, b2s, out):
    B, N, C = x.shape
    L, E = ctx_768.shape[1:]
    H = 16
    DH = C // H
    DK = Wq.shape[1] // H
    T = B * N
    ROWS = H * N
    TILES = ROWS // P
    KP = 125
    KC = L // KP
    GROUPS = 3
    GB = KC // GROUPS
    GW = GB * KP
    HALF_TILES = [4, 3]
    HW = [P * n for n in HALF_TILES]
    CHUNKS = 2 * KC
    NMAX = TILES * GROUPS
    NE, F = fc1s.shape[:2]
    FC = F // P
    CAP = T // NE
    TT = T // CAP
    REP = P // NE
    ROUNDS = 7
    SCALE = float(DK) ** -0.5
    ATT = float(C) ** -0.5
    HALF = T // 2

    ctx = ExitStack()
    with ctx:
        def sb(name, shape, dt=F32):
            return ctx.enter_context(nc.sbuf_tensor(name, shape, dt))

        def sem(name):
            return ctx.enter_context(nc.semaphore(name))

        bank = [ctx.enter_context(nc.psum_tensor(f"bank{i}", [P, 512], F32)) for i in range(8)]
        SC = bank[0:2]
        MX = bank[2:4]
        ACC = bank[4:6]
        MISC = bank[6:8]

        ident = sb("ident", [P, P])
        ident16 = sb("ident16", [P, P], F16)
        headmask = sb("headmask", [P, H])
        tri = sb("tri", [CAP, CAP], F16)
        ones16 = sb("ones16", [CAP, CAP], F16)
        onesrow = sb("onesrow", [1, CAP])
        block = sb("block", [P, P], F16)
        jcol_i = sb("jcol_i", [P, NE], I32)
        jcol8 = sb("jcol8", [P, NE])
        jcol = sb("jcol", [P, 1])
        iota_i = sb("iota_i", [CAP, CAP], I32)
        iota1 = sb("iota1", [CAP, CAP])
        neghalf = sb("neghalf", [P, TT])

        wqkv = sb("wqkv", [C, 3 * C])
        wout = sb("wout", [C, C])
        bq = sb("bq", [C, 1])
        bk = sb("bk", [C, 1])
        bv = sb("bv", [N, C])
        bout = sb("bout", [1, C])
        bpr = sb("bpr", [C, 1])
        Mhi = sb("Mhi", [C, H, E], F16)
        Mlo = sb("Mlo", [C, H, E], F16)
        U = sb("U", [E, H, C])

        first_space = ExitStack()

        def at_first(name, shape, dt=F32):
            return first_space.enter_context(nc.sbuf_tensor(name, shape, dt))

        wq = at_first("wq", [C, H * DK])
        wkv = at_first("wkv", [E, 2 * H * DK])
        wproj = at_first("wproj", [P, H // 2, C])
        wqT = at_first("wqT", [P, H // 2, C])
        wkT = at_first("wkT", [P, H // 2, E])
        wvT = at_first("wvT", [P, H // 2, E])
        first_space.close()
        fc1 = sb("fc1", [P, NE * FC, C])
        fc2 = sb("fc2", [C, NE, F])

        x1 = sb("x1", [N, B, C])
        gate = sb("gate", [NE, C])
        b1r = sb("b1r", [NE * FC, P])

        oT_space = ExitStack()
        oT = oT_space.enter_context(nc.sbuf_tensor("oT", [E, B, ROWS], F32))

        early_space = ExitStack()

        def early(name, shape, dt=F32):
            return early_space.enter_context(nc.sbuf_tensor(name, shape, dt))

        xin = early("xin", [N, B, C])
        st = [early(f"st{k}", [N, 6]) for k in range(2)]
        mv = [early(f"mv{k}", [N, 2]) for k in range(2)]
        ve = [early(f"ve{k}", [N, 1]) for k in range(2)]
        rs = [early(f"rs{k}", [N, 1]) for k in range(2)]
        xn = [early(f"xn{k}", [N, C]) for k in range(2)]
        xT = early("xT", [C, N])
        kT = early("kT", [C, N])
        v = early("v", [N, C])
        qblk = early("qblk", [C, H, N])
        es = early("es", [P, TILES, N])
        ep = early("ep", [P, TILES, N])
        en = early("en", [P, TILES, N])
        amax = early("amax", [P, TILES])
        asum = early("asum", [P, TILES])
        arec = early("arec", [P, TILES])
        aT = early("aT", [N, ROWS])
        ao = early("ao", [N, C])
        aoT = early("aoT", [C, N])
        x1Thi = early("x1Thi", [C, N], F16)
        x1Tlo = early("x1Tlo", [C, N], F16)
        qT = early("qT", [C, N])

        cf = [early(f"cf{i}", [KP, KC, E]) for i in range(2)]
        cs = [early(f"cs{i}", [KP, 2, KC, E + 1], F16) for i in range(2)]
        cT = [early(f"cT{i}", [E + 1, 2, L], F16) for i in range(2)]
        qhi = [early(f"qhi{i}", [E + 1, ROWS], F16) for i in range(2)]
        qlo = [early(f"qlo{i}", [E, ROWS], F16) for i in range(2)]
        prob = [early(f"prob{i}", [KP, HW[0]]) for i in range(3)]
        phi = [early(f"phi{i}", [KP, HW[0]], F16) for i in range(3)]
        plo = [early(f"plo{i}", [KP, HW[0]], F16) for i in range(3)]
        mx = early("mx", [P, TILES, GROUPS])
        nmax = early("nmax", [P, TILES])
        rden = early("rden", [P, HALF_TILES[0]])
        on = [early(f"on{g}", [P, HALF_TILES[g], E]) for g in range(2)]

        early_space.close()
        oT_space.close()

        fc1T = sb("fc1T", [C, NE * FC, P])
        fc2T = sb("fc2T", [P, NE * FC, C])
        G = sb("G", [CAP, TT, NE, CAP], F16)
        th = sb("th", [P, T])
        vals = sb("vals", [P, T])
        mge = sb("mge", [P, T], F16)
        mgt = sb("mgt", [P, T], F16)

        yT = sb("yT", [C, T])
        x2 = sb("x2", [CAP, TT, C])
        xf = sb("xf", [CAP, TT, C])
        base = sb("base", [CAP, TT, C])
        y1 = sb("y1", [CAP, TT, C])
        yhi = sb("yhi", [CAP, TT, C], F16)
        ylo = sb("ylo", [CAP, TT, C], F16)
        fst = sb("fst", [CAP, TT, 6])
        fmv = sb("fmv", [CAP, TT, 2])
        fve = sb("fve", [CAP, TT])
        frs = sb("frs", [CAP, TT])
        gateT = sb("gateT", [C, NE, REP])
        xfT = sb("xfT", [C, T])
        junk = sb("junk", [P, T], F16)
        thr = sb("thr", [P, 1])
        low = sb("low", [P, 1])
        cnt = sb("cnt", [P, 1])
        flag = sb("flag", [P, 1], F16)
        ge = sb("ge", [CAP, TT, NE])
        sel = sb("sel", [CAP, 2, TT, NE], F16)
        vn = sb("vn", [CAP, TT, NE])
        v2 = sb("v2", [CAP, TT, NE, 2], F16)
        cg = sb("cg", [CAP, NE])
        pa = sb("pa", [CAP, TT, NE])
        pb = sb("pb", [CAP, TT, NE])
        slot = sb("slot", [CAP, TT, NE])
        GT = sb("GT", [CAP, NE, TT, CAP], F16)
        wslot = sb("wslot", [CAP, NE])
        w2s = sb("w2s", [CAP, NE, 2])
        ygT = sb("ygT", [C, NE, CAP])
        b1T = sb("b1T", [P, NE, FC])
        hb = [sb(f"hb{i}", [P, FC, CAP]) for i in range(2)]
        hg = [sb(f"hg{i}", [P, FC, CAP]) for i in range(2)]
        ohi = [sb(f"ohi{i}", [CAP, C], F16) for i in range(2)]
        olo = [sb(f"olo{i}", [CAP, C], F16) for i in range(2)]
        res = sb("res", [CAP, TT, C])
        x1p = sb("x1p", [CAP, TT, C])
        gam = sb("gam", [CAP, C])
        bet = sb("bet", [CAP, C])
        b2r = sb("b2r", [1, NE, C])

        ld_x, ld_wq, ld_wkv, ld_qkv, ld_bias, ld_wproj, ld_small, ld_ffn, ld_late = (sem("ld_" + n) for n in (
            "x", "wq", "wkv", "qkv", "bias", "wproj", "small", "ffn", "late"))
        ld_ctx = [sem("ld_ctx0"), sem("ld_ctx1")]
        stored = sem("stored")
        passed = sem("passed")
        const_ready = sem("const_ready")
        wT_full = sem("wT_full")
        wT_ready = sem("wT_ready")
        mu_full = sem("mu_full")
        mu_ready = sem("mu_ready")
        mlo_ready = sem("mlo_ready")
        misc_full = [sem("misc_full0"), sem("misc_full1")]
        stats_done, aggr_done, eps_done, rstd_done, norm_done = ([sem(n + str(k)) for k in range(2)] for n in (
            "stats_done", "aggr_done", "eps_done", "rstd_done", "norm_done"))
        xT_ready, qkv_ready, amax_ready, es_ready, ep_ready, asum_ready, arec_ready, en_ready = (sem(n) for n in (
            "xT_ready", "qkv_ready", "amax_ready", "es_ready", "ep_ready", "asum_ready", "arec_ready", "en_ready"))
        aT_ready, ao_ready, aoT_ready, x1_ready = (sem(n) for n in ("aT_ready", "ao_ready", "aoT_ready", "x1_ready"))
        qT_ready, qblk_ready, arec_scaled, x1Thi_ready, x1Tlo_ready = (sem(n) for n in (
            "qT_ready", "qblk_ready", "arec_scaled", "x1Thi_ready", "x1Tlo_ready"))
        qhi_ready, qlo_ready, cs_ready = (sem(n) for n in ("qhi_ready", "qlo_ready", "cs_ready"))
        cThi_ready, cTlo_ready = sem("cThi_ready"), sem("cTlo_ready")
        ones_ready = sem("ones_ready")
        mx_full, mx_done, nmax_ready, mxT_full, mxT_ready = (sem(n) for n in (
            "mx_full", "mx_done", "nmax_ready", "mxT_full", "mxT_ready"))
        sc_full, prob_ready, phi_ready, plo_ready, plo_pool_ready, pv_done = (sem(n) for n in (
            "sc_full", "prob_ready", "phi_ready", "plo_ready", "plo_pool_ready", "pv_done"))
        rden_ready, on_ready, oT_full, oT_ready = (sem(n) for n in ("rden_ready", "on_ready", "oT_full", "oT_ready"))
        f_pe, f_dve, f_act, f_pool = (sem(n) for n in ("f_pe", "f_dve", "f_act", "f_pool"))

        def count(p, h, per, off):
            return p * (2 * per) + (h * per + off)

        def wait(eng, s, val):
            if isinstance(val, int) and val <= 0:
                return
            eng.wait_ge(s, val)

        USES = [["xT", "qkv", "S", "PT0", "PT1", "c0", "c1", "c2"], ["PV", "aoT", "y", "x1T", "q0", "q1"]]
        READ = {"xT": (xT_ready, 1, 1), "qkv": (qkv_ready, 1, 1), "S": (es_ready, 1, 1),
                "PT0": (aT_ready, 2, 1), "PT1": (aT_ready, 2, 2), "PV": (ao_ready, 1, 1),
                "aoT": (aoT_ready, 1, 1), "y": (x1_ready, 1, 1), "x1T": (x1Tlo_ready, 1, 1),
                "c0": (cTlo_ready, 3, 1), "c1": (cTlo_ready, 3, 2), "c2": (cTlo_ready, 3, 3),
                "q0": (qlo_ready, 2, 1), "q1": (qlo_ready, 2, 2)}

        def stage(name):
            k = int(name in USES[1])
            return (k, USES[k].index(name)) if name in USES[k] else (None, None)

        def wait_full(eng, p, h, name):
            k, n = stage(name)
            eng.wait_ge(misc_full[k], count(p, h, len(USES[k]), n + 1))

        def wait_bank_read(eng, p, h, name):
            k, n = stage(name)
            s, per, off = READ[USES[k][n - 1]]
            wait(eng, s, count(p, h, per, off if n >= 1 else off - per))

        def batch(p, h):
            return p * 2 + h

        MAXIMA = [0, 0, 0, 0, 0, 1, 2, 1, 2, 1, 0, 2, 1, 2, 0, 2, 2, 2, 1, 2, 0, 0, 0, 0]
        assert sum(MAXIMA) == NMAX and len(MAXIMA) == CHUNKS

        POOL_CHUNKS = (13, 17)

        def low_place(i):
            back, k = i // CHUNKS, i % CHUNKS
            mine = [c for c in range(CHUNKS) if (c in POOL_CHUNKS) == (k in POOL_CHUNKS)]
            return (plo_pool_ready if k in POOL_CHUNKS else plo_ready), len(mine), back * len(mine) + mine.index(k) + 1

        def wait_low(eng, p, h, i):
            s, per, off = low_place(i)
            wait(eng, s, count(p, h, per, off))

        def mx_bank(h, j):
            return MX[(h * NMAX + j) % 2]

        def chunk(i):
            g = i % 2
            return i // 2, g, slice(g * HW[0], g * HW[0] + HW[g])

        M_BANK, U_BANK = [0, 1, 2, 3], [4, 5, 0, 1]

        CONSTS = 20
        LD_SMALL = 5 * 16
        LD_LATE = 5 * 16
        LD_FFN = 2 * 16

        AGGR3 = [2 + TT, 4 + 5 * TT // 2]
        NORM3 = [a + TT // 2 for a in AGGR3]
        GATE_T = NORM3[1] + 2
        AGGR4 = GATE_T + 2 * TT
        VALS = AGGR4 + 4
        NORM_ROUNDS = [0, 2, 2, 2, 2, 0, 0]
        FLAG = [VALS + 4 * r + 3 + sum(NORM_ROUNDS[:r]) for r in range(ROUNDS)]
        NORM4 = FLAG[4] + NORM_ROUNDS[4]
        MGE = VALS + 4 * ROUNDS + TT + 1
        MGT = MGE + 1
        V2 = MGT + 4
        SEL = V2 + 3
        G0 = SEL + 8
        YG = G0 + TT + 2
        HB = [YG + 3] + [YG + 4 + 3 * e for e in range(NE - 1)]
        OLO = [YG + 6 + 3 * e for e in range(NE - 1)] + [YG + 5 + 3 * (NE - 1)]
        OUT_READY = [OLO[-1] + 1, OLO[-1] + 2]
        EARLY_GROUPS = 5
        SEARCH_GROUPS = [2, 2, 2, 2, 1, 1, 1]
        assert EARLY_GROUPS + sum(SEARCH_GROUPS) == 2 * NE
        PE_BEFORE_SEARCH = 9 + EARLY_GROUPS
        SEARCH = [PE_BEFORE_SEARCH + r + 1 + sum(SEARCH_GROUPS[:r]) for r in range(ROUNDS)]
        VN_FULL = PE_BEFORE_SEARCH + ROUNDS + sum(SEARCH_GROUPS) + 1
        MASK_FULL = VN_FULL + 2
        TOT_FULL = MASK_FULL + 3
        G_FULL = TOT_FULL + 1
        WSLOT = G_FULL + TT
        f = WSLOT + 1
        HID = [f] + [f + 1 if e == 1 else f + 3 * (e - 1) for e in range(1, NE)]
        DOWN = [f + 2] + [f + 1 + 3 * e for e in range(1, NE - 1)] + [f + 3 * (NE - 1)]
        SCAT = [f + 5 + 3 * e for e in range(NE - 2)] + [f + 3 * (NE - 1) + 1, f + 3 * (NE - 1) + 2]
        XFT = EARLY_GROUPS + 1
        TANH = XFT + 2
        GT0 = TANH + 1 + sum(SEARCH_GROUPS)
        GELU0 = GT0 + TT + 1

        def pass_wait(eng):
            eng.sem_inc(passed, 1)

        blk = ctx.enter_context(nc.Block())

        @blk.sync
        def _(sp):
            sp.dma_start(xin[:, :, :], x.rearrange("b n c -> n b c")).then_inc(ld_x, 16)
            sp.dma_start(wq[:, :], Wq).then_inc(ld_wq, 16)
            sp.dma_start(wkv[:, :], Wkv).then_inc(ld_wkv, 16)
            sp.dma_start(wqkv[:, :], W_qkv).then_inc(ld_qkv, 16)
            sp.dma_start(cf[0][:, :, :], ctx_768[0].rearrange("(p c) e -> p c e", p=KP)).then_inc(ld_ctx[0], 16)
            sp.dma_start(cf[1][:, :, :], ctx_768[1].rearrange("(p c) e -> p c e", p=KP)).then_inc(ld_ctx[1], 16)
            sp.dma_start(wproj[:, :, :], Wproj.rearrange("(a p) c -> p a c", p=P)).then_inc(ld_wproj, 16)
            sp.wait_ge(mu_ready, 8)
            sp.dma_start(fc1[:, :, :], fc1s.rearrange("e (f p) c -> p (e f) c", p=P)).then_inc(ld_ffn, 16)
            sp.dma_start(fc2[:, :, :], fc2s.rearrange("e c f -> c e f")).then_inc(ld_ffn, 16)

            def load_context(s, b):
                sp.dma_start(cf[s][:, :, :], ctx_768[b].rearrange("(p c) e -> p c e", p=KP)).then_inc(ld_ctx[s], 16)

            with sp.Fori(1, B // 2) as p:
                for h in range(2):
                    sp.wait_ge(cs_ready, count(p, h, 2, -2))
                    sp.wait_ge(cTlo_ready, count(p, h, GROUPS, -GROUPS))
                    load_context(h, p * 2 + h)
            sp.wait_ge(oT_ready, 2 * B)
            for h in range(2):
                sp.dma_start(x1p[h * N:(h + 1) * N, :, :], x1[:, h::2, :]).then_inc(ld_late, 16)
            sp.dma_start(gam[:, :], ln_gamma.partition_broadcast(CAP)).then_inc(ld_late, 16)
            sp.dma_start(bet[:, :], ln_beta.partition_broadcast(CAP)).then_inc(ld_late, 16)
            sp.dma_start(b2r[:, :, :], b2s.unsqueeze(0)).then_inc(ld_late, 16)
            o = out.rearrange("b n c -> (b n) c").rearrange("(j t) c -> t j c", t=CAP)
            for g in range(2):
                sp.wait_ge(f_dve, OUT_READY[g])
                sp.dma_start(o[:, 4 * g:4 * g + 4, :], res[:, 4 * g:4 * g + 4, :]).then_inc(stored, 16)
            sp.wait_ge(stored, 32)

        @blk.gpsimd
        def _(pool):
            steps = [0]

            def made(ins):
                steps[0] += 1
                ins.then_inc(const_ready, 1)

            def follows():
                pool.wait_ge(const_ready, steps[0])

            made(pool.memset(ident[:, :], 0.0))
            made(pool.memset(headmask[:, :], 1.0))
            made(pool.memset(neghalf[:, :], -0.5))
            made(pool.memset(tri[:, :], 1.0))
            made(pool.memset(block[:, :], 1.0))
            made(pool.memset(ones16[:, :], 1.0))
            made(pool.memset(onesrow[:, :], 1.0))
            made(pool.iota(iota_i[:, :], pattern=[[1, CAP]], base=1, channel_multiplier=0))
            made(pool.iota(jcol_i[:, :], pattern=[[-REP, NE]], base=0, channel_multiplier=1))
            follows()
            made(pool.affine_select(out=ident[:, :], in_=ident[:, :], compare_op=ALU.not_equal, fill=1.0, base=0,
                                    pattern=[[-1, P]], channel_multiplier=1))
            made(pool.affine_select(out=headmask[:, :], in_=headmask[:, :], compare_op=ALU.is_ge, fill=0.0, base=0,
                                    pattern=[[-DH, H]], channel_multiplier=1))
            made(pool.affine_select(out=tri[:, :], in_=tri[:, :], compare_op=ALU.is_ge, fill=0.0, base=0,
                                    pattern=[[1, CAP]], channel_multiplier=-1))
            made(pool.affine_select(out=block[:, :], in_=block[:, :], compare_op=ALU.is_ge, fill=0.0, base=-1,
                                    pattern=[[-REP, NE], [0, REP]], channel_multiplier=1))
            made(pool.tensor_copy(iota1[:, :], iota_i[:, :]))
            made(pool.tensor_copy(jcol8[:, :], jcol_i[:, :]))
            follows()
            made(pool.affine_select(out=jcol8[:, :], in_=jcol8[:, :], compare_op=ALU.is_ge, fill=0.0, base=0,
                                    pattern=[[-REP, NE]], channel_multiplier=1))
            made(pool.tensor_copy(ident16[:, :], ident[:, :]))
            made(pool.affine_select(out=headmask[:, :], in_=headmask[:, :], compare_op=ALU.is_ge, fill=0.0, base=DH - 1,
                                    pattern=[[DH, H]], channel_multiplier=-1))
            made(pool.affine_select(out=block[:, :], in_=block[:, :], compare_op=ALU.is_ge, fill=0.0, base=REP - 1,
                                    pattern=[[REP, NE], [0, REP]], channel_multiplier=-1))
            follows()
            made(pool.affine_select(out=jcol8[:, :], in_=jcol8[:, :], compare_op=ALU.is_ge, fill=0.0, base=REP - 1,
                                    pattern=[[REP, NE]], channel_multiplier=-1))
            assert steps[0] == CONSTS, steps[0]

            def rstd(p, h, k):
                pool.wait_ge(aggr_done[k], count(p, h, 1, 1))
                pass_wait(pool)
                pool.tensor_scalar(ve[k][:, :], mv[k][:, 1:2], EPS, None, ALU.add).then_inc(eps_done[k], 1)
                pool.wait_ge(eps_done[k], count(p, h, 1, 1))
                pool.tensor_tensor(rs[k][:, :], ve[k][:, :], neghalf[0:N, 0:1], ALU.pow).then_inc(rstd_done[k], 1)

            def bc(ap, shape, axis):
                return ap.unsqueeze(axis).to_broadcast(shape)

            def mask_q(p, h):
                pool.wait_ge(qT_ready, count(p, h, 1, 1))
                pool.tensor_tensor(qblk[:, :, :], bc(qT[:, :], [C, H, N], 1), bc(headmask[:, :], [C, H, N], 2),
                                   ALU.mult).then_inc(qblk_ready, 1)

            def soften(p, h):
                pool.wait_ge(arec_scaled, count(p, h, 1, 1))
                pool.tensor_tensor(en[:, :, :], ep[:, :, :], bc(arec[:, :], [P, TILES, N], 2),
                                   ALU.mult).then_inc(en_ready, 1)

            def split_high(p, h):
                pool.wait_ge(ld_ctx[h], (p + 1) * 16)
                wait(pool, pv_done, count(p, h, CHUNKS, -CHUNKS))
                pass_wait(pool)
                pool.tensor_copy(cs[h][:, 0, :, 0:E], cf[h][:, :, :]).then_inc(cs_ready, 1)

            def split_low(p, h):
                pool.wait_ge(cs_ready, count(p, h, 2, 1))
                pool.tensor_tensor(cs[h][:, 1, :, 0:E], cf[h][:, :, :], cs[h][:, 0, :, 0:E],
                                   ALU.subtract).then_inc(cs_ready, 1)

            def low_parts(p, h, i):
                _, g, _ = chunk(i)
                pool.wait_ge(phi_ready, count(p, h, CHUNKS, i + 1))
                pool.tensor_tensor(plo[i % 3][:, 0:HW[g]], prob[i % 3][:, 0:HW[g]], phi[i % 3][:, 0:HW[g]],
                                   ALU.subtract).then_inc(plo_pool_ready, 1)

            def half(p, h, last=False):
                np_, nh = (p, 1) if h == 0 else (p + 1, 0)
                if not last:
                    rstd(p + 1, h, 0)
                split_high(np_, nh)
                split_low(np_, nh)
                if not last:
                    mask_q(p + 1, h)
                for i in [c for c in POOL_CHUNKS if c < 14]:
                    low_parts(p, h, i)
                if not last:
                    soften(p + 1, h)
                for i in [c for c in POOL_CHUNKS if c >= 14]:
                    low_parts(p, h, i)
                if not last:
                    rstd(p + 1, h, 1)

            pool.wait_ge(const_ready, CONSTS)
            rstd(0, 0, 0)
            mask_q(0, 0)
            rstd(0, 1, 0)
            split_high(0, 0)
            soften(0, 0)
            split_low(0, 0)
            rstd(0, 0, 1)
            mask_q(0, 1)
            soften(0, 1)
            rstd(0, 1, 1)
            half(0, 0)
            half(0, 1)
            with pool.Fori(1, B // 2 - 1) as p:
                half(p, 0)
                half(p, 1)
            half(B // 2 - 1, 0, last=True)
            for i in POOL_CHUNKS:
                low_parts(B // 2 - 1, 1, i)

            def f_rstd(n, after, tiles):
                pool.wait_ge(f_dve, after)
                pool.tensor_scalar(fve[:, tiles], fmv[:, tiles, 1], EPS, None, ALU.add).then_inc(f_pool, 1)
                pool.wait_ge(f_pool, n)
                pool.tensor_tensor(frs[:, tiles], fve[:, tiles], neghalf[0:CAP, tiles], ALU.pow).then_inc(f_pool, 1)

            for g in range(2):
                f_rstd(1 + 2 * g, AGGR3[g], slice(g * TT // 2, (g + 1) * TT // 2))
            f_rstd(5, AGGR4, slice(0, TT))
            pool.wait_ge(f_dve, NORM4)
            pool.wait_ge(ld_late, LD_LATE)
            pool.tensor_tensor(y1[:, :, :], y1[:, :, :], gam[:, :].unsqueeze(1).to_broadcast([CAP, TT, C]),
                               ALU.mult).then_inc(f_pool, 1)
            pool.wait_ge(f_pool, 7)
            pool.tensor_tensor(y1[:, :, :], y1[:, :, :], bet[:, :].unsqueeze(1).to_broadcast([CAP, TT, C]),
                               ALU.add).then_inc(f_pool, 1)
            pool.wait_ge(f_pool, 8)
            pool.tensor_copy(yhi[:, :, :], y1[:, :, :]).then_inc(f_pool, 1)
            pool.wait_ge(f_pool, 9)
            pool.tensor_tensor(ylo[:, :, :], y1[:, :, :], yhi[:, :, :], ALU.subtract).then_inc(f_pool, 1)

        @blk.tensor
        def _(pe):
            def prep(name, p, h):
                m = MISC[stage(name)[0]]
                wait_bank_read(pe, p, h, name)
                if name == "xT":
                    pe.wait_ge(norm_done[0], count(p, h, 1, 1))
                    pass_wait(pe)
                    ins = pe.transpose(m[:, 0:N], xn[0][:, :], ident[0:N, 0:N])
                elif name == "qkv":
                    pe.wait_ge(xT_ready, count(p, h, 1, 1))
                    pe.matmul(m[:, 0:N], wqkv[:, 0:C], xT[:, :], start=True, stop=True)
                    pe.matmul(m[:, N:2 * N], wqkv[:, C:2 * C], xT[:, :], start=True, stop=True)
                    ins = pe.matmul(m[0:N, P:2 * P], xT[:, :], wqkv[:, 2 * C:3 * C], start=True, stop=True)
                elif name == "S":
                    pe.wait_ge(qkv_ready, count(p, h, 1, 1))
                    pe.wait_ge(qblk_ready, count(p, h, 1, 1))
                    q = qblk[:, :, :].rearrange("c h n -> c (h n)")
                    for t in range(TILES):
                        ins = pe.matmul(m[:, t * N:(t + 1) * N], q[:, t * P:(t + 1) * P], kT[:, :],
                                        start=True, stop=True)
                elif name in ("PT0", "PT1"):
                    pe.wait_ge(en_ready, count(p, h, 1, 1))
                    pass_wait(pe)
                    first = 0 if name == "PT0" else 4
                    for t in range(first, min(first + 4, TILES)):
                        ins = pe.transpose(m[0:N, (t - first) * P:(t - first + 1) * P], en[:, t, :], ident[:, :])
                elif name == "PV":
                    pe.wait_ge(aT_ready, count(p, h, 2, 2))
                    pass_wait(pe)
                    for k in range(H):
                        ins = pe.matmul(m[0:N, k * DH:(k + 1) * DH], aT[:, k * N:(k + 1) * N],
                                        v[:, k * DH:(k + 1) * DH], start=True, stop=True)
                elif name == "aoT":
                    pe.wait_ge(ao_ready, count(p, h, 1, 1))
                    pass_wait(pe)
                    ins = pe.transpose(m[:, 0:N], ao[:, :], ident[0:N, 0:N])
                elif name == "y":
                    pe.wait_ge(aoT_ready, count(p, h, 1, 1))
                    pe.matmul(m[0:N, 0:C], aoT[:, :], wout[:, :], start=True, stop=False)
                    ins = pe.matmul(m[0:N, 0:C], onesrow[:, 0:N], bout[:, :], start=False, stop=True)
                elif name == "x1T":
                    pe.wait_ge(norm_done[1], count(p, h, 1, 1))
                    pass_wait(pe)
                    ins = pe.transpose(m[:, 0:N], xn[1][:, :], ident[0:N, 0:N])
                elif name in ("c0", "c1", "c2"):
                    k = int(name[1])
                    if k == 0:
                        pe.wait_ge(ld_ctx[h], (p + 1) * 16)
                    for j in range(GB):
                        ins = pe.transpose(m[0:E, j * KP:(j + 1) * KP], cf[h][:, GB * k + j, :], ident[0:KP, 0:KP])
                else:
                    pe.wait_ge(x1Tlo_ready, count(p, h, 1, 1))
                    first = 0 if name == "q0" else H // 2
                    for k in range(H // 2):
                        o = m[0:E, k * N:(k + 1) * N]
                        pe.matmul(o, Mhi[:, first + k, :], x1Thi[:, :], start=True, stop=False)
                        pe.matmul(o, Mhi[:, first + k, :], x1Tlo[:, :], start=False, stop=False)
                        ins = pe.matmul(o, Mlo[:, first + k, :], x1Thi[:, :], start=False, stop=True)
                ins.then_inc(misc_full[stage(name)[0]], 1)

            def maximum(p, h, j):
                t, k = j // GROUPS, j % GROUPS
                if j == 0:
                    pe.wait_ge(cTlo_ready, count(p, h, GROUPS, GROUPS))
                    wait(pe, mxT_ready, count(p, h, 2, 0))
                pe.wait_ge(qlo_ready, count(p, h, 2, 1 if (t + 1) * P <= HALF else 2))
                wait(pe, mx_done, count(p, h, NMAX, j - 1))
                pe.matmul(mx_bank(h, j)[:, 0:GW], qhi[h][0:E, t * P:(t + 1) * P], cT[h][0:E, 0, k * GW:(k + 1) * GW],
                          start=True, stop=True).then_inc(mx_full, 1)

            def turn_maxima(p, h, g):
                pe.wait_ge(nmax_ready, count(p, h, 1, 1))
                for a in range(HALF_TILES[g]):
                    t = g * HALF_TILES[0] + a
                    ins = pe.transpose(MX[g][0:1, a * P:(a + 1) * P], nmax[:, t:t + 1], ident[:, :])
                ins.then_inc(mxT_full, 1)

            def scores(p, h, i):
                c, g, cols = chunk(i)
                if i < 2:
                    pe.wait_ge(mxT_ready, count(p, h, 2, g + 1))
                wait(pe, phi_ready, count(p, h, CHUNKS, i - 1))
                hi, lo = cT[h][:, 0, c * KP:(c + 1) * KP], cT[h][0:E, 1, c * KP:(c + 1) * KP]
                o = SC[i % 2][0:KP, 0:HW[g]]
                pe.matmul(o, hi, qhi[h][:, cols], start=True, stop=False)
                pe.matmul(o, hi[0:E, :], qlo[h][:, cols], start=False, stop=False)
                pe.matmul(o, lo, qhi[h][0:E, cols], start=False, stop=True).then_inc(sc_full, 1)

            def weigh(p, h, i):
                c, g, _ = chunk(i)
                if i == 0:
                    pe.wait_ge(cs_ready, count(p, h, 2, 2))
                if c == 0:
                    wait(pe, oT_ready, count(p, h, 2, g - 1))
                wait_low(pe, p, h, i)
                hi, lo = cs[h][:, 0, c, :], cs[h][:, 1, c, 0:E]
                for a in range(HALF_TILES[g]):
                    rows = slice(a * P, (a + 1) * P)
                    o = ACC[g][:, a * P:a * P + E + 1]
                    pe.matmul(o, phi[i % 3][:, rows], hi, start=(c == 0 and a == 0), stop=False, skip_group_check=True)
                    pe.matmul(o[:, 0:E], phi[i % 3][:, rows], lo, start=False, stop=False, skip_group_check=True)
                    ins = pe.matmul(o, plo[i % 3][:, rows], hi, start=False, stop=(c == KC - 1),
                                    skip_group_check=True)
                ins.then_inc(pv_done, 1)

            def turn_out(p, h, g):
                pe.wait_ge(on_ready, count(p, h, 2, g + 1))
                g %= 2
                for a in range(HALF_TILES[g]):
                    ins = pe.transpose(ACC[g][0:E, a * P:(a + 1) * P], on[g][:, a, :], ident[:, :])
                ins.then_inc(oT_full, 1)

            FIRST_STAGE = {(5, "a"): ["xT"], (6, "b"): ["qkv"], (10, "a"): ["S"], (15, "a"): ["PT0"],
                           (16, "a"): ["PT1"], (18, "a"): ["PV"], (20, "b"): ["aoT"], (21, "a"): ["y"],
                           (22, "b"): ["c0"]}
            SECOND_STAGE = {(0, "b"): ["c1"], (1, "a"): ["x1T"], (3, "a"): ["c2", "q0"], (7, "b"): ["q1"]}

            def half(p, h, last=False, more_first=True):
                np_, nh = (p, 1) if h == 0 else (p + 1, 0)
                j = 0

                def prepare(i, place):
                    for name in FIRST_STAGE.get((i, place), []) if more_first else []:
                        prep(name, p + 1, h)
                    for name in SECOND_STAGE.get((i, place), []) if not last else []:
                        prep(name, np_, nh)

                for i in range(CHUNKS):
                    if i + 2 < CHUNKS:
                        scores(p, h, i + 2)
                    elif not last:
                        scores(np_, nh, i + 2 - CHUNKS)
                    if i == CHUNKS - 1:
                        turn_out(p, h, 0)
                    prepare(i, "a")
                    for m in range(0 if last else MAXIMA[i]):
                        if m == 1:
                            weigh(p, h, i)
                        maximum(np_, nh, j)
                        j += 1
                    if last or MAXIMA[i] < 2:
                        weigh(p, h, i)
                    if i == 0 and not (isinstance(p, int) and p == 0 and h == 0):
                        turn_out(p, h, -1)
                    prepare(i, "b")
                    if i == 20 and not last:
                        turn_maxima(np_, nh, 0)
                    if i == 21 and not last:
                        turn_maxima(np_, nh, 1)

            def turn_weight(g):
                for a in range(4):
                    if g < 2:
                        c = (4 * g + a) * P
                        ins = pe.transpose(bank[g][:, a * P:(a + 1) * P], wq[:, c:c + P], ident[:, :])
                    else:
                        c = (4 * (g - 2) + a) * P
                        ins = pe.transpose(bank[g][:, a * P:a * P + E], wkv[:, c:c + P], ident[0:E, 0:E])
                ins.then_inc(wT_full, 1)

            def make_m(g):
                if g == 0:
                    pe.wait_ge(wT_ready, 4)
                for k in range(4):
                    a, q = 4 * (g // 2) + k, g % 2
                    ins = pe.matmul(bank[M_BANK[g]][:, k * P:k * P + E], wqT[q * DK:(q + 1) * DK, a, :],
                                    wkT[q * DK:(q + 1) * DK, a, :], start=True, stop=True)
                ins.then_inc(mu_full, 1)

            def make_u(g):
                if g == 0:
                    pe.wait_ge(wT_ready, 6)
                    pe.wait_ge(ld_wproj, 16)
                if g >= 2:
                    pe.wait_ge(mu_ready, g - 1)
                    pe.wait_ge(mlo_ready, g - 1)
                for k in range(4):
                    a, q = 4 * (g // 2) + k, g % 2
                    ins = pe.matmul(bank[U_BANK[g]][0:E, k * P:(k + 1) * P], wvT[q * DK:(q + 1) * DK, a, :],
                                    wproj[q * DK:(q + 1) * DK, a, :], start=True, stop=True)
                ins.then_inc(mu_full, 1)

            pe.wait_ge(const_ready, CONSTS)
            pe.wait_ge(ld_wq, 16)
            turn_weight(0)
            turn_weight(1)
            prep("xT", 0, 0)
            pe.wait_ge(ld_wkv, 16)
            turn_weight(2)
            turn_weight(3)
            pe.wait_ge(ld_qkv, 16)
            prep("qkv", 0, 0)
            turn_weight(4)
            turn_weight(5)
            make_m(0)
            prep("S", 0, 0)
            make_m(1)
            make_m(2)
            prep("PT0", 0, 0)
            make_m(3)
            prep("PT1", 0, 0)
            make_u(0)
            prep("PV", 0, 0)
            prep("c0", 0, 0)
            make_u(1)
            prep("aoT", 0, 0)
            prep("c1", 0, 0)
            pe.wait_ge(ld_small, LD_SMALL)
            prep("y", 0, 0)
            prep("c2", 0, 0)
            make_u(2)
            prep("xT", 0, 1)
            prep("x1T", 0, 0)
            prep("qkv", 0, 1)
            make_u(3)
            pe.wait_ge(mlo_ready, 4)
            prep("q0", 0, 0)
            prep("S", 0, 1)
            pe.wait_ge(ones_ready, 4)
            j = 0
            for maxima_before, b, name in ((2, 0, "q1"), (4, 1, "PT0"), (3, 1, "PT1"), (2, 1, "PV"), (2, 1, "aoT"),
                                           (1, 1, "c0"), (1, 1, "y"), (NMAX - 15, 0, None)):
                for _ in range(maxima_before):
                    maximum(0, 0, j)
                    j += 1
                if name:
                    prep(name, 0, b)
            pe.wait_ge(mu_ready, 8)
            for g in range(2):
                turn_maxima(0, 0, g)
            scores(0, 0, 0)
            scores(0, 0, 1)
            half(0, 0)
            half(0, 1)
            with pe.Fori(1, B // 2 - 1) as p:
                half(p, 0)
                half(p, 1)
            half(B // 2 - 1, 0, more_first=False)
            half(B // 2 - 1, 1, last=True, more_first=False)

            def done(ins):
                ins.then_inc(f_pe, 1)

            def turn_y(g):
                pe.wait_ge(f_dve, 1 if g == 0 else NORM3[0] + 1)
                for a in range(4):
                    j = 4 * g + a
                    ins = pe.transpose(bank[2 + g][0:CAP, a * P:(a + 1) * P], yT[:, j * CAP:(j + 1) * CAP],
                                       ident[:, :])
                done(ins)

            pe.wait_ge(phi_ready, CHUNKS * B)
            pe.wait_ge(oT_ready, B)
            for g in range(2):
                if g == 1:
                    pe.wait_ge(oT_ready, 2 * B)
                for k in range(H):
                    if g == 0 and k == H // 4:
                        turn_out(B // 2 - 1, 1, 1)
                    if g == 1 and k == 4:
                        turn_y(0)
                    ins = pe.matmul(bank[g][:, 0:HALF], U[:, k, :],
                                    oT[:, g * B // 2:(g + 1) * B // 2, k * N:(k + 1) * N],
                                    start=(k == 0), stop=(k == H - 1))
                done(ins)
            turn_y(1)
            pe.wait_ge(ld_small, LD_SMALL)
            pe.transpose(bank[6][:, 0:NE], gate[:, :], ident[0:NE, 0:NE])
            ins = pe.transpose(bank[6][:, P:P + NE * FC], b1r[:, :], ident[0:NE * FC, 0:NE * FC])
            done(ins)
            pe.wait_ge(ld_ffn, LD_FFN)

            def turn_weights(g):
                if g >= 2:
                    pe.wait_ge(f_act, g - 1 if g - 2 < EARLY_GROUPS else TANH + 1 + g - 1 - EARLY_GROUPS)
                for a in range(4):
                    if g < NE:
                        src = fc1[:, 4 * g + a, :]
                    else:
                        src = fc2[:, g - NE, a * P:(a + 1) * P]
                    ins = pe.transpose(bank[1 + g % 2][:, a * P:(a + 1) * P], src, ident[:, :])
                done(ins)

            for g in range(EARLY_GROUPS):
                turn_weights(g)
            for g in range(2):
                pe.wait_ge(f_dve, NORM3[g])
                for a in range(4):
                    j = 4 * g + a
                    ins = pe.transpose(bank[4 + g][:, a * CAP:(a + 1) * CAP], xf[:, j, :], ident[0:CAP, 0:CAP])
                done(ins)
            pe.wait_ge(f_dve, GATE_T)
            for g in range(2):
                pe.wait_ge(f_act, XFT + g)
                ins = pe.matmul(bank[6 + g][:, 0:HALF], gateT[:, :, :].rearrange("c e r -> c (e r)"),
                                xfT[:, g * HALF:(g + 1) * HALF], start=True, stop=True)
                done(ins)
            g = EARLY_GROUPS
            for r in range(ROUNDS):
                pe.wait_ge(f_dve, FLAG[r])
                done(pe.matmul(bank[0][:, 0:1], block[:, :], flag[:, :], start=True, stop=True))
                for _ in range(SEARCH_GROUPS[r]):
                    turn_weights(g)
                    g += 1
            assert g == 2 * NE
            pe.wait_ge(f_dve, VALS)
            for g in range(2):
                for a in range(4):
                    j = 4 * g + a
                    ins = pe.transpose(bank[3 + g][0:CAP, a * P:(a + 1) * P], vals[:, j * CAP:(j + 1) * CAP],
                                       ident[:, :])
                done(ins)
            for g, (m, after) in enumerate(((mge, MGE), (mgt, MGT))):
                pe.wait_ge(f_dve, after)
                m16 = bank[5 + g][:, :].bitcast(F16).rearrange("p (j k) -> p j k", k=P)
                for j in range(TT):
                    ins = pe.transpose(m16[0:CAP, j, :], m[:, j * CAP:(j + 1) * CAP], ident16[:, :])
                done(ins)
            pe.wait_ge(f_dve, SEL)
            cum = bank[7][0:CAP, 0:2 * TT * NE].rearrange("p (k j e) -> p k j e", k=2, e=NE)
            pe.matmul(cum, tri[:, :], sel[:, :, :, :], start=True, stop=False, skip_group_check=True)
            for s in range(1, TT):
                ins = pe.matmul(cum[:, :, s:TT, :], ones16[:, :], sel[:, :, 0:TT - s, :], start=False,
                                stop=(s == TT - 1), skip_group_check=True)
            done(ins)
            for j in range(TT):
                ins = pe.matmul(bank[0][0:CAP, 0:NE], ones16[:, :], sel[:, 0, j, :], start=(j == 0),
                                stop=(j == TT - 1))
            done(ins)
            pe.wait_ge(f_pool, 10)
            pe.wait_ge(f_dve, V2)
            pe.wait_ge(f_act, GT0)
            for j in range(TT):
                pe.wait_ge(f_dve, G0 + j)
                gj = G[:, j, :, :].rearrange("p e s -> p (e s)")
                for g in range(2):
                    for part, w in enumerate((yhi, ylo)):
                        pe.matmul(bank[3 + g][:, 0:HALF], w[:, j, :], gj[:, g * HALF:(g + 1) * HALF],
                                  start=(j == 0 and part == 0), stop=(j == TT - 1 and part == 1))
                if j >= 2:
                    pe.wait_ge(f_act, GT0 + j - 1)
                m16 = bank[1 + j % 2][:, :].bitcast(F16).rearrange("p (e k) -> p e k", k=P)
                for e in range(NE):
                    ins = pe.transpose(m16[0:CAP, e, 0:CAP], G[:, j, e, :], ident16[0:CAP, 0:CAP])
                done(ins)
            for j in range(TT):
                for e in range(NE):
                    ins = pe.matmul(bank[0][0:CAP, P + 2 * e:P + 2 * e + 2], G[:, j, e, :], v2[:, j, e, :],
                                    start=(j == 0 and e == 0), stop=(j == TT - 1), skip_group_check=True)
            done(ins)
            def hidden(e):
                if e == 0:
                    pe.wait_ge(f_dve, YG)
                if e >= 2:
                    pe.wait_ge(f_dve, HB[e - 2])
                for a in range(FC):
                    ins = pe.matmul(bank[5 + e % 2][:, a * CAP:(a + 1) * CAP], fc1T[:, FC * e + a, :],
                                    ygT[:, e, :], start=True, stop=True)
                done(ins)

            def down(e):
                pe.wait_ge(f_act, GELU0 + e)
                if e >= 1:
                    pe.wait_ge(f_dve, OLO[e - 1])
                o = bank[7][0:CAP, 0:C]
                for a in range(FC):
                    pe.matmul(o, hg[e % 2][:, a, :], fc2T[:, FC * e + a, :], start=(a == 0), stop=False)
                done(pe.matmul(o, onesrow[:, :], b2r[:, e, :], start=False, stop=True))

            def scatter(e):
                pe.wait_ge(f_dve, OLO[e])
                if e == 0:
                    pe.wait_ge(f_act, GT0 + TT)
                for j in range(TT):
                    for part, w in enumerate((ohi, olo)):
                        ins = pe.matmul(bank[1 + j // 4][0:CAP, (j % 4) * C:(j % 4 + 1) * C], GT[:, e, j, :],
                                        w[e % 2][:, :], start=(e == 0 and j % 4 == 0 and part == 0),
                                        stop=(e == NE - 1 and part == 1), skip_group_check=True)
                done(ins)

            pe.wait_ge(ld_late, LD_LATE)
            hidden(0)
            for e in range(NE):
                if e + 1 < NE:
                    hidden(e + 1)
                down(e)
                if e >= 1:
                    scatter(e - 1)
            scatter(NE - 1)

        @blk.scalar
        def _(act):
            for a, b, s in ((bq[:, :], b_qkv[0:C].rearrange("(c a) -> c a", a=1), ld_bias),
                            (bk[:, :], b_qkv[C:2 * C].rearrange("(c a) -> c a", a=1), ld_bias),
                            (bv[:, :], b_qkv[2 * C:3 * C].partition_broadcast(N), ld_bias),
                            (wout[:, :], W_out, ld_small),
                            (bout[:, :], b_out.unsqueeze(0), ld_small),
                            (bpr[:, :], bproj.rearrange("(c a) -> c a", a=1), ld_small),
                            (gate[:, :], gate_w, ld_small),
                            (b1r[:, :], b1s.rearrange("e (f p) -> (e f) p", p=P), ld_small)):
                act.dma_start(a, b).then_inc(s, 16)
            act.preload_act_table(ACT.Exp)

            def copy(o, i):
                return act.activation(o, i, ACT.Copy)

            def turn_weight(g):
                act.wait_ge(wT_full, g + 1)
                b = bank[g][:, :].rearrange("p (a k) -> p a k", k=P)
                if g < 2:
                    copy(wqT[:, 4 * g:4 * g + 4, :], b).then_inc(wT_ready, 1)
                else:
                    w = wkT if g < 4 else wvT
                    copy(w[:, 4 * (g % 2):4 * (g % 2) + 4, :], b[:, :, 0:E]).then_inc(wT_ready, 1)

            def heads(g):
                return slice(8 * (g // 2) + g % 2, 8 * (g // 2) + 8, 2)

            def make_m(g):
                act.wait_ge(mu_full, g + 1)
                act.activation(Mhi[:, heads(g), :], bank[M_BANK[g]][:, :].rearrange("p (a k) -> p a k", k=P)[:, :, 0:E],
                               ACT.Copy, scale=SCALE).then_inc(mu_ready, 1)

            def make_u(g):
                act.wait_ge(mu_full, g + 5)
                copy(U[:, heads(g), :], bank[U_BANK[g]][0:E, :].rearrange("p (a k) -> p a k", k=P)).then_inc(mu_ready, 1)

            def prep(name, p, h):
                if name == "exp":
                    act.wait_ge(es_ready, count(p, h, 1, 1))
                    act.activation(ep[:, :, :], es[:, :, :], ACT.Exp).then_inc(ep_ready, 1)
                    return
                m = MISC[stage(name)[0]]
                wait_full(act, p, h, name)
                if name == "xT":
                    copy(xT[:, :], m[:, 0:N]).then_inc(xT_ready, 1)
                elif name == "x1T":
                    copy(x1Thi[:, :], m[:, 0:N]).then_inc(x1Thi_ready, 1)
                elif name in ("c0", "c1", "c2"):
                    k = int(name[1])
                    copy(cT[h][0:E, 0, k * GW:(k + 1) * GW], m[0:E, 0:GW]).then_inc(cThi_ready, 1)
                elif name == "PT0":
                    copy(aT[:, 0:4 * P], m[0:N, :]).then_inc(aT_ready, 1)
                elif name == "PT1":
                    copy(aT[:, 4 * P:ROWS], m[0:N, 0:ROWS - 4 * P]).then_inc(aT_ready, 1)
                elif name == "PV":
                    copy(ao[:, :], m[0:N, 0:C]).then_inc(ao_ready, 1)
                elif name == "aoT":
                    copy(aoT[:, :], m[:, 0:N]).then_inc(aoT_ready, 1)
                else:
                    c = HALF * (name == "q1")
                    copy(qhi[h][0:E, c:c + HALF], m[0:E, 0:HALF]).then_inc(qhi_ready, 1)

            def expo(p, h, i):
                _, g, _ = chunk(i)
                src = SC[i % 2][0:KP, 0:HW[g]]
                act.wait_ge(sc_full, count(p, h, CHUNKS, i + 1))
                wait_low(act, p, h, i - 3)
                act.activation(prob[i % 3][:, 0:HW[g]], src, ACT.Exp).then_inc(prob_ready, 1)
                wait(act, pv_done, count(p, h, CHUNKS, i - 2))
                act.activation(phi[i % 3][:, 0:HW[g]], src, ACT.Exp).then_inc(phi_ready, 1)

            def take_maxima(p, h, g):
                act.wait_ge(mxT_full, count(p, h, 2, g + 1))
                copy(qhi[h][E:E + 1, g * HW[0]:g * HW[0] + HW[g]], MX[g][0:1, 0:HW[g]]).then_inc(mxT_ready, 1)

            def take_out(p, h, g, b):
                act.wait_ge(oT_full, count(p, h, 2, g + 1))
                g %= 2
                copy(oT[:, b, g * HW[0]:g * HW[0] + HW[g]], ACC[g][0:E, 0:HW[g]]).then_inc(oT_ready, 1)

            FIRST_STAGE = {5: ["xT"], 11: ["exp"], 15: ["PT0"], 16: ["PT1"], 18: ["PV"], 20: ["aoT"], 22: ["c0"]}
            SECOND_STAGE = {0: ["c1"], 1: ["x1T"], 3: ["c2", "q0"], 7: ["q1"]}

            def half(p, h, last=False, more_first=True):
                np_, nh = (p, 1) if h == 0 else (p + 1, 0)
                for i in range(CHUNKS):
                    if i + 2 < CHUNKS:
                        expo(p, h, i + 2)
                    elif not last:
                        expo(np_, nh, i + 2 - CHUNKS)
                    if i == 0 and not (isinstance(p, int) and p == 0 and h == 0):
                        take_out(p, h, -1, batch(p, h) - 1)
                    if i == CHUNKS - 1:
                        take_out(p, h, 0, batch(p, h))
                    for name in FIRST_STAGE.get(i, []) if more_first else []:
                        prep(name, p + 1, h)
                    for name in SECOND_STAGE.get(i, []) if not last else []:
                        prep(name, np_, nh)
                    if i in (20, 21) and not last:
                        take_maxima(np_, nh, i - 20)

            turn_weight(0)
            turn_weight(1)
            prep("xT", 0, 0)
            for g in range(2, 6):
                turn_weight(g)
            make_m(0)
            prep("exp", 0, 0)
            make_m(1)
            make_m(2)
            prep("PT0", 0, 0)
            make_m(3)
            prep("PT1", 0, 0)
            make_u(0)
            prep("PV", 0, 0)
            prep("c0", 0, 0)
            make_u(1)
            prep("aoT", 0, 0)
            prep("c1", 0, 0)
            prep("c2", 0, 0)
            make_u(2)
            prep("xT", 0, 1)
            prep("x1T", 0, 0)
            make_u(3)
            prep("q0", 0, 0)
            prep("exp", 0, 1)
            prep("q1", 0, 0)
            prep("PT0", 0, 1)
            prep("PT1", 0, 1)
            prep("PV", 0, 1)
            prep("aoT", 0, 1)
            prep("c0", 0, 1)
            take_maxima(0, 0, 0)
            take_maxima(0, 0, 1)
            expo(0, 0, 0)
            expo(0, 0, 1)
            half(0, 0)
            half(0, 1)
            with act.Fori(1, B // 2 - 1) as p:
                half(p, 0)
                half(p, 1)
            half(B // 2 - 1, 0, more_first=False)
            half(B // 2 - 1, 1, last=True, more_first=False)
            take_out(B // 2 - 1, 1, 1, B - 1)

            n = [0]

            def done(ins, at=None):
                n[0] += 1
                ins.then_inc(f_act, 1)
                assert at is None or at == n[0], (at, n[0])

            def turn_weights(g):
                w = fc1T if g < NE else fc2T
                a = 4 * (g % NE)
                done(copy(w[:, a:a + 4, :].rearrange("p a k -> p (a k)"), bank[1 + g % 2][:, :]))

            for g in range(EARLY_GROUPS):
                act.wait_ge(f_pe, 6 + g)
                turn_weights(g)
            for g in range(2):
                act.wait_ge(f_pe, PE_BEFORE_SEARCH - 3 + g)
                done(copy(xfT[:, g * HALF:(g + 1) * HALF], bank[4 + g][:, 0:HALF]), XFT + g)
            for g in range(2):
                act.wait_ge(f_pe, PE_BEFORE_SEARCH - 1 + g)
                done(act.activation(th[:, g * HALF:(g + 1) * HALF], bank[6 + g][:, 0:HALF], ACT.Tanh), TANH + g)
            g = EARLY_GROUPS
            for r in range(ROUNDS):
                for _ in range(SEARCH_GROUPS[r]):
                    act.wait_ge(f_pe, PE_BEFORE_SEARCH + (r + 1) + g - EARLY_GROUPS + 1)
                    turn_weights(g)
                    g += 1
            for j in range(TT):
                act.wait_ge(f_pe, G_FULL + j)
                m16 = bank[1 + j % 2][:, :].bitcast(F16).rearrange("p (e k) -> p e k", k=P)
                done(copy(GT[:, :, j, :], m16[0:CAP, :, 0:CAP]))
            for e in range(NE):
                act.wait_ge(f_dve, HB[e])
                if e >= 2:
                    act.wait_ge(f_pe, DOWN[e - 2])
                done(act.activation(hg[e % 2][:, :, :], hb[e % 2][:, :, :], ACT.Gelu_apprx_tanh))

        @blk.vector
        def _(dve):
            def bc(ap, shape, axis):
                return ap.unsqueeze(axis).to_broadcast(shape)

            def stats(src, p, h, k):
                wait(dve, norm_done[k], count(p, h, 1, 0))
                pass_wait(dve)
                dve.bn_stats(st[k][:, :], src).then_inc(stats_done[k], 1)
                dve.wait_ge(stats_done[k], count(p, h, 1, 1))
                wait(dve, rstd_done[k], count(p, h, 1, 0))
                pass_wait(dve)
                dve.bn_aggr(mv[k][:, :], st[k][:, :]).then_inc(aggr_done[k], 1)

            def norm(src, p, h, k):
                dve.wait_ge(rstd_done[k], count(p, h, 1, 1))
                dve.tensor_scalar(xn[k][:, :], src, mv[k][:, 0:1], rs[k][:, 0:1], ALU.subtract,
                                  ALU.mult).then_inc(norm_done[k], 1)

            def prep(name, p, h):
                b = batch(p, h)
                k, _ = stage(name)
                if k is not None:
                    m = MISC[k]
                    wait_full(dve, p, h, name)
                if name == "stats1":
                    stats(xin[:, b, :], p, h, 0)
                elif name == "norm1":
                    norm(xin[:, b, :], p, h, 0)
                elif name == "qkv":
                    dve.tensor_scalar(qT[:, :], m[:, 0:N], bq[:, 0:1], None, ALU.add).then_inc(qT_ready, 1)
                    dve.tensor_scalar(kT[:, :], m[:, N:2 * N], bk[:, 0:1], None, ALU.add)
                    dve.tensor_tensor(v[:, :], m[0:N, P:2 * P], bv[:, :], ALU.add).then_inc(qkv_ready, 1)
                elif name == "Smax":
                    wait_full(dve, p, h, "S")
                    s = MISC[0][:, 0:TILES * N].rearrange("p (t n) -> p t n", n=N)
                    dve.tensor_reduce(amax[:, :], s, X, ALU.max, negate=True).then_inc(amax_ready, 1)
                elif name == "S":
                    s = m[:, 0:TILES * N].rearrange("p (t n) -> p t n", n=N)
                    dve.wait_ge(amax_ready, count(p, h, 1, 1))
                    dve.tensor_tensor(es[:, :, :], s, bc(amax[:, :], [P, TILES, N], 2), ALU.add).then_inc(es_ready, 1)
                elif name == "soft":
                    dve.wait_ge(ep_ready, count(p, h, 1, 1))
                    dve.tensor_reduce(asum[:, :], ep[:, :, :], X, ALU.add).then_inc(asum_ready, 1)
                    dve.wait_ge(asum_ready, count(p, h, 1, 1))
                    dve.reciprocal(arec[:, :], asum[:, :]).then_inc(arec_ready, 1)
                    dve.wait_ge(arec_ready, count(p, h, 1, 1))
                    dve.tensor_scalar(arec[:, :], arec[:, :], ATT, None, ALU.mult).then_inc(arec_scaled, 1)
                elif name == "y":
                    dve.tensor_tensor(x1[:, b, :], m[0:N, 0:C], xin[:, b, :], ALU.add).then_inc(x1_ready, 1)
                    dve.wait_ge(x1_ready, count(p, h, 1, 1))
                    stats(x1[:, b, :], p, h, 1)
                elif name == "norm2":
                    norm(x1[:, b, :], p, h, 1)
                elif name in ("q0", "q1"):
                    k = int(name == "q1")
                    dve.wait_ge(qhi_ready, count(p, h, 2, k + 1))
                    cols = slice(k * HALF, (k + 1) * HALF)
                    dve.tensor_tensor(qlo[h][:, cols], m[0:E, 0:HALF], qhi[h][0:E, cols],
                                      ALU.subtract).then_inc(qlo_ready, 1)
                elif name in ("c0", "c1", "c2"):
                    k = int(name[1])
                    dve.wait_ge(cThi_ready, count(p, h, GROUPS, k + 1))
                    dve.tensor_tensor(cT[h][0:E, 1, k * GW:(k + 1) * GW], m[0:E, 0:GW],
                                      cT[h][0:E, 0, k * GW:(k + 1) * GW], ALU.subtract).then_inc(cTlo_ready, 1)
                elif name == "x1T":
                    dve.wait_ge(x1Thi_ready, count(p, h, 1, 1))
                    dve.tensor_tensor(x1Tlo[:, :], m[:, 0:N], x1Thi[:, :], ALU.subtract).then_inc(x1Tlo_ready, 1)

            def maximum(p, h, j):
                dve.wait_ge(mx_full, count(p, h, NMAX, j + 1))
                if j == 0:
                    wait(dve, nmax_ready, count(p, h, 1, 0))
                dve.tensor_reduce(mx[:, j // GROUPS, j % GROUPS:j % GROUPS + 1], mx_bank(h, j)[:, 0:GW], X,
                                  ALU.max).then_inc(mx_done, 1)

            def maxima(p, h):
                dve.wait_ge(mx_done, count(p, h, NMAX, NMAX))
                wait(dve, mxT_full, count(p, h, 2, 0))
                dve.tensor_reduce(nmax[:, :], mx[:, :, :], X, ALU.max, negate=True).then_inc(nmax_ready, 1)

            def low_parts(p, h, i):
                _, g, _ = chunk(i)
                dve.wait_ge(phi_ready, count(p, h, CHUNKS, i + 1))
                dve.tensor_tensor(plo[i % 3][:, 0:HW[g]], prob[i % 3][:, 0:HW[g]], phi[i % 3][:, 0:HW[g]],
                                  ALU.subtract).then_inc(plo_ready, 1)

            def normalise(p, h, g):
                n = HALF_TILES[g]
                o = ACC[g][:, :].rearrange("p (a k) -> p a k", k=P)
                dve.wait_ge(pv_done, count(p, h, CHUNKS, CHUNKS - 1 + g))
                wait(dve, on_ready, count(p, h, 2, g))
                dve.reciprocal(rden[:, 0:n], o[:, 0:n, E]).then_inc(rden_ready, 1)
                dve.wait_ge(rden_ready, count(p, h, 2, g + 1))
                wait(dve, oT_full, count(p, h, 2, g - 1))
                dve.tensor_tensor(on[g][:, :, :], o[:, 0:n, 0:E], bc(rden[:, 0:n], [P, n, E], 2),
                                  ALU.mult).then_inc(on_ready, 1)

            FIRST_STAGE = {2: ["stats1"], 4: ["norm1"], 6: ["qkv"], 10: ["Smax", "S"], 12: ["soft"], 22: ["y"],
                           23: ["c0"]}
            SECOND_STAGE = {0: ["norm2"], 1: ["c1"], 2: ["x1T"], 4: ["c2", "q0"], 8: ["q1"]}

            def half(p, h, last=False, more_first=True):
                np_, nh = (p, 1) if h == 0 else (p + 1, 0)
                j = 0
                for i in range(CHUNKS):
                    if i + 1 < CHUNKS:
                        if i + 1 not in POOL_CHUNKS:
                            low_parts(p, h, i + 1)
                    elif not last:
                        low_parts(np_, nh, 0)
                    if i >= CHUNKS - 2:
                        normalise(p, h, i - CHUNKS + 2)
                    for _ in range(0 if last else MAXIMA[i]):
                        maximum(np_, nh, j)
                        j += 1
                    if j == NMAX and MAXIMA[i]:
                        maxima(np_, nh)
                    for name in FIRST_STAGE.get(i, []) if more_first else []:
                        prep(name, p + 1, h)
                    for name in SECOND_STAGE.get(i, []) if not last else []:
                        prep(name, np_, nh)

            for i in range(2):
                dve.memset(cs[i][:, 0, :, E:E + 1], 1.0).then_inc(ones_ready, 1)
                dve.memset(cT[i][E:E + 1, 0, :], 1.0).then_inc(ones_ready, 1)
            dve.wait_ge(const_ready, CONSTS)
            dve.wait_ge(ld_x, 16)
            prep("stats1", 0, 0)
            prep("norm1", 0, 0)
            dve.wait_ge(ld_bias, 48)

            def make_m(g):
                dve.wait_ge(mu_ready, g + 1)
                heads = slice(8 * (g // 2) + g % 2, 8 * (g // 2) + 8, 2)
                dve.scalar_tensor_tensor(Mlo[:, heads, :],
                                         bank[M_BANK[g]][:, :].rearrange("p (a k) -> p a k", k=P)[:, :, 0:E],
                                         SCALE, Mhi[:, heads, :], ALU.mult, ALU.subtract).then_inc(mlo_ready, 1)

            prep("qkv", 0, 0)
            prep("stats1", 0, 1)
            prep("norm1", 0, 1)
            make_m(0)
            prep("Smax", 0, 0)
            prep("S", 0, 0)
            make_m(1)
            make_m(2)
            prep("soft", 0, 0)
            make_m(3)
            prep("c0", 0, 0)
            prep("c1", 0, 0)
            prep("y", 0, 0)
            prep("c2", 0, 0)
            prep("norm2", 0, 0)
            prep("x1T", 0, 0)
            prep("qkv", 0, 1)
            prep("q0", 0, 0)
            prep("Smax", 0, 1)
            prep("S", 0, 1)
            j = 0
            for maxima_before, b, name in ((2, 0, "q1"), (0, 1, "soft"), (12, 1, "c0"), (1, 1, "y"),
                                           (NMAX - 15, 0, None)):
                for _ in range(maxima_before):
                    maximum(0, 0, j)
                    j += 1
                if name:
                    prep(name, 0, b)
            maxima(0, 0)
            low_parts(0, 0, 0)
            half(0, 0)
            half(0, 1)
            with dve.Fori(1, B // 2 - 1) as p:
                half(p, 0)
                half(p, 1)
            half(B // 2 - 1, 0, more_first=False)
            half(B // 2 - 1, 1, last=True, more_first=False)

            n = [0]

            def done(ins, at=None):
                n[0] += 1
                ins.then_inc(f_dve, 1)
                assert at is None or at == n[0], (at, n[0])

            def settle():
                dve.wait_ge(f_dve, n[0])

            def f_stats(src, tiles, at):
                settle()
                for j in tiles:
                    done(dve.bn_stats(fst[:, j, :], src[:, j, :]))
                settle()
                for j in tiles:
                    done(dve.bn_aggr(fmv[:, j, :], fst[:, j, :]), at if j == tiles[-1] else None)

            def f_norm(dst, src, tiles, at=None):
                for j in tiles:
                    done(dve.tensor_scalar(dst[:, j, :], src[:, j, :], fmv[:, j, 0:1], frs[:, j:j + 1],
                                           ALU.subtract, ALU.mult), at if j == tiles[-1] else None)

            dve.wait_ge(oT_ready, 2 * B)
            for g in range(2):
                tiles = range(4 * g, 4 * g + 4)
                dve.wait_ge(f_pe, 1 + 2 * g)
                done(dve.tensor_scalar(yT[:, g * HALF:(g + 1) * HALF], bank[g][:, 0:HALF], bpr[:, 0:1], None, ALU.add))
                if g == 0:
                    dve.wait_ge(ld_late, LD_LATE)
                dve.wait_ge(f_pe, 2 + 2 * g)
                done(dve.tensor_tensor(x2[:, 4 * g:4 * g + 4, :],
                                       bank[2 + g][0:CAP, :].rearrange("p (a k) -> p a k", k=P),
                                       x1p[:, 4 * g:4 * g + 4, :], ALU.add))
                f_stats(x2, tiles, AGGR3[g])
                dve.wait_ge(f_pool, 2 + 2 * g)
                f_norm(xf, x2, tiles, NORM3[g])
            dve.wait_ge(f_pe, 5)
            done(dve.tensor_copy(gateT[:, :, :], bc(bank[6][:, 0:NE], [C, NE, REP], 2)))
            done(dve.tensor_copy(b1T[:, :, :], bank[6][:, P:P + NE * FC].rearrange("p (e f) -> p e f", f=FC)), GATE_T)
            f_stats(xf, range(TT), AGGR4)
            done(dve.tensor_reduce(jcol[:, :], jcol8[:, :], X, ALU.add))
            done(dve.memset(low[:, :], 0.0))
            for g in range(2):
                dve.wait_ge(f_act, TANH + g)
                done(dve.tensor_scalar(vals[:, g * HALF:(g + 1) * HALF], th[:, g * HALF:(g + 1) * HALF], 1.0, 0.5,
                                       ALU.add, ALU.mult), VALS if g else None)
            for r in range(ROUNDS):
                step = 2.0 ** -(3 + 4 * r)
                settle()
                done(dve.tensor_scalar(thr[:, :], jcol[:, :], step, low[:, 0:1], ALU.mult, ALU.add))
                settle()
                done(dve.tensor_scalar(junk[:, :], vals[:, :], thr[:, 0:1], None, ALU.is_ge, ALU.add,
                                       accum_out=cnt[:, :]))
                settle()
                done(dve.tensor_scalar(flag[:, :], cnt[:, :], float(CAP), None, ALU.is_ge), FLAG[r])
                if NORM_ROUNDS[r]:
                    dve.wait_ge(f_pool, 6)
                    first = sum(NORM_ROUNDS[:r])
                    f_norm(y1, xf, range(first, first + NORM_ROUNDS[r]))
                dve.wait_ge(f_pe, SEARCH[r])
                done(dve.tensor_scalar(low[:, :], bank[0][:, 0:1], step, low[:, 0:1], ALU.mult, ALU.add))
            settle()
            done(dve.tensor_scalar(mge[:, :], vals[:, :], low[:, 0:1], None, ALU.is_ge), MGE)
            done(dve.tensor_scalar(mgt[:, :], vals[:, :], low[:, 0:1], None, ALU.is_gt), MGT)
            for g in range(2):
                dve.wait_ge(f_pe, VN_FULL + g)
                done(dve.tensor_copy(vn[:, 4 * g:4 * g + 4, :],
                                     bank[3 + g][0:CAP, :].rearrange("p (a e r) -> p a e r", a=4, r=REP)[:, :, :, 0]))
            settle()
            done(dve.tensor_copy(v2[:, :, :, 0], vn[:, :, :]))
            settle()
            done(dve.tensor_tensor(v2[:, :, :, 1], vn[:, :, :], v2[:, :, :, 0], ALU.subtract), V2)
            mask = [bank[5 + g][0:CAP, :].bitcast(F16).rearrange("p (j e r) -> p j e r", e=NE, r=REP)[:, :, :, 0]
                    for g in range(2)]
            dve.wait_ge(f_pe, MASK_FULL)
            done(dve.tensor_copy(ge[:, :, :], mask[0]))
            dve.wait_ge(f_pe, MASK_FULL + 1)
            done(dve.tensor_copy(sel[:, 0, :, :], mask[1]))
            settle()
            done(dve.tensor_tensor(sel[:, 1, :, :], ge[:, :, :], sel[:, 0, :, :], ALU.subtract), SEL)
            cum = bank[7][0:CAP, 0:2 * TT * NE].rearrange("p (k j e) -> p k j e", k=2, e=NE)
            dve.wait_ge(f_pe, TOT_FULL)
            done(dve.tensor_copy(cg[:, :], bank[0][0:CAP, 0:NE]))
            settle()
            done(dve.tensor_tensor(pa[:, :, :], cum[:, 1, :, :], bc(cg[:, :], [CAP, TT, NE], 1), ALU.add))
            done(dve.tensor_tensor(pb[:, :, :], cum[:, 0, :, :], sel[:, 0, :, :], ALU.mult))
            settle()
            done(dve.tensor_tensor(pa[:, :, :], pa[:, :, :], sel[:, 1, :, :], ALU.mult))
            settle()
            done(dve.tensor_tensor(pa[:, :, :], pa[:, :, :], pb[:, :, :], ALU.add))
            settle()
            done(dve.tensor_scalar(pb[:, :, :], ge[:, :, :], -2.0 * T, 2.0 * T, ALU.mult, ALU.add))
            settle()
            done(dve.tensor_tensor(slot[:, :, :], pa[:, :, :], pb[:, :, :], ALU.add))
            settle()
            for j in range(TT):
                done(dve.tensor_tensor(G[:, j, :, :], bc(iota1[:, :], [CAP, NE, CAP], 1),
                                       bc(slot[:, j, :], [CAP, NE, CAP], 2), ALU.is_equal), G0 + j)
            done(dve.tensor_tensor(base[:, :, :], x2[:, :, :], xf[:, :, :], ALU.add))
            dve.wait_ge(f_pe, G_FULL + TT - 1)
            for g in range(2):
                done(dve.tensor_copy(ygT[:, 4 * g:4 * g + 4, :],
                                     bank[3 + g][:, 0:HALF].rearrange("p (e s) -> p e s", s=CAP)), YG if g else None)
            dve.wait_ge(f_pe, WSLOT)
            done(dve.tensor_copy(w2s[:, :, :], bank[0][0:CAP, P:P + 2 * NE].rearrange("p (e k) -> p e k", k=2)))
            settle()
            done(dve.tensor_tensor(wslot[:, :], w2s[:, :, 0], w2s[:, :, 1], ALU.add))

            def add_b1(e):
                dve.wait_ge(f_pe, HID[e])
                if e >= 2:
                    dve.wait_ge(f_act, GELU0 + e - 2)
                done(dve.tensor_tensor(hb[e % 2][:, :, :], bank[5 + e % 2][:, 0:HALF].rearrange("p (f s) -> p f s", s=CAP),
                                       bc(b1T[:, e, :], [P, FC, CAP], 2), ALU.add), HB[e])

            settle()
            add_b1(0)
            for e in range(NE):
                if e + 1 < NE:
                    add_b1(e + 1)
                dve.wait_ge(f_pe, DOWN[e])
                if e >= 2:
                    dve.wait_ge(f_pe, SCAT[e - 2])
                o = bank[7][0:CAP, 0:C]
                done(dve.tensor_scalar(ohi[e % 2][:, :], o, wslot[:, e:e + 1], None, ALU.mult))
                settle()
                done(dve.scalar_tensor_tensor(olo[e % 2][:, :], o, wslot[:, e:e + 1], ohi[e % 2][:, :],
                                              ALU.mult, ALU.subtract), OLO[e])
            dve.wait_ge(f_pe, SCAT[NE - 1])
            for g in range(2):
                done(dve.tensor_tensor(res[:, 4 * g:4 * g + 4, :],
                                       bank[1 + g][0:CAP, :].rearrange("p (a k) -> p a k", k=P),
                                       base[:, 4 * g:4 * g + 4, :], ALU.add), OUT_READY[g])


_INS = ['x', 'ctx_768', 'L0_attn_W_qkv', 'L0_attn_b_qkv', 'L0_attn_W_out', 'L0_attn_b_out', 'L0_xattn_Wq',
        'L0_xattn_Wkv', 'L0_xattn_Wproj', 'L0_xattn_bproj', 'L0_ffn_gate_w', 'L0_ffn_ln_gamma', 'L0_ffn_ln_beta',
        'L0_ffn_fc1s', 'L0_ffn_b1s', 'L0_ffn_fc2s', 'L0_ffn_b2s']


def kernel(**inputs):
    import numpy as _np
    import concourse.bacc as _bacc
    from concourse import mybir as _mybir
    from concourse.bass_utils import run_bass_kernel_spmd as _run

    nc = _bacc.Bacc("TRN2", target_bir_lowering=False, num_devices=1)
    arrays, args = {}, []
    for name in _INS:
        a = _np.ascontiguousarray(inputs[name])
        arrays[f"in_{name}"] = a
        args.append(nc.dram_tensor(f"in_{name}", a.shape, _mybir.dt.from_np(a.dtype), kind="ExternalInput").ap())
    shape = arrays["in_x"].shape
    args.append(nc.dram_tensor("out_0", shape, _mybir.dt.float32, kind="ExternalOutput").ap())
    decoder_layer(nc, *args)
    r = _run(nc, [arrays], core_ids=[0])
    return r.results[0]["out_0"]
```
